# Optimizing a Trainium2 kernel written in Bass

```python
import numpy as np
import jax
import jax.numpy as jnp

def _softmax(x, axis=-1):
    return jax.nn.softmax(x, axis=axis)

def _gelu(x):
    return jax.nn.gelu(x, approximate=True)

def _silu(x):
    return jax.nn.silu(x)

def _sigmoid(x):
    return jax.nn.sigmoid(x)

def _layernorm(x, axis=-1, eps=1e-05):
    m = jnp.mean(x, axis=axis, keepdims=True)
    v = jnp.var(x, axis=axis, keepdims=True)
    return (x - m) / jnp.sqrt(v + eps)

def _scatter_add(tgt, idx, src, axis=0):
    return tgt.at[idx].add(src)

def _segment_sum(src, seg, n):
    return jax.ops.segment_sum(src, seg, n)
kernel_name = 'mk_flamingo_gated_d4_seqx_r8_246784'

def setup_inputs(seed: int=0):
    np.random.seed(seed)
    _w = jnp.asarray

    def _rec_inputs():
        import jax
        import jax.numpy as jnp
        _rk = jax.random.key(seed)
        x = -0.0002928 + 1 * jax.random.normal(jax.random.fold_in(_rk, 1), (4, 512, 128), jnp.float32)
        _lenS = 512 - jax.random.randint(jax.random.fold_in(_rk, 7), (4,), 0, max(1, 512 // 4) + 1, jnp.int32)
        _lenS2 = 32 - jax.random.randint(jax.random.fold_in(_rk, 8), (4,), 0, max(1, 32 // 4) + 1, jnp.int32)
        _ctx_1024P = jax.random.normal(jax.random.fold_in(_rk, 11), (4, 16, 128), jnp.float32)
        _ctx_1024c = jax.random.dirichlet(jax.random.fold_in(_rk, 511), 0.3 * jnp.ones((16,), jnp.float32), (4, 32))
        _ctx_1024t = jnp.einsum('bsk,bkd->bsd', _ctx_1024c, _ctx_1024P)
        _ctx_1024t = _ctx_1024t * jax.lax.rsqrt(jnp.mean(jnp.square(_ctx_1024t)) + 1e-12) * 0.953939
        ctx_1024 = -1.39393e-06 + 0.999914 * (_ctx_1024t + 0.3 * jax.random.normal(jax.random.fold_in(_rk, 611), (4, 32, 128), jnp.float32))
        _validS = jnp.arange(512)[None, :] < _lenS[:, None]
        _validS2 = jnp.arange(32)[None, :] < _lenS2[:, None]
        _causal = jnp.tril(jnp.ones((512, 512), dtype=bool))
        mask_Bx1xSxS2_ik1 = jnp.where(jnp.broadcast_to(_validS2[:, None, None, :], (4, 1, 512, 32)), 1, 0).astype(jnp.int32)
        _g = jax.random.normal(jax.random.fold_in(_rk, 9001), (2, 4), jnp.float32)
        _g = jnp.sign(_g) * jnp.maximum(jnp.abs(_g), 1.0) + (_g == 0) * 1.0
        g_xattn = _g[0]
        g_ffn = _g[1]
        return (x, ctx_1024, mask_Bx1xSxS2_ik1, g_xattn, g_ffn)
    x, ctx_1024, mask_Bx1xSxS2_ik1, g_xattn, g_ffn = _rec_inputs()

    def _L0_xattn_setup():
        import jax, jax.numpy as jnp
        import numpy as np
        EMBED = 128
        HEADS = 16
        HEAD_DIM = EMBED // HEADS

        def _split_heads(x):
            B, S, _ = x.shape
            return x.reshape(B, S, HEADS, HEAD_DIM).transpose(0, 2, 1, 3)
        key = jax.random.key(seed)
        ks = jax.random.split(key, 11)
        B, S = (2, 256)
        scale = 1.0 / np.sqrt(EMBED)
        inp = {'query': jax.random.normal(ks[0], (B, S, EMBED), jnp.float32), 'key': jax.random.normal(ks[1], (B, S, EMBED), jnp.float32), 'value': jax.random.normal(ks[2], (B, S, EMBED), jnp.float32), 'Wq': jax.random.normal(ks[3], (EMBED, EMBED), jnp.float32) * scale, 'bq': jnp.zeros((EMBED,), jnp.float32), 'Wk': jax.random.normal(ks[4], (EMBED, EMBED), jnp.float32) * scale, 'bk': jnp.zeros((EMBED,), jnp.float32), 'Wv': jax.random.normal(ks[5], (EMBED, EMBED), jnp.float32) * scale, 'bv': jnp.zeros((EMBED,), jnp.float32), 'Wo': jax.random.normal(ks[6], (EMBED, EMBED), jnp.float32) * scale, 'bo': jnp.zeros((EMBED,), jnp.float32)}
        return inp
    _L0_xattn_all = _L0_xattn_setup()
    _L0_xattn_in = {k: v for k, v in _L0_xattn_all.items() if k in ('Wq', 'bq', 'Wk', 'bk', 'Wv', 'bv', 'Wo', 'bo')}
    del _L0_xattn_all

    def _L0_ffn_setup():
        import jax, jax.numpy as jnp
        import numpy as np
        EPS = 1e-05
        LN_EPS = 1e-05
        NUM_EXPERTS = 8
        TOP_K = 2
        HIDDEN = 128
        INTER = 256

        def _swiglu(x, wg, wu, wd):
            return jax.nn.silu(x @ wg) * (x @ wu) @ wd
        key = jax.random.key(seed)
        ks = jax.random.split(key, 10)
        B, S, H, I, E = (8, 512, HIDDEN, INTER, NUM_EXPERTS)
        std_h = 1.0 / np.sqrt(H)
        std_i = 1.0 / np.sqrt(I)
        return {'x': jax.random.normal(ks[0], (B, S, H), dtype=jnp.float32), 'ln_scale': jnp.ones((H,), dtype=jnp.float32), 'ln_bias': jnp.zeros((H,), dtype=jnp.float32), 'gate_w': jax.random.normal(ks[1], (E, H), dtype=jnp.float32) * 0.01, 'Wg': jax.random.normal(ks[2], (E, H, I), dtype=jnp.float32) * std_h, 'Wu': jax.random.normal(ks[3], (E, H, I), dtype=jnp.float32) * std_h, 'Wd': jax.random.normal(ks[4], (E, I, H), dtype=jnp.float32) * std_i, 'sWg': jax.random.normal(ks[5], (H, I), dtype=jnp.float32) * std_h, 'sWu': jax.random.normal(ks[6], (H, I), dtype=jnp.float32) * std_h, 'sWd': jax.random.normal(ks[7], (I, H), dtype=jnp.float32) * std_i}
    _L0_ffn_all = _L0_ffn_setup()
    _L0_ffn_in = {k: v for k, v in _L0_ffn_all.items() if k in ('ln_scale', 'ln_bias', 'gate_w', 'Wg', 'Wu', 'Wd', 'sWg', 'sWu', 'sWd')}
    del _L0_ffn_all

    def _L1_xattn_setup():
        import jax, jax.numpy as jnp
        import numpy as np
        DIM = 128
        HEADS = 16
        HEAD_DIM = DIM // HEADS
        SCALE = HEAD_DIM ** (-0.5)
        EPS = 1e-05

        def layer_norm(x, g, b):
            mu = jnp.mean(x, axis=-1, keepdims=True)
            var = jnp.mean(jnp.square(x - mu), axis=-1, keepdims=True)
            return (x - mu) * jax.lax.rsqrt(var + EPS) * g + b
        key = jax.random.key(seed)
        ks = jax.random.split(key, 8)
        B, Ls, Lt = (2, 256, 128)
        w_std = DIM ** (-0.5)
        return {'src': jax.random.normal(ks[0], (B, Ls, DIM), jnp.float32), 'tgt': jax.random.normal(ks[1], (B, Lt, DIM), jnp.float32), 'ln1_g': jnp.ones((DIM,), jnp.float32), 'ln1_b': jnp.zeros((DIM,), jnp.float32), 'ln2_g': jnp.ones((DIM,), jnp.float32), 'ln2_b': jnp.zeros((DIM,), jnp.float32), 'Wq': jax.random.normal(ks[2], (DIM, DIM), jnp.float32) * w_std, 'Wk': jax.random.normal(ks[3], (DIM, DIM), jnp.float32) * w_std, 'Wv': jax.random.normal(ks[4], (DIM, DIM), jnp.float32) * w_std, 'Wfc': jax.random.normal(ks[5], (DIM, DIM), jnp.float32) * w_std}
    _L1_xattn_all = _L1_xattn_setup()
    _L1_xattn_in = {k: v for k, v in _L1_xattn_all.items() if k in ('ln1_g', 'ln1_b', 'ln2_g', 'ln2_b', 'Wq', 'Wk', 'Wv', 'Wfc')}
    del _L1_xattn_all

    def _L1_ffn_setup():
        import jax, jax.numpy as jnp
        import numpy as np
        NUM_EXPERTS = 8
        TOP_K = 2
        CAPACITY_FACTOR = 1.0

        def _dispatch_compute(xf, top_expert, w1, w2, capacity):
            tokens, hs = xf.shape
            tpe = jnp.bincount(top_expert, length=NUM_EXPERTS)
            indices = jnp.argsort(top_expert)
            offsets = jnp.concatenate([jnp.zeros((1,), tpe.dtype), jnp.cumsum(tpe)[:-1]])
            slot = jnp.arange(capacity)
            pos = offsets[:, None] + slot[None, :]
            valid = slot[None, :] < tpe[:, None]
            tok_idx = indices[jnp.minimum(pos, tokens - 1)]
            xe = jnp.where(valid[..., None], xf[tok_idx], 0.0)
            h = jax.nn.gelu(jnp.einsum('ech,ehf->ecf', xe, w1), approximate=True)
            ye = jnp.einsum('ecf,efh->ech', h, w2)
            tok_safe = jnp.where(valid, tok_idx, tokens)
            out = jnp.zeros((tokens + 1, hs), xf.dtype).at[tok_safe.reshape(-1)].add(ye.reshape(-1, hs))
            return out[:tokens]
        key = jax.random.key(seed)
        k1, k2, k3, k4 = jax.random.split(key, 4)
        hs, ffn = (128, 512)
        x = jax.random.normal(k1, (256, 2, hs), dtype=jnp.float32)
        router_w = jax.random.normal(k2, (hs, NUM_EXPERTS), dtype=jnp.float32) * hs ** (-0.5)
        w1 = jax.random.normal(k3, (NUM_EXPERTS, hs, ffn), dtype=jnp.float32) * 0.02
        w2 = jax.random.normal(k4, (NUM_EXPERTS, ffn, hs), dtype=jnp.float32) * 0.02
        bias = jnp.zeros((1, 1, hs), dtype=jnp.float32)
        return {'x': x, 'router_w': router_w, 'w1': w1, 'w2': w2, 'bias': bias}
    _L1_ffn_all = _L1_ffn_setup()
    _L1_ffn_in = {k: v for k, v in _L1_ffn_all.items() if k in ('router_w', 'w1', 'w2', 'bias')}
    del _L1_ffn_all

    def _L2_xattn_setup():
        import jax, jax.numpy as jnp
        import numpy as np
        EMBED = 128
        HEADS = 16
        HEAD_DIM = EMBED // HEADS
        key = jax.random.key(seed)
        ks = jax.random.split(key, 9)
        N, L = (2, 256)
        values = jax.random.normal(ks[0], (N, L, EMBED), dtype=jnp.float32)
        keys = jax.random.normal(ks[1], (N, L, EMBED), dtype=jnp.float32)
        query = jax.random.normal(ks[2], (N, L, EMBED), dtype=jnp.float32)
        mask = jax.random.randint(ks[3], (N, 1, L, L), 0, 2, dtype=jnp.int32)
        s = 1.0 / np.sqrt(HEAD_DIM)
        Wv = jax.random.normal(ks[4], (HEAD_DIM, HEAD_DIM), dtype=jnp.float32) * s
        Wk = jax.random.normal(ks[5], (HEAD_DIM, HEAD_DIM), dtype=jnp.float32) * s
        Wq = jax.random.normal(ks[6], (HEAD_DIM, HEAD_DIM), dtype=jnp.float32) * s
        Wout = jax.random.normal(ks[7], (EMBED, EMBED), dtype=jnp.float32) * (1.0 / np.sqrt(EMBED))
        bout = jax.random.normal(ks[8], (EMBED,), dtype=jnp.float32) * 0.01
        return {'values': values, 'keys': keys, 'query': query, 'mask': mask, 'Wv': Wv, 'Wk': Wk, 'Wq': Wq, 'Wout': Wout, 'bout': bout}
    _L2_xattn_all = _L2_xattn_setup()
    _L2_xattn_in = {k: v for k, v in _L2_xattn_all.items() if k in ('Wv', 'Wk', 'Wq', 'Wout', 'bout')}
    del _L2_xattn_all

    def _L2_ffn_setup():
        import jax, jax.numpy as jnp
        import numpy as np
        B, S, DIM = (2, 256, 128)
        HID = 256
        E, NSH, TOPK = (8, 2, 2)

        def _ffn(x, w1, w2, w3):
            return jax.nn.silu(x @ w1.T) * (x @ w3.T) @ w2.T
        key = jax.random.key(seed)
        ks = jax.random.split(key, 8)
        sc = 0.02
        return {'x': jax.random.normal(ks[0], (B, S, DIM), jnp.float32), 'router_w': jax.random.normal(ks[1], (E, DIM), jnp.float32) * sc, 'expert_bias': jnp.zeros((E,), jnp.float32), 'w1': jax.random.normal(ks[2], (E, HID, DIM), jnp.float32) * sc, 'w3': jax.random.normal(ks[3], (E, HID, DIM), jnp.float32) * sc, 'w2': jax.random.normal(ks[4], (E, DIM, HID), jnp.float32) * sc, 'sw1': jax.random.normal(ks[5], (NSH, HID, DIM), jnp.float32) * sc, 'sw3': jax.random.normal(ks[6], (NSH, HID, DIM), jnp.float32) * sc, 'sw2': jax.random.normal(ks[7], (NSH, DIM, HID), jnp.float32) * sc}
    _L2_ffn_all = _L2_ffn_setup()
    _L2_ffn_in = {k: v for k, v in _L2_ffn_all.items() if k in ('router_w', 'expert_bias', 'w1', 'w3', 'w2', 'sw1', 'sw3', 'sw2')}
    del _L2_ffn_all

    def _L3_xattn_setup():
        import jax, jax.numpy as jnp
        import numpy as np
        HIDDEN = 128
        ATTN = 128
        B, S = (4, 256)
        key = jax.random.key(seed)
        ks = jax.random.split(key, 6)
        bound = 1.0 / np.sqrt(HIDDEN)
        return {'query': jax.random.normal(ks[0], (B, S, HIDDEN), jnp.float32), 'value': jax.random.normal(ks[1], (B, S, HIDDEN), jnp.float32), 'Wq': jax.random.uniform(ks[2], (HIDDEN, ATTN), jnp.float32, -bound, bound), 'bq': jax.random.uniform(ks[3], (ATTN,), jnp.float32, -bound, bound), 'Wv': jax.random.uniform(ks[4], (HIDDEN, ATTN), jnp.float32, -bound, bound), 'bv': jax.random.uniform(ks[5], (ATTN,), jnp.float32, -bound, bound)}
    _L3_xattn_all = _L3_xattn_setup()
    _L3_xattn_in = {k: v for k, v in _L3_xattn_all.items() if k in ('Wq', 'bq', 'Wv', 'bv')}
    del _L3_xattn_all

    def _L3_ffn_setup():
        import jax, jax.numpy as jnp
        import numpy as np
        B, S, D, E, F = (2, 256, 128, 8, 512)
        key = jax.random.key(seed)
        ks = jax.random.split(key, 4)
        return {'hidden_states': jax.random.normal(ks[0], (B, S, D), dtype=jnp.float32), 'Wr': jax.random.normal(ks[1], (D, E), dtype=jnp.float32) * (1.0 / np.sqrt(D)), 'W1': jax.random.normal(ks[2], (E, D, F), dtype=jnp.float32) * (1.0 / np.sqrt(D)), 'b1': jnp.zeros((E, F), dtype=jnp.float32), 'W2': jax.random.normal(ks[3], (E, F, D), dtype=jnp.float32) * (1.0 / np.sqrt(F)), 'b2': jnp.zeros((E, D), dtype=jnp.float32)}
    _L3_ffn_all = _L3_ffn_setup()
    _L3_ffn_in = {k: v for k, v in _L3_ffn_all.items() if k in ('Wr', 'W1', 'b1', 'W2', 'b2')}
    del _L3_ffn_all
    return {'x': x, 'ctx_1024': ctx_1024, 'mask_Bx1xSxS2_ik1': mask_Bx1xSxS2_ik1, 'g_xattn': g_xattn, 'g_ffn': g_ffn, 'L0_xattn_Wq': _L0_xattn_in['Wq'], 'L0_xattn_bq': _L0_xattn_in['bq'], 'L0_xattn_Wk': _L0_xattn_in['Wk'], 'L0_xattn_bk': _L0_xattn_in['bk'], 'L0_xattn_Wv': _L0_xattn_in['Wv'], 'L0_xattn_bv': _L0_xattn_in['bv'], 'L0_xattn_Wo': _L0_xattn_in['Wo'], 'L0_xattn_bo': _L0_xattn_in['bo'], 'L0_ffn_ln_scale': _L0_ffn_in['ln_scale'], 'L0_ffn_ln_bias': _L0_ffn_in['ln_bias'], 'L0_ffn_gate_w': _L0_ffn_in['gate_w'], 'L0_ffn_Wg': _L0_ffn_in['Wg'], 'L0_ffn_Wu': _L0_ffn_in['Wu'], 'L0_ffn_Wd': _L0_ffn_in['Wd'], 'L0_ffn_sWg': _L0_ffn_in['sWg'], 'L0_ffn_sWu': _L0_ffn_in['sWu'], 'L0_ffn_sWd': _L0_ffn_in['sWd'], 'L1_xattn_ln1_g': _L1_xattn_in['ln1_g'], 'L1_xattn_ln1_b': _L1_xattn_in['ln1_b'], 'L1_xattn_ln2_g': _L1_xattn_in['ln2_g'], 'L1_xattn_ln2_b': _L1_xattn_in['ln2_b'], 'L1_xattn_Wq': _L1_xattn_in['Wq'], 'L1_xattn_Wk': _L1_xattn_in['Wk'], 'L1_xattn_Wv': _L1_xattn_in['Wv'], 'L1_xattn_Wfc': _L1_xattn_in['Wfc'], 'L1_ffn_router_w': _L1_ffn_in['router_w'], 'L1_ffn_w1': _L1_ffn_in['w1'], 'L1_ffn_w2': _L1_ffn_in['w2'], 'L1_ffn_bias': _L1_ffn_in['bias'], 'L2_xattn_Wv': _L2_xattn_in['Wv'], 'L2_xattn_Wk': _L2_xattn_in['Wk'], 'L2_xattn_Wq': _L2_xattn_in['Wq'], 'L2_xattn_Wout': _L2_xattn_in['Wout'], 'L2_xattn_bout': _L2_xattn_in['bout'], 'L2_ffn_router_w': _L2_ffn_in['router_w'], 'L2_ffn_expert_bias': _L2_ffn_in['expert_bias'], 'L2_ffn_w1': _L2_ffn_in['w1'], 'L2_ffn_w3': _L2_ffn_in['w3'], 'L2_ffn_w2': _L2_ffn_in['w2'], 'L2_ffn_sw1': _L2_ffn_in['sw1'], 'L2_ffn_sw3': _L2_ffn_in['sw3'], 'L2_ffn_sw2': _L2_ffn_in['sw2'], 'L3_xattn_Wq': _L3_xattn_in['Wq'], 'L3_xattn_bq': _L3_xattn_in['bq'], 'L3_xattn_Wv': _L3_xattn_in['Wv'], 'L3_xattn_bv': _L3_xattn_in['bv'], 'L3_ffn_Wr': _L3_ffn_in['Wr'], 'L3_ffn_W1': _L3_ffn_in['W1'], 'L3_ffn_b1': _L3_ffn_in['b1'], 'L3_ffn_W2': _L3_ffn_in['W2'], 'L3_ffn_b2': _L3_ffn_in['b2']}

def reference(x, ctx_1024, mask_Bx1xSxS2_ik1, g_xattn, g_ffn, L0_xattn_Wq, L0_xattn_bq, L0_xattn_Wk, L0_xattn_bk, L0_xattn_Wv, L0_xattn_bv, L0_xattn_Wo, L0_xattn_bo, L0_ffn_ln_scale, L0_ffn_ln_bias, L0_ffn_gate_w, L0_ffn_Wg, L0_ffn_Wu, L0_ffn_Wd, L0_ffn_sWg, L0_ffn_sWu, L0_ffn_sWd, L1_xattn_ln1_g, L1_xattn_ln1_b, L1_xattn_ln2_g, L1_xattn_ln2_b, L1_xattn_Wq, L1_xattn_Wk, L1_xattn_Wv, L1_xattn_Wfc, L1_ffn_router_w, L1_ffn_w1, L1_ffn_w2, L1_ffn_bias, L2_xattn_Wv, L2_xattn_Wk, L2_xattn_Wq, L2_xattn_Wout, L2_xattn_bout, L2_ffn_router_w, L2_ffn_expert_bias, L2_ffn_w1, L2_ffn_w3, L2_ffn_w2, L2_ffn_sw1, L2_ffn_sw3, L2_ffn_sw2, L3_xattn_Wq, L3_xattn_bq, L3_xattn_Wv, L3_xattn_bv, L3_ffn_Wr, L3_ffn_W1, L3_ffn_b1, L3_ffn_W2, L3_ffn_b2):
    import jax
    import jax.numpy as jnp

    def _L0_xattn_ref(query, key, value, Wq, bq, Wk, bk, Wv, bv, Wo, bo):
        import jax, jax.numpy as jnp
        import numpy as np
        EMBED = 128
        HEADS = 16
        HEAD_DIM = EMBED // HEADS

        def _split_heads(x):
            B, S, _ = x.shape
            return x.reshape(B, S, HEADS, HEAD_DIM).transpose(0, 2, 1, 3)
        q = _split_heads(query @ Wq.T + bq)
        k = _split_heads(key @ Wk.T + bk)
        v = _split_heads(value @ Wv.T + bv)
        scores = jnp.einsum('bhqd,bhkd->bhqk', q, k) / np.sqrt(HEAD_DIM).astype(jnp.float32)
        attn = jax.nn.softmax(scores, axis=-1)
        ctx = jnp.einsum('bhqk,bhkd->bhqd', attn, v)
        B, H, S, D = ctx.shape
        ctx = ctx.transpose(0, 2, 1, 3).reshape(B, S, H * D)
        return ctx @ Wo.T + bo

    def _L0_ffn_ref(x, ln_scale, ln_bias, gate_w, Wg, Wu, Wd, sWg, sWu, sWd):
        import jax, jax.numpy as jnp
        import numpy as np
        EPS = 1e-05
        LN_EPS = 1e-05
        NUM_EXPERTS = 8
        TOP_K = 2
        HIDDEN = 128
        INTER = 256

        def _swiglu(x, wg, wu, wd):
            return jax.nn.silu(x @ wg) * (x @ wu) @ wd
        B, S, H = x.shape
        xf = x.reshape(-1, H)
        mu = jnp.mean(xf, axis=-1, keepdims=True)
        var = jnp.var(xf, axis=-1, keepdims=True)
        xn = (xf - mu) * jax.lax.rsqrt(var + LN_EPS) * ln_scale + ln_bias
        logits = xn @ gate_w.T
        probs = jax.nn.softmax(logits, axis=-1)
        tk_probs, tk_idx = jax.lax.top_k(probs, TOP_K)
        tk_probs = tk_probs / (jnp.sum(tk_probs, axis=-1, keepdims=True) + EPS)
        onehot = tk_idx[..., None] == jnp.arange(NUM_EXPERTS)[None, None, :]
        w = jnp.sum(tk_probs[..., None] * onehot.astype(tk_probs.dtype), axis=1)
        out = _swiglu(xf, sWg, sWu, sWd)
        for e in range(NUM_EXPERTS):
            out = out + w[:, e:e + 1] * _swiglu(xf, Wg[e], Wu[e], Wd[e])
        return out.reshape(B, S, H)

    def _L1_xattn_ref(src, tgt, ln1_g, ln1_b, ln2_g, ln2_b, Wq, Wk, Wv, Wfc):
        import jax, jax.numpy as jnp
        import numpy as np
        DIM = 128
        HEADS = 16
        HEAD_DIM = DIM // HEADS
        SCALE = HEAD_DIM ** (-0.5)
        EPS = 1e-05

        def layer_norm(x, g, b):
            mu = jnp.mean(x, axis=-1, keepdims=True)
            var = jnp.mean(jnp.square(x - mu), axis=-1, keepdims=True)
            return (x - mu) * jax.lax.rsqrt(var + EPS) * g + b
        B = src.shape[0]
        s = layer_norm(src, ln1_g, ln1_b)
        t = layer_norm(tgt, ln2_g, ln2_b)
        q = (t @ Wq).reshape(B, -1, HEADS, HEAD_DIM)
        k = (s @ Wk).reshape(B, -1, HEADS, HEAD_DIM)
        v = (s @ Wv).reshape(B, -1, HEADS, HEAD_DIM)
        attn = jnp.einsum('bqhd,bkhd->bhqk', q, k) * SCALE
        attn = jax.nn.softmax(attn, axis=-1)
        out = jnp.einsum('bhqk,bkhd->bqhd', attn, v).reshape(B, -1, DIM)
        return out @ Wfc

    def _L1_ffn_ref(x, router_w, w1, w2, bias):
        import jax, jax.numpy as jnp
        import numpy as np
        NUM_EXPERTS = 8
        TOP_K = 2
        CAPACITY_FACTOR = 1.0

        def _dispatch_compute(xf, top_expert, w1, w2, capacity):
            tokens, hs = xf.shape
            tpe = jnp.bincount(top_expert, length=NUM_EXPERTS)
            indices = jnp.argsort(top_expert)
            offsets = jnp.concatenate([jnp.zeros((1,), tpe.dtype), jnp.cumsum(tpe)[:-1]])
            slot = jnp.arange(capacity)
            pos = offsets[:, None] + slot[None, :]
            valid = slot[None, :] < tpe[:, None]
            tok_idx = indices[jnp.minimum(pos, tokens - 1)]
            xe = jnp.where(valid[..., None], xf[tok_idx], 0.0)
            h = jax.nn.gelu(jnp.einsum('ech,ehf->ecf', xe, w1), approximate=True)
            ye = jnp.einsum('ecf,efh->ech', h, w2)
            tok_safe = jnp.where(valid, tok_idx, tokens)
            out = jnp.zeros((tokens + 1, hs), xf.dtype).at[tok_safe.reshape(-1)].add(ye.reshape(-1, hs))
            return out[:tokens]
        sl, bs, hs = x.shape
        tokens = sl * bs
        capacity = int(CAPACITY_FACTOR * tokens / NUM_EXPERTS)
        xf = x.reshape(tokens, hs)
        scores = jax.nn.softmax(xf @ router_w, axis=-1)
        expert_weights, top_experts = jax.lax.top_k(scores, TOP_K)
        out = jnp.zeros_like(xf)
        for k in range(TOP_K):
            y = _dispatch_compute(xf, top_experts[:, k].astype(jnp.int32), w1, w2, capacity)
            out = out + y * expert_weights[:, k][:, None]
        return out.reshape(sl, bs, hs) + bias

    def _L2_xattn_ref(values, keys, query, mask, Wv, Wk, Wq, Wout, bout):
        import jax, jax.numpy as jnp
        import numpy as np
        EMBED = 128
        HEADS = 16
        HEAD_DIM = EMBED // HEADS
        N, Lq, _ = query.shape
        Lk = keys.shape[1]
        v = values.reshape(N, Lk, HEADS, HEAD_DIM)
        k = keys.reshape(N, Lk, HEADS, HEAD_DIM)
        q = query.reshape(N, Lq, HEADS, HEAD_DIM)
        v = jnp.einsum('nlhd,ed->nlhe', v, Wv)
        k = jnp.einsum('nlhd,ed->nlhe', k, Wk)
        q = jnp.einsum('nlhd,ed->nlhe', q, Wq)
        scores = jnp.einsum('nqhd,nkhd->nhqk', q, k)
        scores = jnp.where(mask == 0, jnp.float32(-1e+20), scores)
        attn = jax.nn.softmax(scores / jnp.sqrt(jnp.float32(EMBED)), axis=3)
        out = jnp.einsum('nhqk,nkhd->nqhd', attn, v).reshape(N, Lq, EMBED)
        return out @ Wout.T + bout

    def _L2_ffn_ref(x, router_w, expert_bias, w1, w3, w2, sw1, sw3, sw2):
        import jax, jax.numpy as jnp
        import numpy as np
        B, S, DIM = (2, 256, 128)
        HID = 256
        E, NSH, TOPK = (8, 2, 2)

        def _ffn(x, w1, w2, w3):
            return jax.nn.silu(x @ w1.T) * (x @ w3.T) @ w2.T
        bs, sl, d = x.shape
        xf = x.reshape(-1, d)
        shared = jnp.zeros_like(xf)
        for i in range(sw1.shape[0]):
            shared = shared + _ffn(xf, sw1[i], sw2[i], sw3[i])
        logits = xf @ router_w.T + expert_bias
        rw, sel = jax.lax.top_k(logits, TOPK)
        rw = jax.nn.softmax(rw.astype(jnp.float32), axis=-1).astype(x.dtype)
        onehot = jax.nn.one_hot(sel, E, dtype=x.dtype)
        combine = jnp.einsum('tk,tke->te', rw, onehot)

        def body(acc, ew):
            e1, e3, e2, cw = ew
            acc = acc + cw[:, None] * _ffn(xf, e1, e2, e3)
            return (acc, None)
        out, _ = jax.lax.scan(body, jnp.zeros_like(xf), (w1, w3, w2, combine.T))
        out = out + shared
        return out.reshape(bs, sl, -1)

    def _L3_xattn_ref(query, value, Wq, bq, Wv, bv):
        import jax, jax.numpy as jnp
        import numpy as np
        HIDDEN = 128
        ATTN = 128
        B, S = (4, 256)
        q = jnp.einsum('bsh,hd->bsd', query, Wq) + bq
        v = jnp.einsum('bsh,hd->bsd', value, Wv) + bv
        scores = jnp.einsum('bqd,bkd->bqk', q, v)
        attn = jax.nn.softmax(scores, axis=-1)
        context = jnp.einsum('bqk,bkd->bqd', attn, v)
        return context

    def _L3_ffn_ref(hidden_states, Wr, W1, b1, W2, b2):
        import jax, jax.numpy as jnp
        import numpy as np
        B, S, D, E, F = (2, 256, 128, 8, 512)
        b, s, d = hidden_states.shape
        e = Wr.shape[1]
        x = hidden_states.reshape(b * s, d)
        router_logits = x @ Wr
        router_probs = jax.nn.softmax(router_logits, axis=-1)
        expert_idx = jnp.argmax(router_probs, axis=-1)
        p_max = jnp.max(router_probs, axis=-1, keepdims=True)

        def expert_mlp(w1, bb1, w2, bb2):
            h = jax.nn.gelu(x @ w1 + bb1, approximate=False)
            return h @ w2 + bb2
        outs = jax.vmap(expert_mlp)(W1, b1, W2, b2)
        onehot = jax.nn.one_hot(expert_idx, e, dtype=x.dtype)
        next_states = jnp.einsum('te,etd->td', onehot, outs)
        out = p_max * next_states
        return out.reshape(b, s, d)
    x = x + jnp.tanh(g_xattn[0]) * _L0_xattn_ref(_layernorm(x, axis=-1), ctx_1024, ctx_1024, L0_xattn_Wq, L0_xattn_bq, L0_xattn_Wk, L0_xattn_bk, L0_xattn_Wv, L0_xattn_bv, L0_xattn_Wo, L0_xattn_bo)
    x = x + jnp.tanh(g_ffn[0]) * _L0_ffn_ref(_layernorm(x, axis=-1), L0_ffn_ln_scale, L0_ffn_ln_bias, L0_ffn_gate_w, L0_ffn_Wg, L0_ffn_Wu, L0_ffn_Wd, L0_ffn_sWg, L0_ffn_sWu, L0_ffn_sWd)
    x = x + jnp.tanh(g_xattn[1]) * _L1_xattn_ref(ctx_1024, _layernorm(x, axis=-1), L1_xattn_ln1_g, L1_xattn_ln1_b, L1_xattn_ln2_g, L1_xattn_ln2_b, L1_xattn_Wq, L1_xattn_Wk, L1_xattn_Wv, L1_xattn_Wfc)
    x = x + jnp.tanh(g_ffn[1]) * _L1_ffn_ref(_layernorm(x, axis=-1), L1_ffn_router_w, L1_ffn_w1, L1_ffn_w2, L1_ffn_bias)
    x = x + jnp.tanh(g_xattn[2]) * _L2_xattn_ref(ctx_1024, ctx_1024, _layernorm(x, axis=-1), mask_Bx1xSxS2_ik1, L2_xattn_Wv, L2_xattn_Wk, L2_xattn_Wq, L2_xattn_Wout, L2_xattn_bout)
    x = x + jnp.tanh(g_ffn[2]) * _L2_ffn_ref(_layernorm(x, axis=-1), L2_ffn_router_w, L2_ffn_expert_bias, L2_ffn_w1, L2_ffn_w3, L2_ffn_w2, L2_ffn_sw1, L2_ffn_sw3, L2_ffn_sw2)
    x = x + jnp.tanh(g_xattn[3]) * _L3_xattn_ref(_layernorm(x, axis=-1), ctx_1024, L3_xattn_Wq, L3_xattn_bq, L3_xattn_Wv, L3_xattn_bv)
    x = x + jnp.tanh(g_ffn[3]) * _L3_ffn_ref(_layernorm(x, axis=-1), L3_ffn_Wr, L3_ffn_W1, L3_ffn_b1, L3_ffn_W2, L3_ffn_b2)
    return x

_drawn_inputs = setup_inputs


def setup_inputs(seed=0):
    import zlib

    import numpy as np

    out = dict(_drawn_inputs(seed))
    spreads = {'L0_xattn_bq': (0.0, 0.1),
     'L0_xattn_bk': (0.0, 2.0),
     'L0_xattn_bv': (0.0, 0.1),
     'L0_xattn_bo': (0.0, 0.1),
     'L0_ffn_ln_scale': (1.0, 0.2),
     'L0_ffn_ln_bias': (0.0, 0.1),
     'L1_xattn_ln1_g': (1.0, 0.2),
     'L1_xattn_ln1_b': (0.0, 0.1),
     'L1_xattn_ln2_g': (1.0, 0.2),
     'L1_xattn_ln2_b': (0.0, 0.356),
     'L1_ffn_bias': (0.0, 0.1),
     'L2_ffn_expert_bias': (0.0, 0.8),
     'L3_ffn_b1': (0.0, 0.485),
     'L3_ffn_b2': (0.0, 0.351)}
    factors = {'g_ffn': 6.368,
     'L1_ffn_router_w': 3.185,
     'L1_ffn_w1': 3.06,
     'L1_ffn_w2': 2.973,
     'L2_xattn_bout': 7.748,
     'L2_ffn_router_w': 8.0,
     'L2_ffn_w1': 6.923,
     'L2_ffn_w3': 6.543,
     'L2_ffn_w2': 7.227,
     'L2_ffn_sw1': 5.255,
     'L2_ffn_sw3': 5.031,
     'L2_ffn_sw2': 4.525,
     'L3_xattn_bq': 3.94,
     'L3_xattn_bv': 3.976}
    for name, (base, spread) in spreads.items():
        noise = np.random.default_rng([zlib.crc32(name.encode()), seed]).standard_normal(out[name].shape)
        drawn = base * np.exp(spread * noise) if base else spread * noise
        out[name] = jnp.asarray(drawn.astype(out[name].dtype))
    for name, factor in factors.items():
        out[name] = (out[name] * factor).astype(out[name].dtype)
    return out
```

```python
import concourse.bass as bass
from concourse import mybir
from contextlib import ExitStack

F32 = mybir.dt.float32
BF16 = mybir.dt.bfloat16
I32 = mybir.dt.int32
U32 = mybir.dt.uint32
ALU = mybir.AluOpType
ACT = mybir.ActivationFunctionType
AX = mybir.AxisListType

P = 128
B, S, D, KEYS = 4, 512, 128, 32
TOK = B * S
NTILE = TOK // P
NG = B
GT = S // P
HEADS, HD = 16, 8
HC = P // KEYS
NC = HEADS // HC
VW = HC * HD + HC
E = 8
EPS = 1e-5
LAYERS = 4
TOPK = [2, 2, 2, 1]
WIDE = 512
FC = [2, 4, 2, 4]
CAP = TOK // E
SEG = 2 * E
REGION = TOK + P
ROW = P + 1
NOWHERE = 2 * TOK
TILES = [(k * TOK + E * (P - 1)) // P for k in TOPK]
TILES[1] = SEG * CAP // P
MAXT = max(TILES)
RING = 4


def flamingo(nc, x_d, ctx_d, mask_d, cols_d, rows_d, attnw_d, small_d, w1_d, w2_d, b1_d, b2_d, out_d):
    ctx = ExitStack()
    with ctx:
        def sb(name, shape, dt=F32):
            return ctx.enter_context(nc.sbuf_tensor(name, shape, dt))

        def sem(name):
            return ctx.enter_context(nc.semaphore(name))

        x = sb("x", [P, NTILE, D])
        ctx_sb = sb("ctx_sb", [P, D])
        ctxn = sb("ctxn", [P, D])
        ctxT = sb("ctxT", [P, P])
        ctxTn = sb("ctxTn", [P, P])
        ctxR = sb("ctxR", [P, 2, B, HC, KEYS])
        cols = sb("cols", [P, 10 + 4 * E])
        rows = sb("rows", [P, 5 * P + 8 + 8])
        attnw = sb("attnw", [P, 11, P])
        small = sb("small", [P, 3, HD])
        blockw = sb("blockw", [P, 3, P])
        tg = sb("tg", [P, 8])
        brow = sb("brow", [P, P])
        w1 = [sb("w1_0", [P, E + 1, WIDE]), sb("w1_1", [P, E, WIDE]), sb("w1_2", [P, E + 2, WIDE])]
        w2 = [sb("w2_0", [P, E * 4, D]), sb("w2_1", [P, E * 4, D]), sb("w2_2", [P, (E + 2) * 2, D])]
        w1.append(w1[0])
        w2.append(w2[0])
        b1 = w1[1][:].rearrange("p e n -> p (e n)")
        b2 = w2[1][:, 0:E].rearrange("p c n -> p (c n)")
        kT = sb("kT", [P, P])
        kblk = sb("kblk", [P, B, HEADS, KEYS])
        vblk = sb("vblk", [P, B, NC, VW])
        v3 = sb("v3", [KEYS, B, D])
        xn = sb("xn", [P, GT, D])
        xT = sb("xT", [P, S])
        qT = sb("qT", [P, S])
        prob = sb("prob", [P, 2, HEADS, KEYS])
        probT = sb("probT", [P, 2, NC, P])
        o = sb("o", [P, 2, P])
        oT = sb("oT", [P, 2, P])
        stat = sb("stat", [P, GT, 6])
        mv = sb("mv", [P, GT, 2])
        rstd = sb("rstd", [P, GT])
        mx = sb("mx", [P, 2, HEADS])
        rinv = sb("rinv", [P, 2, HEADS])
        mask_i = sb("mask_i", [P, NTILE, KEYS], I32)
        maskb = sb("maskb", [P, NTILE, KEYS])
        xfT = sb("xfT", [P, TOK])
        pay = sb("pay", [P, 2, NTILE, ROW])
        logit = sb("logit", [P, GT, E])
        top = sb("top", [P, GT, 8])
        topi = sb("topi", [P, GT, 8], U32)
        topf = sb("topf", [P, GT, 2])
        ex = sb("ex", [P, GT, 8])
        s4 = sb("s4", [P, GT, 2])
        wts = sb("wts", [P, NTILE, 2])
        hot = sb("hot", [P, GT, 2, E])
        picks = sb("picks", [P, NG, GT, 2, E], BF16)
        place = sb("place", [P, GT, 2, E])
        posf = sb("posf", [P, GT, 2])
        rank = sb("rank", [P, GT, 2])
        pos = sb("pos", [P, NTILE, 2], U32)
        count = sb("count", [P, SEG])
        ntil = sb("ntil", [P, E])
        cmp1 = sb("cmp1", [P, E, NTILE])
        cmp2 = sb("cmp2", [P, E, E])
        cum = sb("cum", [P, E])
        cumx = sb("cumx", [P, E])
        ge_in = sb("ge_in", [P, MAXT, E])
        ge_ex = sb("ge_ex", [P, MAXT, E])
        tw = sb("tw", [P, MAXT, E])
        te = sb("te", [P, MAXT])
        tb = sb("tb", [P, MAXT])
        tn = sb("tn", [P, MAXT])
        valid = sb("valid", [P, MAXT])
        tabf = sb("tabf", [P, MAXT])
        tab_e = sb("tab_e", [1, MAXT], I32)
        tab_r = sb("tab_r", [1, MAXT], I32)
        pad_f = sb("pad_f", [P, E])
        pad_r = sb("pad_r", [1, E], I32)
        gat = sb("gat", [P, 2, S])
        hsh = sb("hsh", [P, 4, S])
        xg = sb("xg", [P, RING, ROW])
        xgT = sb("xgT", [P, 2, P])
        hid = hsh[:, 0:2]
        pre = hsh[:, 2:4]
        hidT = gat[:].rearrange("p b (c n) -> p b c n", c=4)
        ysb = sb("ysb", [P, 2, D])
        idf = sb("idf", [P, 2], I32)
        idu = sb("idu", [P, 2], I32)
        ident = sb("ident", [P, P])
        headmask = sb("headmask", [P, HEADS])
        chunkmask = sb("chunkmask", [P, HC])
        before = sb("before", [P, P], BF16)
        onesb = sb("onesb", [P, P], BF16)
        ones = sb("ones", [1, P])
        minus_half = sb("minus_half", [P, GT])
        iota_e = sb("iota_e", [P, E])
        region0 = sb("region0", [P, 2, E])
        segment0 = sb("segment0", [P, 2, E])
        slot128 = sb("slot128", [P, NTILE])
        iota_t = sb("iota_t", [P, MAXT])
        part = sb("part", [P, 1])
        nowhere = sb("nowhere", [P, 1])
        nowhere_i = sb("nowhere_i", [P, 1], I32)
        upper = sb("upper", [P, E, E])
        static_e = sb("static_e", [1, MAXT], I32)
        static_r = sb("static_r", [1, MAXT], I32)
        seg_at = sb("seg_at", [P, TILES[1]])
        zeros = sb("zeros", [P, ROW])

        bank = [ctx.enter_context(nc.psum_tensor(f"bank{i}", [P, 512], F32)) for i in range(8)]

        slots = nc.dram_tensor("slots", [E * REGION, ROW], F32, kind="Internal").ap()
        slots1 = nc.dram_tensor("slots1", [SEG * CAP, ROW], F32, kind="Internal").ap()
        result = nc.dram_tensor("result", [2 * TOK, D], F32, kind="Internal").ap()

        C = {n: cols[:, i:i + 1] for i, n in enumerate(
            ["bq0", "bk0", "ln1_g", "ln1_b", "ln2_g", "ln2_b", "ffn_g", "ffn_b", "bq3", "bv3"])}
        router = [cols[:, 10 + E * l:10 + E * (l + 1)] for l in range(LAYERS)]
        R = {n: i * P for i, n in enumerate(["bv0", "bo0", "bo2", "bv3", "ffn1"])}
        ebias = rows[:, 5 * P:5 * P + E]
        gates = rows[:, 5 * P + E:5 * P + E + 8]
        WQ = [attnw[:, 0, :], attnw[:, 4, :], blockw[:, 0, :], attnw[:, 9, :]]
        WK = [attnw[:, 1, :], attnw[:, 5, :], blockw[:, 1, :], attnw[:, 10, :]]
        WV = [attnw[:, 2, :], attnw[:, 6, :], blockw[:, 2, :], attnw[:, 10, :]]
        WO = [attnw[:, 3, :], attnw[:, 7, :], attnw[:, 8, :], None]
        SCALE = [HD ** -0.5, HD ** -0.5, D ** -0.5, 1.0]

        ld_small = sem("ld_small")
        ld_x = sem("ld_x")
        ld_w = [sem(f"ld_w{l}") for l in range(LAYERS)]
        zero_done = sem("zero_done")
        const = sem("const")
        blk_done = sem("blk_done")
        tg_done = sem("tg_done")
        names = ["c_stat", "c_rstd", "c_norm", "c_t", "c_T", "c_k", "c_kT", "c_v", "c_blk",
                 "a_stat", "a_rstd", "a_xn", "a_xt", "a_xT", "a_q", "a_qT", "a_s", "a_sub", "a_exp",
                 "a_pt", "a_pT", "a_pv", "a_o", "a_ot", "a_oT", "a_pr", "a_x", "x_done",
                 "r_stat", "r_rstd", "r_xf", "r_pay", "r_xt", "r_xT", "r_lg", "r_top", "r_ex", "r_pick", "r_rank",
                 "r_pos", "m_tab", "m_count",
                 "s_h", "s_gate", "s_act", "s_y", "s_x",
                 "t_x", "t_xT", "t_h", "t_pre", "t_hid", "t_ht", "t_hT", "t_y", "t_ysb", "t_id"]
        Z = {n: sem(n) for n in names}
        scat = [sem(f"scat{l}") for l in range(LAYERS)]
        padded = sem("padded")
        filled = [sem(f"filled{q}") for q in range(RING)]
        put = [sem(f"put{q}") for q in range(2)]
        back = [sem(f"back{g}") for g in range(NG)]
        out_done = sem("out_done")

        def grown(per_layer, l):
            return sum(per_layer[:l])

        NLN = [1, 2, 1, 1]
        NRN = [2, 1, 1, 1]
        NSH = [1, 0, 2, 0]
        PRE = [TILES[0], 0, TILES[2], TILES[3]]

        def tile_base(l, counts=TILES):
            return grown(counts, l)

        def ring_base(l, q, n=RING):
            return 16 * sum(len(range(q, TILES[i], n)) for i in range(l))

        def g_at(l, g):
            return l * NG + g

        def t_at(l, g, t):
            return (l * NG + g) * GT + t

        def steps(eng, tiles, step):
            turns = (tiles - 1 - RING) // RING
            for s in range(RING):
                step(s, s)
            with eng.Fori(0, turns) as turn:
                for k in range(RING, 2 * RING):
                    step(turn * RING + k, k, True)
            for s in range(RING + turns * RING, tiles + 2):
                step(s, s)

        block = ctx.enter_context(nc.Block())

        @block.sync
        def _(sp):
            sp.dma_start(ctx_sb[:], ctx_d).then_inc(ld_small, 16)
            sp.dma_start(cols[:], cols_d).then_inc(ld_small, 16)
            sp.dma_start(rows[:], rows_d.to_broadcast([P, 5 * P + 16])).then_inc(ld_small, 16)
            sp.dma_start(x[:], x_d.rearrange("(t p) d -> p t d", p=P)).then_inc(ld_x, 16)
            sp.dma_start(attnw[:], attnw_d).then_inc(ld_small, 16)
            for h in range(HEADS):
                sp.dma_start(small[h * HD:(h + 1) * HD], small_d).then_inc(ld_small, 16)
            sp.dma_start(mask_i[:], mask_d.rearrange("(t p) k -> p t k", p=P)).then_inc(ld_small, 16)
            sp.dma_start(w1[0][:], w1_d[0]).then_inc(ld_w[0], 16)
            sp.dma_start(w2[0][:, 0:(E + 1) * 2], w2_d[0]).then_inc(ld_w[0], 16)
            sp.wait_ge(const, 1)
            sp.dma_start(slots1.rearrange("(t p) d -> p t d", p=P),
                         zeros[:].unsqueeze(1).to_broadcast([P, SEG * CAP // P, ROW])).then_inc(zero_done, 16)
            for l in (1, 2):
                sp.dma_start(w1[l][:], w1_d[l]).then_inc(ld_w[l], 16)
                sp.dma_start(w2[l][:], w2_d[l]).then_inc(ld_w[l], 16)

            for l in range(LAYERS):
                src = slots1 if l == 1 else slots
                sp.wait_ge(Z["m_tab"], l + 1)
                sp.wait_ge(scat[l], 16 * TOPK[l] * NTILE)
                if l != 1:
                    npad = sum(1 for i in range(l + 1) if i != 1)
                    for e in range(E):
                        r = sp.value_load(pad_r[0:1, e:e + 1], min_val=0, max_val=E * REGION - P)
                        sp.dma_start(slots[bass.ds(r, P), :], zeros[:]).then_inc(padded, 16)
                    sp.wait_ge(padded, 16 * E * npad)
                else:
                    sp.wait_ge(zero_done, 16)
                tab = static_r if l == 1 else tab_r
                base = tile_base(l)

                def load(s, k, q):
                    r = sp.value_load(tab[0:1, bass.ds(s, 1)], min_val=0,
                                      max_val=(SEG * CAP if l == 1 else E * REGION) - P)
                    if k >= RING:
                        sp.wait_ge(Z["t_x"], s + (base - RING + 1))
                        sp.wait_ge(Z["t_id"], s + (base - RING + 1))
                    sp.dma_start(xg[:, q, :], src[bass.ds(r, P), :]).then_inc(filled[q], 16)

                n = TILES[l]
                turns = n // RING - 1
                for s in range(RING):
                    load(s, s, s)
                with sp.Fori(0, turns) as turn:
                    for k in range(RING):
                        load(turn * RING + (RING + k), RING, k)
                for s in range(RING * (turns + 1), n):
                    load(s, s, s % RING)
                for q in range(2):
                    sp.wait_ge(put[q], ring_base(l + 1, q, 2))
                for g in range(NG):
                    for k in range(TOPK[l]):
                        r0 = k * TOK + g * S
                        sp.dma_start(pay[:, k, g * GT:(g + 1) * GT, 0:D],
                                     result[r0:r0 + S, :].rearrange("(t p) d -> p t d", p=P)).then_inc(back[g], 16)
                if l == 0:
                    sp.dma_start(w1[3][:, 0:E], w1_d[3]).then_inc(ld_w[3], 16)
                    sp.dma_start(w2[3][:, 0:4 * E], w2_d[3]).then_inc(ld_w[3], 16)
                if l == 1:
                    sp.dma_start(b1, b1_d.to_broadcast([P, E * WIDE])).then_inc(ld_w[3], 16)
                    sp.dma_start(b2, b2_d.to_broadcast([P, E * D])).then_inc(ld_w[3], 16)
            for g in range(NG):
                sp.wait_ge(Z["x_done"], g + 1)
                sp.dma_start(out_d[g * S:(g + 1) * S, :].rearrange("(t p) d -> p t d", p=P),
                             x[:, g * GT:(g + 1) * GT]).then_inc(out_done, 16)
            sp.wait_ge(out_done, 16 * NG)

        @block.gpsimd
        def _(pool):
            pool.memset(zeros[:], 0.0).then_inc(const, 1)
            pool.memset(ident[:], 0.0)
            pool.memset(headmask[:], 1.0)
            pool.memset(chunkmask[:], 1.0)
            pool.memset(before[:], 1.0)
            pool.memset(onesb[:], 1.0)
            pool.memset(ones[:], 1.0)
            pool.memset(minus_half[:], -0.5)
            pool.memset(upper[:], 1.0)
            pool.iota(iota_e[:], [[1, E]], base=0, channel_multiplier=0, allow_small_or_imprecise_dtypes=True)
            pool.iota(region0[:], [[0, 2], [REGION, E]], base=0, channel_multiplier=0, allow_small_or_imprecise_dtypes=True)
            pool.iota(segment0[:], [[CAP, 2], [2 * CAP, E]], base=0, channel_multiplier=0, allow_small_or_imprecise_dtypes=True)
            pool.iota(slot128[:], [[P, NTILE]], base=0, channel_multiplier=0, allow_small_or_imprecise_dtypes=True)
            pool.iota(iota_t[:], [[1, MAXT]], base=0, channel_multiplier=0, allow_small_or_imprecise_dtypes=True)
            pool.iota(part[:], [[0, 1]], base=0, channel_multiplier=1, allow_small_or_imprecise_dtypes=True)
            pool.iota(nowhere[:], [[0, 1]], base=NOWHERE, channel_multiplier=1, allow_small_or_imprecise_dtypes=True)
            pool.iota(nowhere_i[:], [[0, 1]], base=NOWHERE, channel_multiplier=1)
            pool.iota(static_e[:, 0:TILES[1]], [[1, E], [0, TILES[1] // E]], base=0, channel_multiplier=0)
            pool.iota(static_r[:, 0:TILES[1]], [[P, TILES[1]]], base=0, channel_multiplier=0)
            pool.iota(seg_at[:], [[0, SEG], [P, CAP // P]], base=0, channel_multiplier=1, allow_small_or_imprecise_dtypes=True)
            pool.iota(pay[:, :, :, D], [[TOK, 2], [P, NTILE]], base=0, channel_multiplier=1, allow_small_or_imprecise_dtypes=True)
            pool.drain()
            pool.affine_select(out=ident[:], in_=ident[:], compare_op=ALU.not_equal, fill=1.0, base=0,
                               pattern=[[-1, P]], channel_multiplier=1)
            pool.affine_select(out=before[:], in_=before[:], compare_op=ALU.is_gt, fill=0.0, base=0,
                               pattern=[[1, P]], channel_multiplier=-1)
            pool.affine_select(out=upper[:], in_=upper[:], compare_op=ALU.is_ge, fill=0.0, base=0,
                               pattern=[[1, E], [-1, E]], channel_multiplier=0)
            pool.affine_select(out=headmask[:], in_=headmask[:], compare_op=ALU.is_ge, fill=0.0, base=0,
                               pattern=[[-HD, HEADS]], channel_multiplier=1)
            pool.affine_select(out=chunkmask[:], in_=chunkmask[:], compare_op=ALU.is_ge, fill=0.0, base=0,
                               pattern=[[-KEYS, HC]], channel_multiplier=1)
            pool.drain()
            pool.affine_select(out=headmask[:], in_=headmask[:], compare_op=ALU.is_ge, fill=0.0, base=HD - 1,
                               pattern=[[HD, HEADS]], channel_multiplier=-1)
            pool.affine_select(out=chunkmask[:], in_=chunkmask[:], compare_op=ALU.is_ge, fill=0.0, base=KEYS - 1,
                               pattern=[[KEYS, HC]], channel_multiplier=-1)
            pool.drain()
            pool.memset(mx[:, 0, 0:1], 0.0).then_inc(const, 1)

            def root(n, done_name, stat_name, width):
                pool.wait_ge(Z[stat_name], n)
                pool.tensor_scalar(rstd[:, 0:width], mv[:, 0:width, 1], EPS, None, ALU.add)
                pool.drain()
                pool.tensor_tensor(rstd[:, 0:width], rstd[:, 0:width], minus_half[:, 0:width],
                                   ALU.pow).then_inc(Z[done_name], 1)

            for l in range(LAYERS):
                if l == 0:
                    root(1, "c_rstd", "c_stat", 1)
                for g in range(NG):
                    for i in range(NLN[l]):
                        root(NG * grown(NLN, l) + NLN[l] * g + i + 1, "a_rstd", "a_stat", GT)
                    for i in range(NRN[l]):
                        root(NG * grown(NRN, l) + NRN[l] * g + i + 1, "r_rstd", "r_stat", GT)
                    pool.wait_ge(Z["r_pos"], g_at(l, g) + 1)
                    if l == 1 and g == 0:
                        pool.wait_ge(zero_done, 16)
                    for k in range(TOPK[l]):
                        for t in range(g * GT, (g + 1) * GT):
                            pool.indirect_dma_start(
                                out=(slots1 if l == 1 else slots)[:, :],
                                out_offset=bass.IndirectOffsetOnAxis(ap=pos[:, t, k:k + 1], axis=0),
                                in_=pay[:, k, t, :], in_offset=None,
                                bounds_check=(SEG * CAP if l == 1 else E * REGION) - 1, oob_is_err=False).then_inc(scat[l], 16)
                base = tile_base(l)

                def scatter(s, p):
                    pool.wait_ge(Z["t_ysb"], s + (base + 1))
                    pool.wait_ge(Z["t_id"], s + (base + 1))
                    pool.tensor_tensor(idu[:, p:p + 1], idf[:, p:p + 1], nowhere_i[:], ALU.add)
                    pool.drain()
                    pool.indirect_dma_start(
                        out=result[:, :], out_offset=bass.IndirectOffsetOnAxis(ap=idu[:, p:p + 1].bitcast(U32), axis=0),
                        in_=ysb[:, p, :], in_offset=None,
                        bounds_check=2 * TOK - 1, oob_is_err=False).then_inc(put[p], 16)

                with pool.Fori(0, TILES[l] // 2) as turn:
                    for p in range(2):
                        scatter(turn * 2 + p, p)
                if TILES[l] % 2:
                    scatter(TILES[l] - 1, 0)

        @block.tensor
        def _(pe):
            pe.wait_ge(const, 2)
            pe.wait_ge(ld_small, 16 * (5 + HEADS))

            def context(l):
                src = ctxTn if l == 1 else ctxT
                if l == 0:
                    pe.transpose(bank[0][:, 0:P], ctx_sb[:], ident[:])
                    pe.wait_ge(Z["c_norm"], 1)
                    pe.transpose(bank[0][:, P:2 * P], ctxn[:], ident[:]).then_inc(Z["c_t"], 1)
                    pe.wait_ge(Z["c_T"], 1)
                if l == 2:
                    pe.wait_ge(blk_done, 1)
                pe.matmul(bank[1][:, 0:P], WK[l], src[:], start=True, stop=True).then_inc(Z["c_k"], 1)
                if l < 3:
                    for b in range(B):
                        keys = ctxR[:, 1 if l == 1 else 0, b].rearrange("p j k -> p (j k)")
                        last = pe.matmul(bank[2][:, b * P:(b + 1) * P], keys, WV[l], start=True, stop=l != 0)
                        if l == 0:
                            last = pe.matmul(bank[2][:, b * P:(b + 1) * P], ones[:],
                                             rows[0:1, R["bv0"]:R["bv0"] + P], start=False, stop=True)
                else:
                    for b in range(B):
                        pe.matmul(bank[2][0:KEYS, b * P:(b + 1) * P], src[:, b * KEYS:(b + 1) * KEYS], WV[l],
                                  start=True, stop=False)
                        last = pe.matmul(bank[2][0:KEYS, b * P:(b + 1) * P], ones[:, 0:KEYS],
                                         rows[0:1, R["bv3"]:R["bv3"] + P], start=False, stop=True)
                last.then_inc(Z["c_v"], 1)
                pe.wait_ge(Z["c_blk"], l + 1)

            def attention(l, g):
                pe.wait_ge(Z["a_xn"], g_at(l, g) + 1)
                for t in range(GT):
                    last = pe.transpose(bank[0][:, t * P:(t + 1) * P], xn[:, t, :], ident[:])
                last.then_inc(Z["a_xt"], 1)
                pe.wait_ge(Z["a_xT"], g_at(l, g) + 1)
                pe.matmul(bank[1][:], WQ[l], xT[:], start=True, stop=True).then_inc(Z["a_q"], 1)
                pe.wait_ge(Z["a_qT"], g_at(l, g) + 1)
                if l == 3:
                    for t in range(GT):
                        last = pe.matmul(bank[2][:, t * KEYS:(t + 1) * KEYS], qT[:, t * P:(t + 1) * P],
                                         kT[:, g * KEYS:(g + 1) * KEYS], start=True, stop=True)
                    last.then_inc(Z["a_s"], 1)
                    pe.wait_ge(Z["a_o"], t_at(3, 0, 0) + g + 1)
                    for t in range(GT):
                        last = pe.transpose(bank[4][0:KEYS, t * P:(t + 1) * P], prob[:, 0, t, :], ident[:])
                    last.then_inc(Z["a_pt"], 1)
                    pe.wait_ge(Z["a_pT"], t_at(3, 0, 0) + g + 1)
                    for t in range(GT):
                        last = pe.matmul(bank[6][:, t * P:(t + 1) * P], probT[0:KEYS, 0, t, :], v3[:, g, :],
                                         start=True, stop=True)
                    last.then_inc(Z["a_pr"], 1)
                    return
                for s in range(GT + 4):
                    if s < GT:
                        t = s
                        if t >= 2:
                            pe.wait_ge(Z["a_sub"], t_at(l, g, t - 2) + 1)
                        pe.matmul(bank[2 + t % 2][:], qT[:, t * P:(t + 1) * P],
                                  kblk[:, g].rearrange("p h k -> p (h k)"), start=True, stop=True).then_inc(Z["a_s"], 1)
                    if 0 <= s - 1 < GT:
                        t = s - 1
                        pe.wait_ge(Z["a_exp"], t_at(l, g, t) + 1)
                        if t >= 2:
                            pe.wait_ge(Z["a_pT"], t_at(l, g, t - 2) + 1)
                        pt = prob[:, t % 2].rearrange("p (c j) k -> p c (j k)", c=NC)
                        for c in range(NC):
                            last = pe.transpose(bank[4 + t % 2][:, c * P:(c + 1) * P], pt[:, c, :], ident[:])
                        last.then_inc(Z["a_pt"], 1)
                    if 0 <= s - 2 < GT:
                        t = s - 2
                        pe.wait_ge(Z["a_pT"], t_at(l, g, t) + 1)
                        if t >= 1:
                            pe.wait_ge(Z["a_o"], t_at(l, g, t - 1) + 1)
                        for c in range(NC):
                            last = pe.matmul(bank[6][:, c * VW:(c + 1) * VW], probT[:, t % 2, c, :], vblk[:, g, c, :],
                                             start=True, stop=True)
                        last.then_inc(Z["a_pv"], 1)
                    if 0 <= s - 3 < GT:
                        t = s - 3
                        pe.wait_ge(Z["a_o"], t_at(l, g, t) + 1)
                        if t >= 2:
                            pe.wait_ge(Z["a_oT"], t_at(l, g, t - 2) + 1)
                        pe.transpose(bank[t % 2][:, 0:P], o[:, t % 2, :], ident[:]).then_inc(Z["a_ot"], 1)
                    if 0 <= s - 4 < GT:
                        t = s - 4
                        pe.wait_ge(Z["a_oT"], t_at(l, g, t) + 1)
                        if t >= 1:
                            pe.wait_ge(Z["a_x"], t_at(l, g, t - 1) + 1)
                        last = pe.matmul(bank[7][:, 0:P], oT[:, t % 2, :], WO[l], start=True, stop=l == 1)
                        if l != 1:
                            r = R["bo0" if l == 0 else "bo2"]
                            last = pe.matmul(bank[7][:, 0:P], ones[:], rows[0:1, r:r + P], start=False, stop=True)
                        last.then_inc(Z["a_pr"], 1)

            def route(l, g):
                n = NG * grown(NRN, l) + NRN[l] * g
                pe.wait_ge(Z["r_xf"], n + 1)
                for t in range(GT):
                    last = pe.transpose(bank[0][:, t * P:(t + 1) * P], pay[:, 0, g * GT + t, 0:D], ident[:])
                last.then_inc(Z["r_xt"], 1)
                if l == 0:
                    pe.wait_ge(Z["r_xf"], n + 2)
                    for t in range(GT):
                        last = pe.transpose(bank[1][:, t * P:(t + 1) * P], xn[:, t, :], ident[:])
                    last.then_inc(Z["r_xt"], 1)
                pe.wait_ge(Z["r_xT"], n + NRN[l])
                src = xT if l == 0 else xfT[:, g * S:(g + 1) * S]
                for t in range(GT):
                    last = pe.matmul(bank[6][:, t * E:(t + 1) * E], src[:, t * P:(t + 1) * P], router[l],
                                     start=True, stop=True)
                last.then_inc(Z["r_lg"], 1)
                pe.wait_ge(Z["r_pick"], g_at(l, g) + 1)
                for t in range(GT):
                    out = bank[7][:, t * SEG:(t + 1) * SEG]
                    here = picks[:, g, t].rearrange("p k e -> p (k e)")
                    pe.matmul(out, before[:], here, start=True, stop=g + t == 0)
                    for u in range(g * GT + t):
                        last = pe.matmul(out, onesb[:], picks[:, u // GT, u % GT].rearrange("p k e -> p (k e)"),
                                         start=False, stop=u == g * GT + t - 1)
                last.then_inc(Z["r_rank"], 1)
                if g == NG - 1:
                    for u in range(NTILE):
                        last = pe.matmul(bank[1][:, 0:SEG], onesb[:], picks[:, u // GT, u % GT].rearrange("p k e -> p (k e)"),
                                         start=u == 0, stop=u == NTILE - 1)
                    last.then_inc(Z["m_count"], 1)

            def shared(l, g):
                for j in range(NSH[l]):
                    n = 2 * (NG * grown(NSH, l) + NSH[l] * g + j)
                    for c in range(2):
                        if n + c >= 2:
                            pe.wait_ge(Z["s_act"], n + c - 1)
                        pe.matmul(bank[2 + c][:], w1[l][:, E + j, c * P:(c + 1) * P], xfT[:, g * S:(g + 1) * S],
                                  start=True, stop=True)
                        pe.matmul(bank[4 + c][:], w1[l][:, E + j, (2 + c) * P:(3 + c) * P], xfT[:, g * S:(g + 1) * S],
                                  start=True, stop=True).then_inc(Z["s_h"], 1)
                done = 2 * (NG * grown(NSH, l) + NSH[l] * (g + 1))
                pe.wait_ge(Z["s_act"], done)
                m = (0 if l == 0 else NG) + g
                if m >= 2:
                    pe.wait_ge(Z["s_x"], m - 1)
                n = 2 * NSH[l]
                for t in range(GT):
                    for c in range(n):
                        last = pe.matmul(bank[6 + g % 2][:, t * P:(t + 1) * P], hsh[:, c, t * P:(t + 1) * P],
                                         w2[l][:, E * 2 + c, :], start=c == 0, stop=c == n - 1)
                last.then_inc(Z["s_y"], 1)

            def experts(l):
                base = tile_base(l)
                nf = FC[l]
                tab = static_e if l == 1 else tab_e
                w1f = w1[l][:].rearrange("p e n -> p (e n)")
                w2f = w2[l][:].rearrange("p c n -> p (c n)")

                def transpose_x(s, k):
                    q = k % RING
                    pe.wait_ge(filled[q], (s + (RING - q)) * (16 // RING) + ring_base(l, q))
                    if k >= 2:
                        pe.wait_ge(Z["t_xT"], s + (base - 1))
                    pe.transpose(bank[k % 2][:, 0:P], xg[:, q, 0:D], ident[:]).then_inc(Z["t_x"], 1)

                def first(s, k):
                    e = pe.value_load(tab[0:1, bass.ds(s, 1)], min_val=0, max_val=E - 1)
                    pe.wait_ge(Z["t_xT"], s + (base + 1))
                    if k >= 2:
                        pe.wait_ge(Z["t_hid"] if l != 3 else Z["t_pre"],
                                   s + (base - 1) if l != 3 else s + (tile_base(3, PRE) - 1))
                    pe.matmul(bank[2 + k % 2][:], xgT[:, k % 2, :], w1f[:, bass.ds(e * WIDE, WIDE)],
                              start=True, stop=True).then_inc(Z["t_h"], 1)

                def transpose_h(s, k):
                    pe.wait_ge(Z["t_hid"], s + (base + 1))
                    if k >= 2:
                        pe.wait_ge(Z["t_hT"], s + (base - 1))
                    for c in range(nf):
                        last = pe.transpose(bank[4 + k % 2][:, c * P:(c + 1) * P], hid[:, k % 2, c * P:(c + 1) * P],
                                            ident[:])
                    last.then_inc(Z["t_ht"], 1)

                def second(s, k):
                    e = pe.value_load(tab[0:1, bass.ds(s, 1)], min_val=0, max_val=E - 1)
                    pe.wait_ge(Z["t_hT"], s + (base + 1))
                    if k >= 2:
                        pe.wait_ge(Z["t_ysb"], s + (base - 1))
                    for c in range(nf):
                        last = pe.matmul(bank[6 + k % 2][:, 0:D], hidT[:, k % 2, c, :],
                                         w2f[:, bass.ds(e * (nf * D) + c * D, D)], start=c == 0, stop=c == nf - 1)
                    last.then_inc(Z["t_y"], 1)

                n = TILES[l]
                transpose_x(0, 0)

                def step(s, k, full=False):
                    if full or k < n:
                        first(s, k)
                    if full or 0 <= k - 1 < n:
                        transpose_h(s - 1, k - 1)
                    if full or 0 <= k - 2 < n:
                        second(s - 2, k - 2)
                    if full or k + 1 < n:
                        transpose_x(s + 1, k + 1)

                steps(pe, n, step)

            for l in range(LAYERS):
                context(l)
                for g in range(NG):
                    attention(l, g)
                    route(l, g)
                pe.wait_ge(ld_w[l], 16 * (4 if l == 3 else 2))
                if NSH[l]:
                    for g in range(NG):
                        shared(l, g)
                pe.wait_ge(Z["m_tab"], l + 1)
                experts(l)

        @block.scalar
        def _(act):
            act.wait_ge(ld_small, 16 * (5 + HEADS))
            act.activation(tg[:], gates, ACT.Tanh).then_inc(tg_done, 1)

            def context(l):
                if l == 0:
                    act.wait_ge(Z["c_t"], 1)
                    act.copy(ctxT[:], bank[0][:, 0:P])
                    act.activation(ctxTn[:], bank[0][:, P:2 * P], ACT.Identity, bias=C["ln1_b"],
                                       scale=C["ln1_g"])
                    act.drain()
                    for i, src in enumerate((ctxT, ctxTn)):
                        for b in range(B):
                            last = act.copy(ctxR[:, i, b], src[:, b * KEYS:(b + 1) * KEYS].unsqueeze(1)
                                            .to_broadcast([P, HC, KEYS]))
                    last.then_inc(Z["c_T"], 1)
                act.wait_ge(Z["c_k"], l + 1)
                if l in (0, 3):
                    act.activation(kT[:], bank[1][:, 0:P], ACT.Identity,
                                   bias=C["bk0" if l == 0 else "bv3"]).then_inc(Z["c_kT"], 1)
                else:
                    act.copy(kT[:], bank[1][:, 0:P]).then_inc(Z["c_kT"], 1)

            def attention(l, g):
                act.wait_ge(Z["a_xt"], g_at(l, g) + 1)
                if l == 1:
                    act.activation(xT[:], bank[0][:], ACT.Identity, bias=C["ln2_b"], scale=C["ln2_g"]).then_inc(Z["a_xT"], 1)
                else:
                    act.copy(xT[:], bank[0][:]).then_inc(Z["a_xT"], 1)
                act.wait_ge(Z["a_q"], g_at(l, g) + 1)
                if l in (0, 3):
                    act.activation(qT[:], bank[1][:], ACT.Identity,
                                   bias=C["bq0" if l == 0 else "bq3"]).then_inc(Z["a_qT"], 1)
                else:
                    act.copy(qT[:], bank[1][:]).then_inc(Z["a_qT"], 1)
                if l == 3:
                    act.wait_ge(Z["a_sub"], t_at(3, 0, 0) + g + 1)
                    act.activation(prob[:, 0, 0:GT, :], prob[:, 0, 0:GT, :], ACT.Exp).then_inc(Z["a_exp"], 1)
                    act.wait_ge(Z["a_pt"], t_at(3, 0, 0) + g + 1)
                    act.copy(probT[0:KEYS, 0].rearrange("p t n -> p (t n)"), bank[4][0:KEYS, :]).then_inc(Z["a_pT"], 1)
                    return
                for s in range(GT + 3):
                    if s < GT:
                        act.wait_ge(Z["a_sub"], t_at(l, g, s) + 1)
                        act.activation(prob[:, s % 2], prob[:, s % 2], ACT.Exp, scale=SCALE[l]).then_inc(Z["a_exp"], 1)
                    if 0 <= s - 1 < GT:
                        t = s - 1
                        act.wait_ge(Z["a_pt"], t_at(l, g, t) + 1)
                        if t >= 2:
                            act.wait_ge(Z["a_pv"], t_at(l, g, t - 2) + 1)
                        act.copy(probT[:, t % 2].rearrange("p c n -> p (c n)"), bank[4 + t % 2][:]).then_inc(Z["a_pT"], 1)
                    if 0 <= s - 3 < GT:
                        t = s - 3
                        act.wait_ge(Z["a_ot"], t_at(l, g, t) + 1)
                        if t >= 2:
                            act.wait_ge(Z["a_pr"], t_at(l, g, t - 2) + 1)
                        act.copy(oT[:, t % 2, :], bank[t % 2][:, 0:P]).then_inc(Z["a_oT"], 1)

            def route(l, g):
                n = NG * grown(NRN, l) + NRN[l] * g
                act.wait_ge(Z["r_xt"], n + 1)
                act.copy(xfT[:, g * S:(g + 1) * S], bank[0][:]).then_inc(Z["r_xT"], 1)
                if l == 0:
                    act.wait_ge(Z["r_xt"], n + 2)
                    act.activation(xT[:], bank[1][:], ACT.Identity, bias=C["ffn_b"], scale=C["ffn_g"]).then_inc(Z["r_xT"], 1)
                act.wait_ge(Z["r_top"], g_at(l, g) + 1)
                act.activation(ex[:], ex[:], ACT.Exp).then_inc(Z["r_ex"], 1)

            def shared(l, g):
                for j in range(NSH[l]):
                    n = 2 * (NG * grown(NSH, l) + NSH[l] * g + j)
                    for c in range(2):
                        act.wait_ge(Z["s_h"], n + c + 1)
                        if n + c >= 2:
                            act.wait_ge(Z["s_act"], n + c - 1)
                        act.activation(gat[:, c, :], bank[2 + c][:], ACT.Silu).then_inc(Z["s_gate"], 1)

            def experts(l):
                base = tile_base(l)
                pbase = tile_base(l, PRE)

                def copy_x(s, k):
                    act.wait_ge(Z["t_x"], s + (base + 1))
                    if k >= 2:
                        act.wait_ge(Z["t_h"], s + (base - 1))
                    act.copy(xgT[:, k % 2, :], bank[k % 2][:, 0:P]).then_inc(Z["t_xT"], 1)

                def function(s, k):
                    p = k % 2
                    if l in (0, 2):
                        act.wait_ge(Z["t_h"], s + (base + 1))
                        if k >= 2:
                            act.wait_ge(Z["t_hid"], s + (base - 1))
                        act.activation(pre[:, p, 0:256], bank[2 + p][:, 0:256], ACT.Silu).then_inc(Z["t_pre"], 1)
                        return
                    if k >= 2:
                        act.wait_ge(Z["t_ht"], s + (base - 1))
                    if l == 1:
                        act.wait_ge(Z["t_h"], s + (base + 1))
                        act.activation(hid[:, p, :], bank[2 + p][:], ACT.Gelu_apprx_tanh).then_inc(Z["t_hid"], 1)
                    else:
                        act.wait_ge(Z["t_pre"], s + (pbase + 1))
                        act.activation(hid[:, p, :], pre[:, p, :], ACT.Gelu).then_inc(Z["t_hid"], 1)

                n = TILES[l]
                copy_x(0, 0)

                def step(s, k, full=False):
                    if full or k < n:
                        function(s, k)
                    if full or k + 1 < n:
                        copy_x(s + 1, k + 1)

                steps(act, n, step)

            for l in range(LAYERS):
                context(l)
                for g in range(NG):
                    attention(l, g)
                    route(l, g)
                if NSH[l]:
                    for g in range(NG):
                        shared(l, g)
                experts(l)

        @block.vector
        def _(dve):
            dve.wait_ge(const, 2)

            def norm(src, width, stat_name, rstd_name, n, dst):
                for t in range(width):
                    dve.bn_stats(stat[:, t, :], src(t))
                dve.drain()
                for t in range(width):
                    last = dve.bn_aggr(mv[:, t, :], stat[:, t, :])
                last.then_inc(Z[stat_name], 1)
                dve.wait_ge(Z[rstd_name], n)
                for t in range(width):
                    last = dve.tensor_scalar(dst(t), src(t), mv[:, t, 0:1], rstd[:, t:t + 1], ALU.subtract, ALU.mult)
                return last

            def context(l):
                if l == 0:
                    dve.wait_ge(ld_small, 16 * (5 + HEADS))
                    norm(lambda t: ctx_sb[:], 1, "c_stat", "c_rstd", 1, lambda t: ctxn[:]).then_inc(Z["c_norm"], 1)
                    dve.tensor_copy(vblk[:, :, :, HC * HD:VW].rearrange("p b c j -> p (b c) j"),
                                    chunkmask[:].unsqueeze(1).to_broadcast([P, B * NC, HC]))
                    for i in range(3):
                        last = dve.tensor_tensor(blockw[:, i, :].rearrange("p (h e) -> p h e", h=HEADS),
                                                 small[:, i, :].unsqueeze(1).to_broadcast([P, HEADS, HD]),
                                                 headmask[:].unsqueeze(2).to_broadcast([P, HEADS, HD]), ALU.mult)
                    last.then_inc(blk_done, 1)
                    dve.tensor_scalar(maskb[:], mask_i[:], 0.0, -1e20, ALU.is_equal, ALU.mult)
                    dve.wait_ge(tg_done, 1)
                    dve.tensor_scalar(brow[:], rows[:, R["ffn1"]:R["ffn1"] + P], tg[:, 5:6], None, ALU.mult)
                if l < 3:
                    dve.wait_ge(Z["c_kT"], l + 1)
                    for b in range(B):
                        dve.tensor_tensor(kblk[:, b],
                                          kT[:, b * KEYS:(b + 1) * KEYS].unsqueeze(1).to_broadcast([P, HEADS, KEYS]),
                                          headmask[:].unsqueeze(2).to_broadcast([P, HEADS, KEYS]), ALU.mult)
                    dve.wait_ge(Z["c_v"], l + 1)
                    for b in range(B):
                        last = dve.tensor_tensor(
                            vblk[:, b, :, 0:HC * HD].rearrange("p c (j d) -> p c j d", j=HC),
                            bank[2][:, b * P:(b + 1) * P].rearrange("p (c j d) -> p c j d", c=NC, j=HC),
                            chunkmask[:].unsqueeze(1).unsqueeze(3).to_broadcast([P, NC, HC, HD]), ALU.mult)
                    last.then_inc(Z["c_blk"], 1)
                else:
                    dve.wait_ge(Z["c_kT"], l + 1)
                    dve.wait_ge(Z["c_v"], l + 1)
                    dve.tensor_copy(v3[:].rearrange("p b d -> p (b d)"), bank[2][0:KEYS, :]).then_inc(Z["c_blk"], 1)

            def attention(l, g):
                tiles = range(g * GT, (g + 1) * GT)
                n = NG * grown(NLN, l) + NLN[l] * g
                last = norm(lambda t: x[:, tiles[t], :], GT, "a_stat", "a_rstd", n + 1, lambda t: xn[:, t, :])
                if l == 1:
                    dve.drain()
                    last = norm(lambda t: xn[:, t, :], GT, "a_stat", "a_rstd", n + 2, lambda t: xn[:, t, :])
                last.then_inc(Z["a_xn"], 1)
                gate = tg[:, l:l + 1]
                if l == 3:
                    dve.wait_ge(Z["a_s"], t_at(3, 0, 0) + g + 1)
                    sc = bank[2][:, 0:GT * KEYS].rearrange("p (t k) -> p t k", t=GT)
                    dve.tensor_reduce(mx[:, 0, 0:GT], sc, AX.X, ALU.max)
                    dve.drain()
                    dve.tensor_tensor(prob[:, 0, 0:GT, :], sc, mx[:, 0, 0:GT].unsqueeze(2).to_broadcast([P, GT, KEYS]),
                                      ALU.subtract).then_inc(Z["a_sub"], 1)
                    dve.wait_ge(Z["a_exp"], t_at(3, 0, 0) + g + 1)
                    dve.tensor_reduce(rinv[:, 0, 0:GT], prob[:, 0, 0:GT, :], AX.X, ALU.add)
                    dve.drain()
                    dve.reciprocal(rinv[:, 1, 0:GT], rinv[:, 0, 0:GT])
                    dve.drain()
                    dve.tensor_tensor(prob[:, 0, 0:GT, :], prob[:, 0, 0:GT, :],
                                      rinv[:, 1, 0:GT].unsqueeze(2).to_broadcast([P, GT, KEYS]),
                                      ALU.mult).then_inc(Z["a_o"], 1)
                    dve.wait_ge(Z["a_pr"], t_at(3, 0, 0) + g + 1)
                    dve.scalar_tensor_tensor(x[:, g * GT:(g + 1) * GT].rearrange("p t d -> p (t d)"), bank[6][:], gate,
                                             x[:, g * GT:(g + 1) * GT].rearrange("p t d -> p (t d)"),
                                             ALU.mult, ALU.add)
                    dve.drain()
                    return
                for s in range(GT + 4):
                    if s < GT:
                        t = s
                        dve.wait_ge(Z["a_s"], t_at(l, g, t) + 1)
                        sc = bank[2 + t % 2][:].rearrange("p (h k) -> p h k", h=HEADS)
                        if t >= 2:
                            dve.wait_ge(Z["a_pt"], t_at(l, g, t - 2) + 1)
                        if l == 2:
                            dve.tensor_tensor(prob[:, t % 2], sc,
                                              maskb[:, tiles[t], :].unsqueeze(1).to_broadcast([P, HEADS, KEYS]), ALU.add)
                            dve.drain()
                            sc = prob[:, t % 2]
                        dve.tensor_reduce(mx[:, t % 2, :], sc, AX.X, ALU.max)
                        dve.drain()
                        dve.tensor_tensor(prob[:, t % 2], sc, mx[:, t % 2, :].unsqueeze(2).to_broadcast([P, HEADS, KEYS]),
                                          ALU.subtract).then_inc(Z["a_sub"], 1)
                    if 0 <= s - 2 < GT:
                        t = s - 2
                        dve.wait_ge(Z["a_pv"], t_at(l, g, t) + 1)
                        pv = bank[6][:, 0:NC * VW].rearrange("p (c w) -> p c w", c=NC)
                        dve.reciprocal(rinv[:, t % 2, :].rearrange("p (c j) -> p c j", c=NC), pv[:, :, HC * HD:VW])
                        dve.drain()
                        if t >= 2:
                            dve.wait_ge(Z["a_ot"], t_at(l, g, t - 2) + 1)
                        dve.tensor_tensor(o[:, t % 2, :].rearrange("p (c j d) -> p c j d", c=NC, j=HC),
                                          pv[:, :, 0:HC * HD].rearrange("p c (j d) -> p c j d", j=HC),
                                          rinv[:, t % 2, :].rearrange("p (c j) -> p c j", c=NC).unsqueeze(3)
                                          .to_broadcast([P, NC, HC, HD]), ALU.mult).then_inc(Z["a_o"], 1)
                    if 0 <= s - 4 < GT:
                        t = s - 4
                        dve.wait_ge(Z["a_pr"], t_at(l, g, t) + 1)
                        dve.scalar_tensor_tensor(x[:, tiles[t], :], bank[7][:, 0:P], gate, x[:, tiles[t], :],
                                                 ALU.mult, ALU.add).then_inc(Z["a_x"], 1)
                dve.drain()

            def route(l, g):
                tiles = range(g * GT, (g + 1) * GT)
                ts = slice(g * GT, (g + 1) * GT)
                K = TOPK[l]
                n = NG * grown(NRN, l) + NRN[l] * g
                norm(lambda t: x[:, tiles[t], :], GT, "r_stat", "r_rstd", n + 1,
                     lambda t: pay[:, 0, tiles[t], 0:D]).then_inc(Z["r_xf"], 1)
                if K == 2:
                    dve.drain()
                    dve.tensor_copy(pay[:, 1, ts, 0:D], pay[:, 0, ts, 0:D])
                if l == 0:
                    norm(lambda t: pay[:, 0, tiles[t], 0:D], GT, "r_stat", "r_rstd", n + 2,
                         lambda t: xn[:, t, :]).then_inc(Z["r_xf"], 1)
                dve.wait_ge(Z["r_lg"], g_at(l, g) + 1)
                lg = bank[6][:, 0:GT * E].rearrange("p (t e) -> p t e", t=GT)
                if l == 2:
                    dve.tensor_tensor(logit[:], lg, ebias.unsqueeze(1).to_broadcast([P, GT, E]), ALU.add)
                else:
                    dve.tensor_copy(logit[:], lg)
                dve.drain()
                for t in range(GT):
                    dve.max(top[:, t, :], logit[:, t, :])
                dve.drain()
                dve.tensor_tensor(ex[:], top[:], top[:, :, 0:1].to_broadcast([P, GT, 8]), ALU.subtract).then_inc(Z["r_top"], 1)
                for t in range(GT):
                    dve.max_index(topi[:, t, :], top[:, t, :], logit[:, t, :])
                dve.drain()
                dve.tensor_copy(topf[:], topi[:, :, 0:2])
                dve.drain()
                for k in range(2):
                    dve.tensor_tensor(hot[:, :, k, :], iota_e[:].unsqueeze(1).to_broadcast([P, GT, E]),
                                      topf[:, :, k:k + 1].to_broadcast([P, GT, E]), ALU.is_equal)
                dve.drain()
                if l == 1:
                    last = dve.tensor_copy(picks[:, g], hot[:])
                elif K == 2:
                    for k in range(2):
                        last = dve.tensor_tensor(picks[:, g, :, k, :], hot[:, :, 0, :], hot[:, :, 1, :], ALU.add)
                else:
                    for k in range(2):
                        last = dve.tensor_copy(picks[:, g, :, k, :], hot[:, :, 0, :])
                last.then_inc(Z["r_pick"], 1)
                dve.wait_ge(Z["r_ex"], g_at(l, g) + 1)
                if l == 2:
                    dve.tensor_tensor(s4[:, :, 0], ex[:, :, 0], ex[:, :, 1], ALU.add)
                else:
                    dve.tensor_reduce(s4[:, :, 0], ex[:], AX.X, ALU.add)
                dve.drain()
                dve.reciprocal(s4[:, :, 1], s4[:, :, 0])
                dve.drain()
                dve.tensor_tensor(wts[:, ts, :], ex[:, :, 0:2], s4[:, :, 1:2].to_broadcast([P, GT, 2]), ALU.mult)
                dve.drain()
                if l == 0:
                    dve.tensor_tensor(s4[:, :, 0], wts[:, ts, 0], wts[:, ts, 1], ALU.add)
                    dve.drain()
                    dve.tensor_scalar(s4[:, :, 0], s4[:, :, 0], EPS, None, ALU.add)
                    dve.drain()
                    dve.reciprocal(s4[:, :, 1], s4[:, :, 0])
                    dve.drain()
                    dve.tensor_tensor(wts[:, ts, :], wts[:, ts, :], s4[:, :, 1:2].to_broadcast([P, GT, 2]), ALU.mult)
                    dve.drain()
                dve.tensor_scalar(wts[:, ts, :], wts[:, ts, :], tg[:, 4 + l:5 + l], None, ALU.mult)
                dve.wait_ge(Z["r_rank"], g_at(l, g) + 1)
                rk = bank[7][:, 0:GT * SEG].rearrange("p (t k e) -> p t (k e)", t=GT, k=2)
                hk = hot[:].rearrange("p t k e -> p t (k e)")
                pk = place[:].rearrange("p t k e -> p t (k e)")
                first = (segment0 if l == 1 else region0)[:].rearrange("p k e -> p (k e)")
                if l == 1:
                    dve.tensor_tensor(pk, rk, hk, ALU.mult)
                    dve.drain()
                    dve.tensor_reduce(rank[:], place[:], AX.X, ALU.add)
                    dve.drain()
                    dve.tensor_scalar(rank[:], rank[:], float(CAP), None, ALU.is_lt)
                    dve.drain()
                    dve.tensor_tensor(wts[:, ts, :], wts[:, ts, :], rank[:], ALU.mult)
                dve.tensor_tensor(pk, rk, first.unsqueeze(1).to_broadcast([P, GT, SEG]), ALU.add)
                dve.drain()
                dve.tensor_tensor(pk, pk, hk, ALU.mult)
                dve.drain()
                dve.tensor_reduce(posf[:], place[:], AX.X, ALU.add)
                dve.drain()
                if l == 1:
                    dve.tensor_scalar(posf[:], posf[:], nowhere[:], None, ALU.subtract)
                    dve.drain()
                    dve.tensor_tensor(posf[:], posf[:], rank[:], ALU.mult)
                    dve.drain()
                    dve.tensor_scalar(pos[:, ts, :], posf[:], nowhere[:], None, ALU.add).then_inc(Z["r_pos"], 1)
                else:
                    dve.tensor_copy(pos[:, ts, :], posf[:]).then_inc(Z["r_pos"], 1)

            def tables(l):
                dve.wait_ge(Z["m_count"], l + 1)
                if l == 1:
                    dve.tensor_copy(count[:], bank[1][:, 0:SEG])
                    dve.drain()
                    n = TILES[1]
                    dve.tensor_tensor(valid[:, 0:n].rearrange("p (e k j) -> p e k j", e=E, k=2),
                                      count[:].rearrange("p (k e) -> p e k", k=2).unsqueeze(3).to_broadcast([P, E, 2, CAP // P]),
                                      seg_at[:].rearrange("p (e k j) -> p e k j", e=E, k=2), ALU.is_gt).then_inc(Z["m_tab"], 1)
                    dve.drain()
                    return
                n = TILES[l]
                cnt = count[:, 0:E]
                dve.tensor_copy(cnt, bank[1][:, 0:E])
                dve.drain()
                dve.tensor_tensor(pad_f[:], cnt, region0[:, 0, :], ALU.add)
                dve.tensor_tensor(cmp1[:], cnt.unsqueeze(2).to_broadcast([P, E, NTILE]),
                                  slot128[:].unsqueeze(1).to_broadcast([P, E, NTILE]), ALU.is_gt)
                dve.drain()
                dve.tensor_copy(pad_r[:], pad_f[0:1, :])
                dve.tensor_reduce(ntil[:], cmp1[:], AX.X, ALU.add)
                dve.drain()
                dve.tensor_tensor(cmp2[:], upper[:], ntil[:].unsqueeze(1).to_broadcast([P, E, E]), ALU.mult)
                dve.drain()
                dve.tensor_reduce(cum[:], cmp2[:], AX.X, ALU.add)
                dve.drain()
                dve.tensor_tensor(cumx[:], cum[:], ntil[:], ALU.subtract)
                it = iota_t[:, 0:n].unsqueeze(2).to_broadcast([P, n, E])
                dve.tensor_tensor(ge_in[:, 0:n], it, cum[:].unsqueeze(1).to_broadcast([P, n, E]), ALU.is_ge)
                dve.drain()
                dve.tensor_tensor(ge_ex[:, 0:n], it, cumx[:].unsqueeze(1).to_broadcast([P, n, E]), ALU.is_ge)
                dve.tensor_reduce(te[:, 0:n], ge_in[:, 0:n], AX.X, ALU.add)
                dve.tensor_tensor(tw[:, 0:n], ge_in[:, 0:n], ntil[:].unsqueeze(1).to_broadcast([P, n, E]), ALU.mult)
                dve.drain()
                dve.tensor_reduce(tb[:, 0:n], tw[:, 0:n], AX.X, ALU.add)
                dve.tensor_tensor(ge_ex[:, 0:n], ge_ex[:, 0:n], ge_in[:, 0:n], ALU.subtract)
                dve.tensor_scalar(te[:, 0:n], te[:, 0:n], float(E - 1), None, ALU.min)
                dve.drain()
                dve.tensor_copy(tab_e[:, 0:n], te[0:1, 0:n])
                dve.tensor_tensor(tw[:, 0:n], ge_ex[:, 0:n], cnt.unsqueeze(1).to_broadcast([P, n, E]), ALU.mult)
                dve.tensor_tensor(tb[:, 0:n], iota_t[:, 0:n], tb[:, 0:n], ALU.subtract)
                dve.drain()
                dve.tensor_scalar(tb[:, 0:n], tb[:, 0:n], float(NTILE - 1), float(P), ALU.min, ALU.mult)
                dve.tensor_reduce(tn[:, 0:n], tw[:, 0:n], AX.X, ALU.add)
                dve.drain()
                dve.scalar_tensor_tensor(tb[:, 0:n], tn[:, 0:n], 0.0, tb[:, 0:n], ALU.is_gt, ALU.mult)
                dve.drain()
                dve.scalar_tensor_tensor(tabf[:, 0:n], te[:, 0:n], float(REGION), tb[:, 0:n], ALU.mult, ALU.add)
                dve.tensor_scalar(tb[:, 0:n], tb[:, 0:n], part[:], None, ALU.add)
                dve.drain()
                dve.tensor_tensor(valid[:, 0:n], tn[:, 0:n], tb[:, 0:n], ALU.is_gt)
                dve.tensor_copy(tab_r[:, 0:n], tabf[0:1, 0:n]).then_inc(Z["m_tab"], 1)
                dve.drain()

            def shared(l, g):
                for j in range(NSH[l]):
                    n = 2 * (NG * grown(NSH, l) + NSH[l] * g + j)
                    for c in range(2):
                        dve.wait_ge(Z["s_gate"], n + c + 1)
                        m = (0 if l == 0 else NG) + g
                        if m:
                            dve.wait_ge(Z["s_y"], m)
                        dve.tensor_tensor(hsh[:, 2 * j + c, :], gat[:, c, :], bank[4 + c][:], ALU.mult).then_inc(Z["s_act"], 1)
                m = (0 if l == 0 else NG) + g
                dve.wait_ge(Z["s_y"], m + 1)
                xs = x[:, g * GT:(g + 1) * GT].rearrange("p t d -> p (t d)")
                dve.scalar_tensor_tensor(xs, bank[6 + g % 2][:], tg[:, 4 + l:5 + l], xs, ALU.mult,
                                         ALU.add).then_inc(Z["s_x"], 1)

            def experts(l):
                base = tile_base(l)
                pbase = tile_base(l, PRE)
                nf = FC[l]
                n = TILES[l]

                def ids(s, k):
                    p, q = k % 2, k % RING
                    dve.wait_ge(filled[q], (s + (RING - q)) * (16 // RING) + ring_base(l, q))
                    if k >= 2:
                        dve.wait_ge(put[p], (s - p) * 8 + ring_base(l, p, 2))
                    dve.tensor_scalar(idf[:, p:p + 1], xg[:, q, D:D + 1], nowhere[:], valid[:, bass.ds(s, 1)],
                                      ALU.subtract, ALU.mult).then_inc(Z["t_id"], 1)

                def gate_up(s, k):
                    p = k % 2
                    dve.wait_ge(Z["t_pre"], s + (pbase + 1))
                    if k >= 2:
                        dve.wait_ge(Z["t_ht"], s + (base - 1))
                    dve.tensor_tensor(hid[:, p, 0:256], pre[:, p, 0:256], bank[2 + p][:, 256:512], ALU.mult).then_inc(Z["t_hid"], 1)

                def bias(s, k):
                    p = k % 2
                    e = dve.value_load(tab_e[0:1, bass.ds(s, 1)], min_val=0, max_val=E - 1)
                    dve.wait_ge(Z["t_h"], s + (base + 1))
                    if k >= 2:
                        dve.wait_ge(Z["t_hid"], s + (base - 1))
                    dve.tensor_tensor(pre[:, p, :], bank[2 + p][:], b1[:, bass.ds(e * WIDE, WIDE)], ALU.add).then_inc(Z["t_pre"], 1)

                def copy_h(s, k):
                    p = k % 2
                    dve.wait_ge(Z["t_ht"], s + (base + 1))
                    if k >= 2:
                        dve.wait_ge(Z["t_y"], s + (base - 1))
                    dve.tensor_copy(hidT[:, p, 0:nf].rearrange("p c n -> p (c n)"), bank[4 + p][:, 0:nf * P]).then_inc(Z["t_hT"], 1)

                def copy_y(s, k):
                    p = k % 2
                    if l == 3:
                        e = dve.value_load(tab_e[0:1, bass.ds(s, 1)], min_val=0, max_val=E - 1)
                    dve.wait_ge(Z["t_y"], s + (base + 1))
                    if k >= 2:
                        dve.wait_ge(put[p], (s - p) * 8 + ring_base(l, p, 2))
                    if l == 3:
                        dve.tensor_tensor(ysb[:, p, :], bank[6 + p][:, 0:D], b2[:, bass.ds(e * D, D)], ALU.add).then_inc(Z["t_ysb"], 1)
                    else:
                        dve.tensor_copy(ysb[:, p, :], bank[6 + p][:, 0:D]).then_inc(Z["t_ysb"], 1)

                def step(s, k, full=False):
                    if full or 0 <= k - 1 < n:
                        copy_h(s - 1, k - 1)
                    if full or 0 <= k - 2 < n:
                        ids(s - 2, k - 2)
                        copy_y(s - 2, k - 2)
                    if full or k < n:
                        if l in (0, 2):
                            gate_up(s, k)
                        elif l == 3:
                            bias(s, k)

                steps(dve, n, step)

            def combine(l, g):
                dve.wait_ge(back[g], 16 * sum(TOPK[:l + 1]))
                for k in range(TOPK[l]):
                    for t in range(g * GT, (g + 1) * GT):
                        last = dve.scalar_tensor_tensor(x[:, t, :], pay[:, k, t, 0:D], wts[:, t, k:k + 1], x[:, t, :],
                                                        ALU.mult, ALU.add)
                    dve.drain()
                if l == 1:
                    xs = x[:, g * GT:(g + 1) * GT]
                    dve.tensor_tensor(xs, xs, brow[:].unsqueeze(1).to_broadcast([P, GT, D]), ALU.add)
                    dve.drain()
                if l == LAYERS - 1:
                    last.then_inc(Z["x_done"], 1)

            for l in range(LAYERS):
                context(l)
                if l == 3:
                    dve.wait_ge(ld_w[3], 16 * 4)
                if l == 0:
                    dve.wait_ge(ld_x, 16)
                for g in range(NG):
                    if l:
                        combine(l - 1, g)
                    attention(l, g)
                    route(l, g)
                tables(l)
                if NSH[l]:
                    for g in range(NG):
                        shared(l, g)
                experts(l)
            for g in range(NG):
                combine(LAYERS - 1, g)


def kernel(**inputs):
    import numpy as np
    import concourse.bacc as bacc
    from concourse.bass_utils import run_bass_kernel_spmd

    a = {k: np.asarray(v) for k, v in inputs.items()}
    c = np.ascontiguousarray

    def columns(*names):
        return [a[n].reshape(P, 1) for n in names]

    def wide(*parts):
        return c(np.concatenate(parts, axis=2).transpose(1, 0, 2))

    def tall(w):
        e, f, d = w.shape
        return c(w.reshape(e, f // P, P, d).transpose(2, 0, 1, 3).reshape(P, e * (f // P), d))

    def stack(*ws):
        return np.concatenate([w if w.ndim == 3 else w[None] for w in ws], axis=0)

    cols = c(np.concatenate(columns("L0_xattn_bq", "L0_xattn_bk", "L1_xattn_ln1_g", "L1_xattn_ln1_b", "L1_xattn_ln2_g",
                                    "L1_xattn_ln2_b", "L0_ffn_ln_scale", "L0_ffn_ln_bias", "L3_xattn_bq", "L3_xattn_bv")
                            + [a["L0_ffn_gate_w"].T, a["L1_ffn_router_w"], a["L2_ffn_router_w"].T, a["L3_ffn_Wr"]], axis=1))
    rows = c(np.concatenate([a["L0_xattn_bv"], a["L0_xattn_bo"], a["L2_xattn_bout"], a["L3_xattn_bv"],
                             a["L1_ffn_bias"].reshape(-1), a["L2_ffn_expert_bias"], a["g_xattn"], a["g_ffn"]])[None])
    attnw = c(np.stack([a["L0_xattn_Wq"].T, a["L0_xattn_Wk"].T, a["L0_xattn_Wv"].T, a["L0_xattn_Wo"].T,
                        a["L1_xattn_Wq"], a["L1_xattn_Wk"], a["L1_xattn_Wv"], a["L1_xattn_Wfc"],
                        a["L2_xattn_Wout"].T, a["L3_xattn_Wq"], a["L3_xattn_Wv"]], axis=1))
    small = c(np.stack([a["L2_xattn_Wq"].T, a["L2_xattn_Wk"].T, a["L2_xattn_Wv"].T], axis=1))
    T = lambda w: w.transpose(0, 2, 1)
    w1 = [wide(stack(a["L0_ffn_Wg"], a["L0_ffn_sWg"]), stack(a["L0_ffn_Wu"], a["L0_ffn_sWu"])),
          wide(a["L1_ffn_w1"]),
          wide(stack(T(a["L2_ffn_w1"]), T(a["L2_ffn_sw1"])), stack(T(a["L2_ffn_w3"]), T(a["L2_ffn_sw3"]))),
          wide(a["L3_ffn_W1"])]
    w2 = [tall(stack(a["L0_ffn_Wd"], a["L0_ffn_sWd"])), tall(a["L1_ffn_w2"]),
          tall(stack(T(a["L2_ffn_w2"]), T(a["L2_ffn_sw2"]))), tall(a["L3_ffn_W2"])]
    arrays = {"x": c(a["x"].reshape(TOK, D)), "ctx": c(a["ctx_1024"].reshape(B * KEYS, D)),
              "mask": c(a["mask_Bx1xSxS2_ik1"].reshape(TOK, KEYS)), "cols": cols, "rows": rows, "attnw": attnw,
              "small": small, **{f"w1_{l}": w1[l] for l in range(LAYERS)}, **{f"w2_{l}": w2[l] for l in range(LAYERS)},
              "b1": c(a["L3_ffn_b1"].reshape(1, -1)), "b2": c(a["L3_ffn_b2"].reshape(1, -1))}
    nc = bacc.Bacc("TRN2", target_bir_lowering=False, num_devices=1)
    h = {n: nc.dram_tensor(f"in_{n}", v.shape, mybir.dt.from_np(v.dtype), kind="ExternalInput").ap()
         for n, v in arrays.items()}
    out = nc.dram_tensor("out_0", (TOK, D), F32, kind="ExternalOutput").ap()
    flamingo(nc, h["x"], h["ctx"], h["mask"], h["cols"], h["rows"], h["attnw"], h["small"],
             [h[f"w1_{l}"] for l in range(LAYERS)], [h[f"w2_{l}"] for l in range(LAYERS)], h["b1"], h["b2"], out)
    got = run_bass_kernel_spmd(nc, [{f"in_{n}": v for n, v in arrays.items()}], core_ids=[0])
    return got.results[0]["out_0"].reshape(B, S, D)
```

```python
import concourse.bass as bass
from concourse import mybir
from contextlib import ExitStack

F32 = mybir.dt.float32
BF16 = mybir.dt.bfloat16
I32 = mybir.dt.int32
U32 = mybir.dt.uint32
ALU = mybir.AluOpType
ACT = mybir.ActivationFunctionType
AX = mybir.AxisListType

P = 128
B, S, D, KEYS = 4, 512, 128, 32
TOK = B * S
NTILE = TOK // P
NG = B
GT = S // P
HEADS, HD = 16, 8
HC = P // KEYS
NC = HEADS // HC
VW = HC * HD + HC
E = 8
EPS = 1e-5
LAYERS = 4
TOPK = [2, 2, 2, 1]
WIDE = 512
FC = [2, 4, 2, 4]
CAP = TOK // E
SEG = 2 * E
REGION = TOK + P
ROW = P + 1
NOWHERE = 2 * TOK
TILES = [(k * TOK + E * (P - 1)) // P for k in TOPK]
TILES[1] = SEG * CAP // P
MAXT = max(TILES)
RING = 4


def flamingo(nc, x_d, ctx_d, mask_d, cols_d, rows_d, attnw_d, small_d, w1_d, w2_d, b1_d, b2_d, out_d):
    ctx = ExitStack()
    with ctx:
        def sb(name, shape, dt=F32):
            return ctx.enter_context(nc.sbuf_tensor(name, shape, dt))

        def sem(name):
            return ctx.enter_context(nc.semaphore(name))

        x = sb("x", [P, NTILE, D])
        ctx_sb = sb("ctx_sb", [P, D])
        ctxn = sb("ctxn", [P, D])
        ctxT = sb("ctxT", [P, P])
        ctxTn = sb("ctxTn", [P, P])
        ctxR = sb("ctxR", [P, 2, B, HC, KEYS])
        cols = sb("cols", [P, 10 + 4 * E])
        rows = sb("rows", [P, 5 * P + 8 + 8])
        attnw = sb("attnw", [P, 11, P])
        small = sb("small", [P, 3, HD])
        blockw = sb("blockw", [P, 3, P])
        tg = sb("tg", [P, 8])
        brow = sb("brow", [P, P])
        w1 = [sb("w1_0", [P, E + 1, WIDE]), sb("w1_1", [P, E, WIDE]), sb("w1_2", [P, E + 2, WIDE])]
        w2 = [sb("w2_0", [P, E * 4, D]), sb("w2_1", [P, E * 4, D]), sb("w2_2", [P, (E + 2) * 2, D])]
        w1.append(w1[0])
        w2.append(w2[0])
        b1 = w1[1][:].rearrange("p e n -> p (e n)")
        b2 = w2[1][:, 0:E].rearrange("p c n -> p (c n)")
        kT = sb("kT", [P, P])
        kblk = sb("kblk", [P, B, HEADS, KEYS])
        vblk = sb("vblk", [P, B, NC, VW])
        v3 = sb("v3", [KEYS, B, D])
        xn = sb("xn", [P, GT, D])
        xT = sb("xT", [P, S])
        qT = sb("qT", [P, 2, S])
        prob = sb("prob", [P, 2, HEADS, KEYS])
        probT = sb("probT", [P, 2, NC, P])
        o = sb("o", [P, 2, P])
        oT = sb("oT", [P, 2, P])
        xn2 = sb("xn2", [P, GT, D])
        xnT = sb("xnT", [P, S])
        stat = sb("stat", [P, 2 * GT, 6])
        mv = [sb(f"mv{i}", [P, 2 * GT, 2]) for i in range(2)]
        rstd = [sb(f"rstd{i}", [P, 2 * GT]) for i in range(2)]
        shift = [sb(f"shift{i}", [P, 2 * GT]) for i in range(2)]
        mx = sb("mx", [P, 2, HEADS])
        rinv = sb("rinv", [P, 2, HEADS])
        maskT = sb("maskT", [KEYS, TOK], BF16)
        every = sb("every", [KEYS, HEADS, KEYS], BF16)
        xfT = sb("xfT", [P, TOK])
        mask_i = xfT[0:KEYS, :].bitcast(I32)
        pay = sb("pay", [P, 2, NTILE, ROW])
        logit = sb("logit", [P, GT, E])
        top = sb("top", [P, GT, 8])
        topi = sb("topi", [P, GT, 8], U32)
        topf = sb("topf", [P, GT, 2])
        ex = sb("ex", [P, GT, 8])
        s4 = sb("s4", [P, GT, 2])
        wts = sb("wts", [P, NTILE, 2])
        hot = sb("hot", [P, GT, 2, E])
        picks = sb("picks", [P, NG, GT, 2, E], BF16)
        place = sb("place", [P, GT, 2, E])
        posf = sb("posf", [P, GT, 2])
        rank = sb("rank", [P, GT, 2])
        pos = sb("pos", [P, NTILE, 2], U32)
        rsum = sb("rsum", [P, SEG])
        radd = sb("radd", [P, SEG])
        count = sb("count", [P, SEG])
        ntil = sb("ntil", [P, E])
        cmp1 = sb("cmp1", [P, E, NTILE])
        cmp2 = sb("cmp2", [P, E, E])
        cum = sb("cum", [P, E])
        cumx = sb("cumx", [P, E])
        ge_in, ge_ex, tw = [prob[:].rearrange("p b h k -> p (b h k)")[:, i * MAXT * E:(i + 1) * MAXT * E]
                            .rearrange("p (t e) -> p t e", e=E) for i in range(3)]
        te = sb("te", [P, MAXT])
        tb = sb("tb", [P, MAXT])
        tn = sb("tn", [P, MAXT])
        valid = sb("valid", [P, MAXT])
        away = sb("away", [P, MAXT])
        tabf = sb("tabf", [P, MAXT])
        tab_e = sb("tab_e", [1, MAXT], I32)
        tab_r = sb("tab_r", [1, MAXT], I32)
        pad_f = sb("pad_f", [P, E])
        pad_r = sb("pad_r", [1, E], I32)
        gat = sb("gat", [P, 2, S])
        hsh = sb("hsh", [P, 4, S])
        xg = sb("xg", [P, RING, ROW])
        xgT = xnT[:, 0:2 * P].rearrange("p (b n) -> p b n", b=2)
        hid = hsh[:, 0:2]
        pre = hsh[:, 2:4]
        hidT = gat[:].rearrange("p b (c n) -> p b c n", c=4)
        ysb = xn2
        row = sb("row", [P, RING], U32)
        ident = sb("ident", [P, P])
        headmask = sb("headmask", [P, HEADS])
        chunkmask = sb("chunkmask", [P, HC])
        before = sb("before", [P, P], BF16)
        onesb = sb("onesb", [P, P], BF16)
        ones = sb("ones", [1, P])
        minus_half = sb("minus_half", [P, 2 * GT])
        iota_e = sb("iota_e", [P, E])
        region0 = sb("region0", [P, 2, E])
        segment0 = sb("segment0", [P, 2, E])
        slot128 = sb("slot128", [P, NTILE])
        iota_t = sb("iota_t", [P, MAXT])
        part = sb("part", [P, 1])
        upper = sb("upper", [P, E, E])
        sofar = sb("sofar", [P, SEG], BF16)
        seg_at = sb("seg_at", [P, TILES[1]])
        zeros = sb("zeros", [P, ROW])

        bank = [ctx.enter_context(nc.psum_tensor(f"bank{i}", [P, 512], F32)) for i in range(8)]

        slots = nc.dram_tensor("slots", [E * REGION, ROW], F32, kind="Internal").ap()
        slots1 = nc.dram_tensor("slots1", [SEG * CAP, ROW], F32, kind="Internal").ap()
        result = nc.dram_tensor("result", [2 * TOK, D], F32, kind="Internal").ap()

        C = {n: cols[:, i:i + 1] for i, n in enumerate(
            ["bq0", "bk0", "ln1_g", "ln1_b", "ln2_g", "ln2_b", "ffn_g", "ffn_b", "bq3", "bv3"])}
        router = [cols[:, 10 + E * l:10 + E * (l + 1)] for l in range(LAYERS)]
        R = {n: i * P for i, n in enumerate(["bv0", "bo0", "bo2", "bv3", "ffn1"])}
        ebias = rows[:, 5 * P:5 * P + E]
        gates = rows[:, 5 * P + E:5 * P + E + 8]
        WQ = [attnw[:, 0, :], attnw[:, 4, :], blockw[:, 0, :], attnw[:, 9, :]]
        WK = [attnw[:, 1, :], attnw[:, 5, :], blockw[:, 1, :], attnw[:, 10, :]]
        WV = [attnw[:, 2, :], attnw[:, 6, :], blockw[:, 2, :], attnw[:, 10, :]]
        WO = [attnw[:, 3, :], attnw[:, 7, :], attnw[:, 8, :], None]
        SCALE = [HD ** -0.5, HD ** -0.5, D ** -0.5, 1.0]

        ld_small = sem("ld_small")
        ld_x = sem("ld_x")
        ld_mask = sem("ld_mask")
        ld_heads = sem("ld_heads")
        ld_w = [sem(f"ld_w{l}") for l in range(LAYERS)]
        zero_done = sem("zero_done")
        const = sem("const")
        blk_done = sem("blk_done")
        tg_done = sem("tg_done")
        names = [
            "c_stat", "c_root", "c_norm", "c_t", "c_T", "c_k", "c_kT", "c_v", "c_blk",
            "a_stat", "a_root", "r_stat", "r_root", "stat2", "root2", "p_self",
            "a_sc", "a_sc2", "a_xt", "a_xT", "a_q", "a_qT", "a_s", "a_sub", "a_exp", "a_pt", "a_pT", "a_pv", "a_o",
            "a_ot", "a_oT", "a_pr", "a_x", "x_done",
            "r_sc", "r_rows", "r_sc2", "r_xt", "r_xT", "r_xt2", "r_xT2", "r_lg", "r_top", "r_ex", "r_pick", "r_rank", "r_pos",
            "m_tab",
            "s_h", "s_gate", "s_act", "s_y", "s_x",
            "t_x", "t_xT", "t_h", "t_pre", "t_hid", "t_ht", "t_hT", "t_y", "t_ysb", "t_id", "t_go"]
        Z = {n: sem(n) for n in names}
        scat = [sem(f"scat{l}") for l in range(LAYERS)]
        padded = sem("padded")
        filled = [sem(f"filled{q}") for q in range(RING)]
        put = [sem(f"put{q}") for q in range(RING)]
        back = [sem(f"back{g}") for g in range(NG)]
        out_done = sem("out_done")

        def grown(per_layer, l):
            return sum(per_layer[:l])

        NSH = [1, 0, 2, 0]
        PRE = [TILES[0], 0, TILES[2], TILES[3]]

        def tile_base(l, counts=TILES):
            return grown(counts, l)

        def ring_base(l, q, n=RING):
            return 16 * sum(len(range(q, TILES[i], n)) for i in range(l))

        def g_at(l, g):
            return l * NG + g

        def n_at(l, n):
            return l * NTILE + n

        def walk(l, tile, pieces):
            for s in range(-2 * GT, NTILE + 4 * GT):
                tile(l, s)
                for distance, groups, piece in pieces:
                    g = (s - distance) // GT
                    if (s - distance) % GT == 0 and g in groups:
                        piece(l, g)

        GROUPS = range(NG)

        def routed_at(l):
            return 6 if l == 3 else 10

        def numbers(engine, table, start, n, top):
            return nc.values_load_multi_w_load_instructions(
                table[0:1, bass.ds(start, n) if not isinstance(start, int) else slice(start, start + n)],
                engines=[engine], min_val=0, max_val=top,
                skip_runtime_bounds_check_because="the table's entries are clamped when it is made")[1]

        def steps(eng, tiles, step, engine=None):
            def experts_of(first, k, n):
                if engine is None:
                    return {}
                if engine[1] == 1:
                    return {k + i: (first + i) // RING if isinstance(first, int) else first + (k + i) // RING
                            for i in range(n)}
                return dict(zip(range(k, k + n), numbers(engine[0], tab_e, first, n, E - 1)))

            turns = (tiles - 1 - RING) // RING
            e = experts_of(0, 0, RING)
            for s in range(RING):
                step(s, s, e)
            with eng.Fori(0, turns) as turn:
                first = turn if engine is not None and engine[1] == 1 else turn * RING + (RING - 2)
                e = experts_of(first, RING - 2, RING + 2)
                for k in range(RING, 2 * RING):
                    step(turn * RING + k, k, e, True)
            s = RING + turns * RING
            e = experts_of(s - 2, s - 2, tiles - s + 2)
            for s in range(s, tiles + 2):
                step(s, s, e)

        block = ctx.enter_context(nc.Block())

        @block.sync
        def _(sp):
            sp.dma_start(x[:], x_d.rearrange("(t p) d -> p t d", p=P)).then_inc(ld_x, 16)
            sp.dma_start(ctx_sb[:], ctx_d).then_inc(ld_small, 16)
            sp.dma_start(cols[:], cols_d).then_inc(ld_small, 16)
            sp.dma_start(rows[:], rows_d.to_broadcast([P, 5 * P + 16])).then_inc(ld_small, 16)
            sp.dma_start(attnw[:], attnw_d).then_inc(ld_small, 16)
            sp.dma_start(mask_i, mask_d).then_inc(ld_mask, 16)
            sp.dma_start(w1[0][:], w1_d[0]).then_inc(ld_w[0], 16)
            sp.dma_start(w2[0][:, 0:(E + 1) * 2], w2_d[0]).then_inc(ld_w[0], 16)
            sp.wait_ge(const, 1)
            sp.dma_start(slots1.rearrange("(t p) d -> p t d", p=P),
                         zeros[:].unsqueeze(1).to_broadcast([P, SEG * CAP // P, ROW])).then_inc(zero_done, 16)
            for h in range(HEADS):
                sp.dma_start(small[h * HD:(h + 1) * HD], small_d).then_inc(ld_heads, 16)
            for l in (1, 2):
                sp.dma_start(w1[l][:], w1_d[l]).then_inc(ld_w[l], 16)
                sp.dma_start(w2[l][:], w2_d[l]).then_inc(ld_w[l], 16)

            for l in range(LAYERS):
                src = slots1 if l == 1 else slots
                sp.wait_ge(Z["m_tab"], l + 1)
                sp.wait_ge(scat[l], 16 * TOPK[l] * NTILE)
                if l != 1:
                    npad = sum(1 for i in range(l + 1) if i != 1)
                    for r in numbers(mybir.EngineType.SP, pad_r, 0, E, E * REGION - P):
                        sp.dma_start(slots[bass.ds(r, P), :], zeros[:]).then_inc(padded, 16)
                    sp.wait_ge(padded, 16 * E * npad)
                else:
                    sp.wait_ge(zero_done, 16)
                base = tile_base(l)

                def load(s, k, q, r):
                    if k >= RING:
                        sp.wait_ge(Z["t_x"], s + (base - RING + 1))
                        sp.wait_ge(Z["t_id"], s + (base - RING + 1))
                    sp.dma_start(xg[:, q, :], src[bass.ds(r, P), :]).then_inc(filled[q], 16)

                def starts(first, n):
                    if l == 1:
                        return [(first + i) * P for i in range(n)]
                    return numbers(mybir.EngineType.SP, tab_r, first, n, E * REGION - P)

                n = TILES[l]
                turns = n // RING - 1
                for s, r in enumerate(starts(0, RING)):
                    load(s, s, s, r)
                with sp.Fori(0, turns) as turn:
                    for k, r in enumerate(starts(turn * RING + RING, RING)):
                        load(turn * RING + (RING + k), RING, k, r)
                s = RING * (turns + 1)
                if s < n:
                    for k, r in enumerate(starts(s, n - s)):
                        load(s + k, s, k, r)
                for q in range(RING):
                    sp.wait_ge(put[q], ring_base(l + 1, q))
                for g in range(NG):
                    for k in range(TOPK[l]):
                        r0 = k * TOK + g * S
                        sp.dma_start(pay[:, k, g * GT:(g + 1) * GT, 0:D],
                                     result[r0:r0 + S, :].rearrange("(t p) d -> p t d", p=P)).then_inc(back[g], 16)
                if l == 0:
                    sp.dma_start(w1[3][:, 0:E], w1_d[3]).then_inc(ld_w[3], 16)
                    sp.dma_start(w2[3][:, 0:4 * E], w2_d[3]).then_inc(ld_w[3], 16)
                if l == 1:
                    sp.dma_start(b1, b1_d.to_broadcast([P, E * WIDE])).then_inc(ld_w[3], 16)
                    sp.dma_start(b2, b2_d.to_broadcast([P, E * D])).then_inc(ld_w[3], 16)
            for g in range(NG):
                sp.wait_ge(Z["x_done"], g + 1)
                sp.dma_start(out_d[g * S:(g + 1) * S, :].rearrange("(t p) d -> p t d", p=P),
                             x[:, g * GT:(g + 1) * GT]).then_inc(out_done, 16)
            sp.wait_ge(out_done, 16 * NG)

        @block.gpsimd
        def _(pool):
            pool.memset(zeros[:], 0.0).then_inc(const, 1)
            pool.memset(ident[:], 0.0)
            pool.memset(headmask[:], 1.0)
            pool.memset(chunkmask[:], 1.0)
            pool.memset(before[:], 1.0)
            pool.memset(onesb[:], 1.0)
            pool.memset(ones[:], 1.0)
            pool.memset(minus_half[:], -0.5)
            pool.memset(upper[:], 1.0)
            pool.memset(every[:], 0.0)
            pool.iota(iota_e[:], [[1, E]], base=0, channel_multiplier=0, allow_small_or_imprecise_dtypes=True)
            pool.iota(region0[:], [[0, 2], [REGION, E]], base=0, channel_multiplier=0, allow_small_or_imprecise_dtypes=True)
            pool.iota(segment0[:], [[CAP, 2], [2 * CAP, E]], base=0, channel_multiplier=0, allow_small_or_imprecise_dtypes=True)
            pool.iota(slot128[:], [[P, NTILE]], base=0, channel_multiplier=0, allow_small_or_imprecise_dtypes=True)
            pool.iota(iota_t[:], [[1, MAXT]], base=0, channel_multiplier=0, allow_small_or_imprecise_dtypes=True)
            pool.iota(part[:], [[0, 1]], base=0, channel_multiplier=1, allow_small_or_imprecise_dtypes=True)
            pool.iota(seg_at[:], [[0, SEG], [P, CAP // P]], base=0, channel_multiplier=1, allow_small_or_imprecise_dtypes=True)
            pool.iota(pay[:, :, :, D], [[TOK, 2], [P, NTILE]], base=0, channel_multiplier=1, allow_small_or_imprecise_dtypes=True)
            pool.drain()
            pool.affine_select(out=ident[:], in_=ident[:], compare_op=ALU.not_equal, fill=1.0, base=0,
                               pattern=[[-1, P]], channel_multiplier=1)
            pool.affine_select(out=before[:], in_=before[:], compare_op=ALU.is_gt, fill=0.0, base=0,
                               pattern=[[1, P]], channel_multiplier=-1)
            pool.affine_select(out=upper[:], in_=upper[:], compare_op=ALU.is_ge, fill=0.0, base=0,
                               pattern=[[1, E], [-1, E]], channel_multiplier=0)
            pool.affine_select(out=every[:], in_=every[:], compare_op=ALU.not_equal, fill=1.0, base=0,
                               pattern=[[0, HEADS], [-1, KEYS]], channel_multiplier=1)
            pool.affine_select(out=headmask[:], in_=headmask[:], compare_op=ALU.is_ge, fill=0.0, base=0,
                               pattern=[[-HD, HEADS]], channel_multiplier=1)
            pool.affine_select(out=chunkmask[:], in_=chunkmask[:], compare_op=ALU.is_ge, fill=0.0, base=0,
                               pattern=[[-KEYS, HC]], channel_multiplier=1)
            pool.drain()
            pool.affine_select(out=headmask[:], in_=headmask[:], compare_op=ALU.is_ge, fill=0.0, base=HD - 1,
                               pattern=[[HD, HEADS]], channel_multiplier=-1)
            pool.affine_select(out=chunkmask[:], in_=chunkmask[:], compare_op=ALU.is_ge, fill=0.0, base=KEYS - 1,
                               pattern=[[KEYS, HC]], channel_multiplier=-1)
            pool.drain()
            pool.sem_inc(const, 1)

            selfs = [0]

            def own(instruction):
                selfs[0] += 1
                instruction.then_inc(Z["p_self"], 1)
                pool.wait_ge(Z["p_self"], selfs[0])

            def roots(i, lo, hi, done):
                pool.tensor_scalar(shift[i][:, lo:hi], mv[i][:, lo:hi, 0], -1.0, None, ALU.mult)
                own(pool.tensor_scalar(rstd[i][:, lo:hi], mv[i][:, lo:hi, 1], EPS, None, ALU.add))
                own(pool.tensor_tensor(rstd[i][:, lo:hi], rstd[i][:, lo:hi], minus_half[:, lo:hi], ALU.pow))
                pool.tensor_tensor(shift[i][:, lo:hi], shift[i][:, lo:hi], rstd[i][:, lo:hi],
                                   ALU.mult).then_inc(done, 1)

            def root(l, g):
                pool.wait_ge(Z["a_stat"], g_at(l, g) + 1)
                if g_at(l, g):
                    pool.wait_ge(Z["a_sc"], g_at(l, g))
                roots(0, 0, GT, Z["a_root"])

            def root_routed(l, g):
                pool.wait_ge(Z["r_stat"], g_at(l, g) + 1)
                if g_at(l, g):
                    pool.wait_ge(Z["r_sc"], g_at(l, g))
                roots(0, GT, 2 * GT, Z["r_root"])

            def root2(l, g):
                pool.wait_ge(Z["stat2"], g_at(l, g) + 1)
                if g:
                    pool.wait_ge(Z["a_sc2" if l else "r_sc2"], g)
                roots(1, 0 if l else GT, GT if l else 2 * GT, Z["root2"])

            def scatter_rows(k):
                def scatter(l, g):
                    if k >= TOPK[l]:
                        return
                    pool.wait_ge(Z["r_pos"], g_at(l, g) + 1)
                    if k == 1:
                        pool.wait_ge(Z["r_rows"], g_at(l, g) + 1)
                    if l == 1 and g == 0 and k == 0:
                        pool.wait_ge(zero_done, 16)
                    for t in range(g * GT, (g + 1) * GT):
                        pool.indirect_dma_start(
                            out=(slots1 if l == 1 else slots)[:, :],
                            out_offset=bass.IndirectOffsetOnAxis(ap=pos[:, t, k:k + 1], axis=0),
                            in_=pay[:, k, t, :], in_offset=None,
                            bounds_check=(SEG * CAP if l == 1 else E * REGION) - 1, oob_is_err=False).then_inc(scat[l], 16)
                return scatter

            pool.wait_ge(Z["c_stat"], 1)
            roots(0, 0, 1, Z["c_root"])
            for l in range(LAYERS):
                route = routed_at(l)
                walk(l, lambda l, s: None, [
                    (-8, GROUPS, root),
                    (route - 1, GROUPS, root_routed),
                    (-6 if l else route + 1, GROUPS if l < 2 else (), root2),
                    (route + (4 if l else 6), GROUPS, scatter_rows(0)),
                    (route + (4 if l else 6), GROUPS, scatter_rows(1))])
                base = tile_base(l)

                def scatter(s, q):
                    pool.wait_ge(Z["t_ysb"], s + (base + 1))
                    pool.wait_ge(Z["t_id"], s + (base + 1))
                    pool.sem_inc(Z["t_go"], 1)
                    pool.indirect_dma_start(
                        out=result[:, :], out_offset=bass.IndirectOffsetOnAxis(ap=row[:, q:q + 1], axis=0),
                        in_=ysb[:, q, :], in_offset=None,
                        bounds_check=2 * TOK - 1, oob_is_err=False).then_inc(put[q], 16)

                with pool.Fori(0, TILES[l] // RING) as turn:
                    for q in range(RING):
                        scatter(turn * RING + q, q)
                for s in range(TILES[l] // RING * RING, TILES[l]):
                    scatter(s, s % RING)

        @block.tensor
        def _(pe):
            pe.wait_ge(const, 2)
            pe.wait_ge(ld_small, 16 * 4)

            def context(l):
                src = ctxTn if l == 1 else ctxT
                if l == 0:
                    pe.transpose(bank[0][:, 0:P], ctx_sb[:], ident[:])
                    pe.wait_ge(Z["c_norm"], 1)
                    pe.transpose(bank[0][:, P:2 * P], ctxn[:], ident[:]).then_inc(Z["c_t"], 1)
                    pe.wait_ge(Z["c_T"], 1)
                if l == 2:
                    pe.wait_ge(blk_done, 1)
                pe.matmul(bank[0][:, 0:P], WK[l], src[:], start=True, stop=True).then_inc(Z["c_k"], 1)
                if l < 3:
                    for b in range(B):
                        keys = ctxR[:, 1 if l == 1 else 0, b].rearrange("p j k -> p (j k)")
                        last = pe.matmul(bank[2][:, b * P:(b + 1) * P], keys, WV[l], start=True, stop=l != 0)
                        if l == 0:
                            last = pe.matmul(bank[2][:, b * P:(b + 1) * P], ones[:],
                                             rows[0:1, R["bv0"]:R["bv0"] + P], start=False, stop=True)
                else:
                    for b in range(B):
                        pe.matmul(bank[2][0:KEYS, b * P:(b + 1) * P], src[:, b * KEYS:(b + 1) * KEYS], WV[l],
                                  start=True, stop=False)
                        last = pe.matmul(bank[2][0:KEYS, b * P:(b + 1) * P], ones[:, 0:KEYS],
                                         rows[0:1, R["bv3"]:R["bv3"] + P], start=False, stop=True)
                last.then_inc(Z["c_v"], 1)
                pe.wait_ge(Z["c_blk"], l + 1)

            def transpose_tokens(l, g):
                if l == 1:
                    pe.wait_ge(Z["a_sc2"], g + 1)
                else:
                    pe.wait_ge(Z["a_sc"], g_at(l, g) + 1)
                for t in range(GT):
                    last = pe.transpose(bank[0][:, t * P:(t + 1) * P], xn[:, t, :], ident[:])
                last.then_inc(Z["a_xt"], 1)

            def queries(l, g):
                pe.wait_ge(Z["a_xT"], g_at(l, g) + 1)
                pe.matmul(bank[0][:], WQ[l], xT[:], start=True, stop=True).then_inc(Z["a_q"], 1)

            def tile(l, s):
                if l == 3:
                    return
                if 0 <= s - 1 < NTILE:
                    n, N = s - 1, n_at(l, s - 1)
                    pe.wait_ge(Z["a_exp"], N + 1)
                    if N >= 1:
                        pe.wait_ge(Z["a_pT"], N)
                    pt = prob[:, n % 2].rearrange("p (c j) k -> p c (j k)", c=NC)
                    for c in range(NC):
                        last = pe.transpose(bank[4][:, c * P:(c + 1) * P], pt[:, c, :], ident[:])
                    last.then_inc(Z["a_pt"], 1)
                if 0 <= s - 4 < NTILE:
                    n, N = s - 4, n_at(l, s - 4)
                    pe.wait_ge(Z["a_o"], N + 1)
                    if N >= 1:
                        pe.wait_ge(Z["a_oT"], N)
                    pe.transpose(bank[5][:, 0:P], o[:, n % 2, :], ident[:]).then_inc(Z["a_ot"], 1)
                if 0 <= s - 5 < NTILE:
                    n, N = s - 5, n_at(l, s - 5)
                    pe.wait_ge(Z["a_oT"], N + 1)
                    if N >= 1:
                        pe.wait_ge(Z["a_x"], N)
                    last = pe.matmul(bank[7][:, 0:P], oT[:, n % 2, :], WO[l], start=True, stop=l == 1)
                    if l != 1:
                        r = R["bo0" if l == 0 else "bo2"]
                        last = pe.matmul(bank[7][:, 0:P], ones[:], rows[0:1, r:r + P], start=False, stop=True)
                    last.then_inc(Z["a_pr"], 1)
                if 0 <= s + 1 < NTILE:
                    n, N, g = s + 1, n_at(l, s + 1), (s + 1) // GT
                    pe.wait_ge(Z["a_qT"], g_at(l, g) + 1)
                    if N >= 2:
                        pe.wait_ge(Z["a_sub"], N - 1)
                    out = bank[2 + n % 2][:]
                    last = pe.matmul(out, qT[:, g % 2, n % GT * P:(n % GT + 1) * P],
                                     kblk[:, g].rearrange("p h k -> p (h k)"), start=True, stop=l != 2)
                    if l == 2:
                        last = pe.matmul(out, maskT[:, n * P:(n + 1) * P], every[:].rearrange("k h i -> k (h i)"),
                                         start=False, stop=True)
                    last.then_inc(Z["a_s"], 1)
                if 0 <= s - 2 < NTILE:
                    n, N = s - 2, n_at(l, s - 2)
                    pe.wait_ge(Z["a_pT"], N + 1)
                    if N >= 1:
                        pe.wait_ge(Z["a_o"], N)
                    for c in range(NC):
                        last = pe.matmul(bank[6][:, c * VW:(c + 1) * VW], probT[:, n % 2, c, :], vblk[:, n // GT, c, :],
                                         start=True, stop=True)
                    last.then_inc(Z["a_pv"], 1)

            def scores3(l, g):
                pe.wait_ge(Z["a_qT"], g_at(l, g) + 1)
                pe.wait_ge(Z["a_sub"], n_at(3, g))
                for t in range(GT):
                    last = pe.matmul(bank[2][:, t * KEYS:(t + 1) * KEYS], qT[:, g % 2, t * P:(t + 1) * P],
                                     kT[:, g * KEYS:(g + 1) * KEYS], start=True, stop=True)
                last.then_inc(Z["a_s"], 1)

            def transpose3(l, g):
                pe.wait_ge(Z["a_o"], n_at(3, g) + 1)
                pe.wait_ge(Z["a_pT"], n_at(3, g))
                for t in range(GT):
                    last = pe.transpose(bank[4][0:KEYS, t * P:(t + 1) * P], prob[:, 0, t, :], ident[:])
                last.then_inc(Z["a_pt"], 1)

            def values3(l, g):
                pe.wait_ge(Z["a_pT"], n_at(3, g) + 1)
                pe.wait_ge(Z["a_x"], n_at(3, g))
                for t in range(GT):
                    last = pe.matmul(bank[6][:, t * P:(t + 1) * P], probT[0:KEYS, 0, t, :], v3[:, g, :],
                                     start=True, stop=True)
                last.then_inc(Z["a_pr"], 1)

            def transpose_routed(l, g):
                pe.wait_ge(Z["r_sc"], g_at(l, g) + 1)
                if g_at(l, g):
                    pe.wait_ge(Z["r_pos"], g_at(l, g))
                for t in range(GT):
                    last = pe.transpose(bank[1][:, t * P:(t + 1) * P], pay[:, 0, g * GT + t, 0:D], ident[:])
                last.then_inc(Z["r_xt"], 1)

            def transpose_routed2(l, g):
                pe.wait_ge(Z["r_sc2"], g + 1)
                pe.wait_ge(Z["r_xT"], g_at(l, g) + 1)
                for t in range(GT):
                    last = pe.transpose(bank[1][:, t * P:(t + 1) * P], xn2[:, t, :], ident[:])
                last.then_inc(Z["r_xt2"], 1)

            def logits(l, g):
                if l == 0:
                    pe.wait_ge(Z["r_xT2"], g + 1)
                else:
                    pe.wait_ge(Z["r_xT"], g_at(l, g) + 1)
                src = xnT if l == 0 else xfT[:, g * S:(g + 1) * S]
                for t in range(GT):
                    last = pe.matmul(bank[1][:, t * E:(t + 1) * E], src[:, t * P:(t + 1) * P], router[l],
                                     start=True, stop=True)
                last.then_inc(Z["r_lg"], 1)

            def ranks(l, g):
                pe.wait_ge(Z["r_pick"], g_at(l, g) + 1)
                out = bank[1][:, 0:GT * SEG].rearrange("p (t n) -> p t n", t=GT)
                now = picks[:, g].rearrange("p t k e -> p t (k e)")
                last = pe.matmul(out, before[:], now, start=True, stop=False)
                for t in range(GT - 1):
                    last = pe.matmul(out[:, t + 1:], onesb[:], now[:, t:t + 1].to_broadcast([P, GT - 1 - t, SEG]),
                                     start=False, stop=g == 0 and t == GT - 2)
                if g:
                    last = pe.matmul(out, onesb[:], sofar[:].unsqueeze(1).to_broadcast([P, GT, SEG]),
                                     start=False, stop=True)
                if g == NG - 1:
                    total = bank[1][:, GT * SEG:(GT + 1) * SEG]
                    pe.matmul(total, onesb[:], sofar[:], start=True, stop=False)
                    for t in range(GT):
                        last = pe.matmul(total, onesb[:], now[:, t], start=False, stop=t == GT - 1)
                last.then_inc(Z["r_rank"], 1)

            def shared(l, g):
                for j in range(NSH[l]):
                    n = 2 * (NG * grown(NSH, l) + NSH[l] * g + j)
                    for c in range(2):
                        if n + c >= 2:
                            pe.wait_ge(Z["s_act"], n + c - 1)
                        pe.matmul(bank[2 + c][:], w1[l][:, E + j, c * P:(c + 1) * P], xfT[:, g * S:(g + 1) * S],
                                  start=True, stop=True)
                        pe.matmul(bank[4 + c][:], w1[l][:, E + j, (2 + c) * P:(3 + c) * P], xfT[:, g * S:(g + 1) * S],
                                  start=True, stop=True).then_inc(Z["s_h"], 1)
                done = 2 * (NG * grown(NSH, l) + NSH[l] * (g + 1))
                pe.wait_ge(Z["s_act"], done)
                m = (0 if l == 0 else NG) + g
                if m >= 2:
                    pe.wait_ge(Z["s_x"], m - 1)
                n = 2 * NSH[l]
                for t in range(GT):
                    for c in range(n):
                        last = pe.matmul(bank[6 + g % 2][:, t * P:(t + 1) * P], hsh[:, c, t * P:(t + 1) * P],
                                         w2[l][:, E * 2 + c, :], start=c == 0, stop=c == n - 1)
                last.then_inc(Z["s_y"], 1)

            def experts(l):
                base = tile_base(l)
                nf = FC[l]
                w1f = w1[l][:].rearrange("p e n -> p (e n)")
                w2f = w2[l][:].rearrange("p c n -> p (c n)")

                def transpose_x(s, k):
                    q = k % RING
                    pe.wait_ge(filled[q], (s + (RING - q)) * (16 // RING) + ring_base(l, q))
                    if k >= 2:
                        pe.wait_ge(Z["t_xT"], s + (base - 1))
                    pe.transpose(bank[k % 2][:, 0:P], xg[:, q, 0:D], ident[:]).then_inc(Z["t_x"], 1)

                def first(s, k, e):
                    pe.wait_ge(Z["t_xT"], s + (base + 1))
                    if k >= 2:
                        pe.wait_ge(Z["t_hid"] if l != 3 else Z["t_pre"],
                                   s + (base - 1) if l != 3 else s + (tile_base(3, PRE) - 1))
                    pe.matmul(bank[2 + k % 2][:], xgT[:, k % 2, :], w1f[:, bass.ds(e * WIDE, WIDE)],
                              start=True, stop=True).then_inc(Z["t_h"], 1)

                def transpose_h(s, k):
                    pe.wait_ge(Z["t_hid"], s + (base + 1))
                    if k >= 2:
                        pe.wait_ge(Z["t_hT"], s + (base - 1))
                    for c in range(nf):
                        last = pe.transpose(bank[4 + k % 2][:, c * P:(c + 1) * P], hid[:, k % 2, c * P:(c + 1) * P],
                                            ident[:])
                    last.then_inc(Z["t_ht"], 1)

                def second(s, k, e):
                    pe.wait_ge(Z["t_hT"], s + (base + 1))
                    if k >= 2:
                        pe.wait_ge(Z["t_ysb"], s + (base - 1))
                    for c in range(nf):
                        last = pe.matmul(bank[6 + k % 2][:, 0:D], hidT[:, k % 2, c, :],
                                         w2f[:, bass.ds(e * (nf * D) + c * D, D)], start=c == 0, stop=c == nf - 1)
                    last.then_inc(Z["t_y"], 1)

                n = TILES[l]
                transpose_x(0, 0)

                def step(s, k, e, full=False):
                    if full or k < n:
                        first(s, k, e[k])
                    if full or k + 1 < n:
                        transpose_x(s + 1, k + 1)
                    if full or 0 <= k - 1 < n:
                        transpose_h(s - 1, k - 1)
                    if full or 0 <= k - 2 < n:
                        second(s - 2, k - 2, e[k - 2])

                steps(pe, n, step, (mybir.EngineType.PE, l))

            context(0)
            for l in range(LAYERS):
                three = GROUPS if l == 3 else ()
                route = routed_at(l)
                walk(l, tile, [
                    (-4 if l == 1 else -6, GROUPS, transpose_tokens),
                    (-3 if l == 1 else -5, GROUPS, queries),
                    (0, three, scores3), (2, three, transpose3), (3, three, values3),
                    (route + (1 if l else 2), GROUPS, transpose_routed),
                    (route + 3, GROUPS if l == 0 else (), transpose_routed2),
                    (route + (2 if l else 4), GROUPS, logits),
                    (route + (3 if l else 5), GROUPS, ranks)])
                if l + 1 < LAYERS:
                    context(l + 1)
                pe.wait_ge(ld_w[l], 16 * (4 if l == 3 else 2))
                if NSH[l]:
                    for g in range(NG):
                        shared(l, g)
                pe.wait_ge(Z["m_tab"], l + 1)
                experts(l)

        @block.scalar
        def _(act):
            act.wait_ge(ld_small, 16 * 4)
            act.activation(tg[:], gates, ACT.Tanh).then_inc(tg_done, 1)

            def context(l):
                if l == 0:
                    act.wait_ge(Z["c_t"], 1)
                    act.copy(ctxT[:], bank[0][:, 0:P])
                    act.activation(ctxTn[:], bank[0][:, P:2 * P], ACT.Identity, bias=C["ln1_b"],
                                       scale=C["ln1_g"])
                    act.drain()
                    for i, src in enumerate((ctxT, ctxTn)):
                        for b in range(B):
                            last = act.copy(ctxR[:, i, b], src[:, b * KEYS:(b + 1) * KEYS].unsqueeze(1)
                                            .to_broadcast([P, HC, KEYS]))
                    last.then_inc(Z["c_T"], 1)
                act.wait_ge(Z["c_k"], l + 1)
                if l in (0, 3):
                    act.activation(kT[:], bank[0][:, 0:P], ACT.Identity,
                                   bias=C["bk0" if l == 0 else "bv3"]).then_inc(Z["c_kT"], 1)
                else:
                    act.copy(kT[:], bank[0][:, 0:P]).then_inc(Z["c_kT"], 1)

            def scale(dst, src, i, lo, done):
                for t in range(GT):
                    last = act.activation(dst(t), src(t), ACT.Identity, bias=shift[i][:, lo + t:lo + t + 1],
                                          scale=rstd[i][:, lo + t:lo + t + 1])
                last.then_inc(done, 1)

            def scale_tokens(l, g):
                act.wait_ge(Z["a_root"], g_at(l, g) + 1)
                if g_at(l, g):
                    act.wait_ge(Z["a_xt"], g_at(l, g))
                scale(lambda t: xn[:, t, :], lambda t: x[:, g * GT + t, :], 0, 0, Z["a_sc"])

            def scale_tokens2(l, g):
                act.wait_ge(Z["root2"], g_at(l, g) + 1)
                scale(lambda t: xn[:, t, :], lambda t: xn[:, t, :], 1, 0, Z["a_sc2"])

            def scale_routed(l, g):
                act.wait_ge(Z["r_root"], g_at(l, g) + 1)
                scale(lambda t: pay[:, 0, g * GT + t, 0:D], lambda t: x[:, g * GT + t, :], 0, GT, Z["r_sc"])

            def scale_routed2(l, g):
                act.wait_ge(Z["root2"], g_at(l, g) + 1)
                if g:
                    act.wait_ge(Z["r_xt2"], g)
                scale(lambda t: xn2[:, t, :], lambda t: pay[:, 0, g * GT + t, 0:D], 1, GT, Z["r_sc2"])

            def copy_tokens(l, g):
                act.wait_ge(Z["a_xt"], g_at(l, g) + 1)
                if g_at(l, g):
                    act.wait_ge(Z["a_q"], g_at(l, g))
                if l == 1:
                    act.activation(xT[:], bank[0][:], ACT.Identity, bias=C["ln2_b"], scale=C["ln2_g"]).then_inc(Z["a_xT"], 1)
                else:
                    act.copy(xT[:], bank[0][:]).then_inc(Z["a_xT"], 1)

            def copy_queries(l, g):
                act.wait_ge(Z["a_q"], g_at(l, g) + 1)
                if l in (0, 3):
                    act.activation(qT[:, g % 2], bank[0][:], ACT.Identity,
                                   bias=C["bq0" if l == 0 else "bq3"]).then_inc(Z["a_qT"], 1)
                else:
                    act.copy(qT[:, g % 2], bank[0][:]).then_inc(Z["a_qT"], 1)

            def tile(l, s):
                if l == 3:
                    return
                if 0 <= s - 1 < NTILE:
                    n, N = s - 1, n_at(l, s - 1)
                    act.wait_ge(Z["a_pt"], N + 1)
                    if N >= 2:
                        act.wait_ge(Z["a_pv"], N - 1)
                    act.copy(probT[:, n % 2].rearrange("p c n -> p (c n)"), bank[4][:]).then_inc(Z["a_pT"], 1)
                if 0 <= s - 4 < NTILE:
                    n, N = s - 4, n_at(l, s - 4)
                    act.wait_ge(Z["a_ot"], N + 1)
                    if N >= 2:
                        act.wait_ge(Z["a_pr"], N - 1)
                    act.copy(oT[:, n % 2, :], bank[5][:, 0:P]).then_inc(Z["a_oT"], 1)
                if 0 <= s < NTILE:
                    act.wait_ge(Z["a_sub"], n_at(l, s) + 1)
                    act.activation(prob[:, s % 2], prob[:, s % 2], ACT.Exp, scale=SCALE[l]).then_inc(Z["a_exp"], 1)

            def exp3(l, g):
                act.wait_ge(Z["a_sub"], n_at(3, g) + 1)
                act.activation(prob[:, 0, 0:GT, :], prob[:, 0, 0:GT, :], ACT.Exp).then_inc(Z["a_exp"], 1)

            def copy3(l, g):
                act.wait_ge(Z["a_pt"], n_at(3, g) + 1)
                act.wait_ge(Z["a_pr"], n_at(3, g))
                act.copy(probT[0:KEYS, 0].rearrange("p t n -> p (t n)"), bank[4][0:KEYS, :]).then_inc(Z["a_pT"], 1)

            def copy_routed(l, g):
                act.wait_ge(Z["r_xt"], g_at(l, g) + 1)
                act.copy(xfT[:, g * S:(g + 1) * S], bank[1][:]).then_inc(Z["r_xT"], 1)
                if TOPK[l] == 2:
                    act.wait_ge(Z["r_sc"], g_at(l, g) + 1)
                    act.copy(pay[:, 1, g * GT:(g + 1) * GT, 0:D],
                             pay[:, 0, g * GT:(g + 1) * GT, 0:D]).then_inc(Z["r_rows"], 1)

            def copy_routed2(l, g):
                act.wait_ge(Z["r_xt2"], g + 1)
                if g:
                    act.wait_ge(Z["r_lg"], g)
                act.activation(xnT[:], bank[1][:], ACT.Identity, bias=C["ffn_b"], scale=C["ffn_g"]).then_inc(Z["r_xT2"], 1)

            def exp_logits(l, g):
                act.wait_ge(Z["r_top"], g_at(l, g) + 1)
                act.activation(ex[:], ex[:], ACT.Exp).then_inc(Z["r_ex"], 1)

            def shared(l, g):
                for j in range(NSH[l]):
                    n = 2 * (NG * grown(NSH, l) + NSH[l] * g + j)
                    for c in range(2):
                        act.wait_ge(Z["s_h"], n + c + 1)
                        if n + c >= 2:
                            act.wait_ge(Z["s_act"], n + c - 1)
                        act.activation(gat[:, c, :], bank[2 + c][:], ACT.Silu).then_inc(Z["s_gate"], 1)

            def experts(l):
                base = tile_base(l)
                pbase = tile_base(l, PRE)

                def copy_x(s, k):
                    act.wait_ge(Z["t_x"], s + (base + 1))
                    if k >= 2:
                        act.wait_ge(Z["t_h"], s + (base - 1))
                    act.copy(xgT[:, k % 2, :], bank[k % 2][:, 0:P]).then_inc(Z["t_xT"], 1)

                def function(s, k):
                    p = k % 2
                    if l in (0, 2):
                        act.wait_ge(Z["t_h"], s + (base + 1))
                        if k >= 2:
                            act.wait_ge(Z["t_hid"], s + (base - 1))
                        act.activation(pre[:, p, 0:256], bank[2 + p][:, 0:256], ACT.Silu).then_inc(Z["t_pre"], 1)
                        return
                    if k >= 2:
                        act.wait_ge(Z["t_ht"], s + (base - 1))
                    if l == 1:
                        act.wait_ge(Z["t_h"], s + (base + 1))
                        act.activation(hid[:, p, :], bank[2 + p][:], ACT.Gelu_apprx_tanh).then_inc(Z["t_hid"], 1)
                    else:
                        act.wait_ge(Z["t_pre"], s + (pbase + 1))
                        act.activation(hid[:, p, :], pre[:, p, :], ACT.Gelu).then_inc(Z["t_hid"], 1)

                def copy_h(s, k):
                    p = k % 2
                    act.wait_ge(Z["t_ht"], s + (base + 1))
                    if k >= 2:
                        act.wait_ge(Z["t_y"], s + (base - 1))
                    act.copy(hidT[:, p].rearrange("p c n -> p (c n)"), bank[4 + p][:]).then_inc(Z["t_hT"], 1)

                n = TILES[l]
                copy_x(0, 0)

                def step(s, k, e, full=False):
                    if full or k + 1 < n:
                        copy_x(s + 1, k + 1)
                    if l == 3 and (full or 0 <= k - 1 < n):
                        copy_h(s - 1, k - 1)
                    if full or k < n:
                        function(s, k)

                steps(act, n, step)

            context(0)
            for l in range(LAYERS):
                three = GROUPS if l == 3 else ()
                route = routed_at(l)
                walk(l, tile, [
                    (-7, GROUPS, scale_tokens),
                    (-5, GROUPS if l == 1 else (), scale_tokens2),
                    (-4 if l == 1 else -6, GROUPS, copy_tokens),
                    (-3 if l == 1 else -5, GROUPS, copy_queries),
                    (0, three, exp3), (2, three, copy3),
                    (route, GROUPS, scale_routed),
                    (route + (1 if l else 2), GROUPS, copy_routed),
                    (route + 2, GROUPS if l == 0 else (), scale_routed2),
                    (route + 3, GROUPS if l == 0 else (), copy_routed2),
                    (route + (3 if l else 5), GROUPS, exp_logits)])
                if l + 1 < LAYERS:
                    context(l + 1)
                if NSH[l]:
                    for g in range(NG):
                        shared(l, g)
                experts(l)

        @block.vector
        def _(dve):
            dve.wait_ge(const, 2)

            def statistics(i, src, lo, done):
                dve.drain()
                for t in range(GT):
                    dve.bn_stats(stat[:, lo + t, :], src(t))
                dve.drain()
                for t in range(GT):
                    last = dve.bn_aggr(mv[i][:, lo + t, :], stat[:, lo + t, :])
                last.then_inc(done, 1)

            def stats(l, g):
                if g_at(l, g):
                    dve.wait_ge(Z["a_root"], g_at(l, g))
                statistics(0, lambda t: x[:, g * GT + t, :], 0, Z["a_stat"])

            def stats_routed(l, g):
                if g_at(l, g):
                    dve.wait_ge(Z["r_root"], g_at(l, g))
                statistics(0, lambda t: x[:, g * GT + t, :], GT, Z["r_stat"])

            def stats2(l, g):
                if g_at(l, g):
                    dve.wait_ge(Z["root2"], g_at(l, g))
                if l == 0:
                    dve.wait_ge(Z["r_sc"], g + 1)
                    statistics(1, lambda t: pay[:, 0, g * GT + t, 0:D], GT, Z["stat2"])
                else:
                    dve.wait_ge(Z["a_sc"], g_at(l, g) + 1)
                    statistics(1, lambda t: xn[:, t, :], 0, Z["stat2"])

            def context(l):
                if l == 0:
                    dve.wait_ge(ld_small, 16 * 4)
                    dve.bn_stats(stat[:, 0, :], ctx_sb[:])
                    dve.drain()
                    dve.bn_aggr(mv[0][:, 0, :], stat[:, 0, :]).then_inc(Z["c_stat"], 1)
                    dve.wait_ge(Z["c_root"], 1)
                    dve.tensor_scalar(ctxn[:], ctx_sb[:], mv[0][:, 0, 0:1], rstd[0][:, 0:1], ALU.subtract,
                                      ALU.mult).then_inc(Z["c_norm"], 1)
                    dve.tensor_copy(vblk[:, :, :, HC * HD:VW].rearrange("p b c j -> p (b c) j"),
                                    chunkmask[:].unsqueeze(1).to_broadcast([P, B * NC, HC]))
                    dve.wait_ge(ld_mask, 16)
                    dve.tensor_scalar(maskT[:], mask_i, 0.0, -1e20, ALU.is_equal, ALU.mult)
                    dve.wait_ge(tg_done, 1)
                    dve.tensor_scalar(brow[:], rows[:, R["ffn1"]:R["ffn1"] + P], tg[:, 5:6], None, ALU.mult)
                if l == 2:
                    dve.wait_ge(ld_heads, 16 * HEADS)
                    for i in range(3):
                        last = dve.tensor_tensor(blockw[:, i, :].rearrange("p (h e) -> p h e", h=HEADS),
                                                 small[:, i, :].unsqueeze(1).to_broadcast([P, HEADS, HD]),
                                                 headmask[:].unsqueeze(2).to_broadcast([P, HEADS, HD]), ALU.mult)
                    last.then_inc(blk_done, 1)
                if l < 3:
                    dve.wait_ge(Z["c_kT"], l + 1)
                    for b in range(B):
                        dve.tensor_tensor(kblk[:, b],
                                          kT[:, b * KEYS:(b + 1) * KEYS].unsqueeze(1).to_broadcast([P, HEADS, KEYS]),
                                          headmask[:].unsqueeze(2).to_broadcast([P, HEADS, KEYS]), ALU.mult)
                    dve.wait_ge(Z["c_v"], l + 1)
                    for b in range(B):
                        last = dve.tensor_tensor(
                            vblk[:, b, :, 0:HC * HD].rearrange("p c (j d) -> p c j d", j=HC),
                            bank[2][:, b * P:(b + 1) * P].rearrange("p (c j d) -> p c j d", c=NC, j=HC),
                            chunkmask[:].unsqueeze(1).unsqueeze(3).to_broadcast([P, NC, HC, HD]), ALU.mult)
                    last.then_inc(Z["c_blk"], 1)
                else:
                    dve.wait_ge(Z["c_kT"], l + 1)
                    dve.wait_ge(Z["c_v"], l + 1)
                    dve.tensor_copy(v3[:].rearrange("p b d -> p (b d)"), bank[2][0:KEYS, :]).then_inc(Z["c_blk"], 1)

            def tile(l, s):
                if l == 3:
                    return
                soft, norm = 0 <= s < NTILE, 0 <= s - 3 < NTILE
                if norm:
                    p, M = (s - 3) % 2, n_at(l, s - 3)
                    dve.wait_ge(Z["a_pv"], M + 1)
                    pv = bank[6][:, 0:NC * VW].rearrange("p (c w) -> p c w", c=NC)
                    dve.reciprocal(rinv[:, p, :].rearrange("p (c j) -> p c j", c=NC), pv[:, :, HC * HD:VW])
                if soft:
                    N = n_at(l, s)
                    dve.wait_ge(Z["a_s"], N + 1)
                    sc = bank[2 + s % 2][:].rearrange("p (h k) -> p h k", h=HEADS)
                    dve.tensor_reduce(mx[:, s % 2, :], sc, AX.X, ALU.max)
                if soft or norm:
                    dve.drain()
                if norm:
                    if M >= 2:
                        dve.wait_ge(Z["a_ot"], M - 1)
                    dve.tensor_tensor(o[:, p, :].rearrange("p (c j d) -> p c j d", c=NC, j=HC),
                                      pv[:, :, 0:HC * HD].rearrange("p c (j d) -> p c j d", j=HC),
                                      rinv[:, p, :].rearrange("p (c j) -> p c j", c=NC).unsqueeze(3)
                                      .to_broadcast([P, NC, HC, HD]), ALU.mult).then_inc(Z["a_o"], 1)
                if soft:
                    if N >= 2:
                        dve.wait_ge(Z["a_pt"], N - 1)
                    dve.tensor_tensor(prob[:, s % 2], sc, mx[:, s % 2, :].unsqueeze(2).to_broadcast([P, HEADS, KEYS]),
                                      ALU.subtract).then_inc(Z["a_sub"], 1)
                if 0 <= s - 6 < NTILE:
                    dve.wait_ge(Z["a_pr"], n_at(l, s - 6) + 1)
                    dve.scalar_tensor_tensor(x[:, s - 6, :], bank[7][:, 0:P], tg[:, l:l + 1], x[:, s - 6, :],
                                             ALU.mult, ALU.add).then_inc(Z["a_x"], 1)

            def soft3(l, g):
                dve.wait_ge(Z["a_s"], n_at(3, g) + 1)
                dve.wait_ge(Z["a_pt"], n_at(3, g))
                sc = bank[2][:, 0:GT * KEYS].rearrange("p (t k) -> p t k", t=GT)
                dve.tensor_reduce(mx[:, 0, 0:GT], sc, AX.X, ALU.max)
                dve.drain()
                dve.tensor_tensor(prob[:, 0, 0:GT, :], sc, mx[:, 0, 0:GT].unsqueeze(2).to_broadcast([P, GT, KEYS]),
                                  ALU.subtract).then_inc(Z["a_sub"], 1)

            def norm3(l, g):
                dve.wait_ge(Z["a_exp"], n_at(3, g) + 1)
                dve.tensor_reduce(rinv[:, 0, 0:GT], prob[:, 0, 0:GT, :], AX.X, ALU.add)
                dve.drain()
                dve.reciprocal(rinv[:, 1, 0:GT], rinv[:, 0, 0:GT])
                dve.drain()
                dve.tensor_tensor(prob[:, 0, 0:GT, :], prob[:, 0, 0:GT, :],
                                  rinv[:, 1, 0:GT].unsqueeze(2).to_broadcast([P, GT, KEYS]),
                                  ALU.mult).then_inc(Z["a_o"], 1)

            def into_x3(l, g):
                dve.wait_ge(Z["a_pr"], n_at(3, g) + 1)
                xs = x[:, g * GT:(g + 1) * GT].rearrange("p t d -> p (t d)")
                dve.scalar_tensor_tensor(xs, bank[6][:], tg[:, 3:4], xs, ALU.mult, ALU.add).then_inc(Z["a_x"], 1)

            def pick(l, g):
                K = TOPK[l]
                dve.wait_ge(Z["r_lg"], g_at(l, g) + 1)
                lg = bank[1][:, 0:GT * E].rearrange("p (t e) -> p t e", t=GT)
                if l == 2:
                    dve.tensor_tensor(logit[:], lg, ebias.unsqueeze(1).to_broadcast([P, GT, E]), ALU.add)
                else:
                    dve.tensor_copy(logit[:], lg)
                dve.drain()
                for t in range(GT):
                    dve.max(top[:, t, :], logit[:, t, :])
                dve.drain()
                dve.tensor_tensor(ex[:], top[:], top[:, :, 0:1].to_broadcast([P, GT, 8]), ALU.subtract).then_inc(Z["r_top"], 1)
                for t in range(GT):
                    dve.max_index(topi[:, t, :], top[:, t, :], logit[:, t, :])
                dve.drain()
                dve.tensor_copy(topf[:], topi[:, :, 0:2])
                dve.drain()
                for k in range(2):
                    dve.tensor_tensor(hot[:, :, k, :], iota_e[:].unsqueeze(1).to_broadcast([P, GT, E]),
                                      topf[:, :, k:k + 1].to_broadcast([P, GT, E]), ALU.is_equal)
                dve.drain()
                if l == 1:
                    last = dve.tensor_copy(picks[:, g], hot[:])
                elif K == 2:
                    for k in range(2):
                        last = dve.tensor_tensor(picks[:, g, :, k, :], hot[:, :, 0, :], hot[:, :, 1, :], ALU.add)
                else:
                    for k in range(2):
                        last = dve.tensor_copy(picks[:, g, :, k, :], hot[:, :, 0, :])
                last.then_inc(Z["r_pick"], 1)

            def place_rows(l, g):
                ts = slice(g * GT, (g + 1) * GT)
                dve.wait_ge(Z["r_ex"], g_at(l, g) + 1)
                if l == 2:
                    dve.tensor_tensor(s4[:, :, 0], ex[:, :, 0], ex[:, :, 1], ALU.add)
                else:
                    dve.tensor_reduce(s4[:, :, 0], ex[:], AX.X, ALU.add)
                dve.drain()
                dve.reciprocal(s4[:, :, 1], s4[:, :, 0])
                dve.drain()
                dve.tensor_tensor(wts[:, ts, :], ex[:, :, 0:2], s4[:, :, 1:2].to_broadcast([P, GT, 2]), ALU.mult)
                dve.drain()
                if l == 0:
                    dve.tensor_tensor(s4[:, :, 0], wts[:, ts, 0], wts[:, ts, 1], ALU.add)
                    dve.drain()
                    dve.tensor_scalar(s4[:, :, 0], s4[:, :, 0], EPS, None, ALU.add)
                    dve.drain()
                    dve.reciprocal(s4[:, :, 1], s4[:, :, 0])
                    dve.drain()
                    dve.tensor_tensor(wts[:, ts, :], wts[:, ts, :], s4[:, :, 1:2].to_broadcast([P, GT, 2]), ALU.mult)
                    dve.drain()
                dve.tensor_scalar(wts[:, ts, :], wts[:, ts, :], tg[:, 4 + l:5 + l], None, ALU.mult)
                dve.wait_ge(Z["r_rank"], g_at(l, g) + 1)
                if g < NG - 1:
                    now = picks[:, g].rearrange("p t k e -> p (k e) t")
                    if g == 0:
                        dve.tensor_reduce(rsum[:], now, AX.X, ALU.add)
                    else:
                        dve.tensor_reduce(radd[:], now, AX.X, ALU.add)
                        dve.drain()
                        dve.tensor_tensor(rsum[:], rsum[:], radd[:], ALU.add)
                    dve.drain()
                    dve.tensor_copy(sofar[:], rsum[:])
                rk = bank[1][:, 0:GT * SEG].rearrange("p (t k e) -> p t (k e)", t=GT, k=2)
                hk = hot[:].rearrange("p t k e -> p t (k e)")
                pk = place[:].rearrange("p t k e -> p t (k e)")
                first = (segment0 if l == 1 else region0)[:].rearrange("p k e -> p (k e)")
                if l == 1:
                    dve.tensor_tensor(pk, rk, hk, ALU.mult)
                    dve.drain()
                    dve.tensor_reduce(rank[:], place[:], AX.X, ALU.add)
                    dve.drain()
                    dve.tensor_scalar(rank[:], rank[:], float(CAP), None, ALU.is_lt)
                    dve.drain()
                    dve.tensor_tensor(wts[:, ts, :], wts[:, ts, :], rank[:], ALU.mult)
                dve.tensor_tensor(pk, rk, first.unsqueeze(1).to_broadcast([P, GT, SEG]), ALU.add)
                dve.drain()
                dve.tensor_tensor(pk, pk, hk, ALU.mult)
                dve.drain()
                dve.tensor_reduce(posf[:], place[:], AX.X, ALU.add)
                dve.drain()
                if l == 1:
                    dve.scalar_tensor_tensor(posf[:], posf[:], -float(NOWHERE), rank[:], ALU.add, ALU.mult)
                    dve.drain()
                    dve.tensor_scalar(pos[:, ts, :], posf[:], float(NOWHERE), None, ALU.add).then_inc(Z["r_pos"], 1)
                else:
                    dve.tensor_copy(pos[:, ts, :], posf[:]).then_inc(Z["r_pos"], 1)

            def tables(l):
                if l == 1:
                    dve.tensor_copy(count[:], bank[1][:, GT * SEG:(GT + 1) * SEG])
                    dve.drain()
                    n = TILES[1]
                    dve.tensor_tensor(valid[:, 0:n].rearrange("p (e k j) -> p e k j", e=E, k=2),
                                      count[:].rearrange("p (k e) -> p e k", k=2).unsqueeze(3).to_broadcast([P, E, 2, CAP // P]),
                                      seg_at[:].rearrange("p (e k j) -> p e k j", e=E, k=2), ALU.is_gt)
                    dve.drain()
                    dve.tensor_scalar(away[:, 0:n], valid[:, 0:n], -float(NOWHERE), float(NOWHERE), ALU.mult,
                                      ALU.add).then_inc(Z["m_tab"], 1)
                    dve.drain()
                    return
                n = TILES[l]
                cnt = count[:, 0:E]
                dve.tensor_copy(cnt, bank[1][:, GT * SEG:GT * SEG + E])
                dve.drain()
                dve.tensor_tensor(pad_f[:], cnt, region0[:, 0, :], ALU.add)
                dve.tensor_tensor(cmp1[:], cnt.unsqueeze(2).to_broadcast([P, E, NTILE]),
                                  slot128[:].unsqueeze(1).to_broadcast([P, E, NTILE]), ALU.is_gt)
                dve.drain()
                dve.tensor_copy(pad_r[:], pad_f[0:1, :])
                dve.tensor_reduce(ntil[:], cmp1[:], AX.X, ALU.add)
                dve.drain()
                dve.tensor_tensor(cmp2[:], upper[:], ntil[:].unsqueeze(1).to_broadcast([P, E, E]), ALU.mult)
                dve.drain()
                dve.tensor_reduce(cum[:], cmp2[:], AX.X, ALU.add)
                dve.drain()
                dve.tensor_tensor(cumx[:], cum[:], ntil[:], ALU.subtract)
                it = iota_t[:, 0:n].unsqueeze(2).to_broadcast([P, n, E])
                dve.tensor_tensor(ge_in[:, 0:n], it, cum[:].unsqueeze(1).to_broadcast([P, n, E]), ALU.is_ge)
                dve.drain()
                dve.tensor_tensor(ge_ex[:, 0:n], it, cumx[:].unsqueeze(1).to_broadcast([P, n, E]), ALU.is_ge)
                dve.tensor_reduce(te[:, 0:n], ge_in[:, 0:n], AX.X, ALU.add)
                dve.tensor_tensor(tw[:, 0:n], ge_in[:, 0:n], ntil[:].unsqueeze(1).to_broadcast([P, n, E]), ALU.mult)
                dve.drain()
                dve.tensor_reduce(tb[:, 0:n], tw[:, 0:n], AX.X, ALU.add)
                dve.tensor_tensor(ge_ex[:, 0:n], ge_ex[:, 0:n], ge_in[:, 0:n], ALU.subtract)
                dve.tensor_scalar(te[:, 0:n], te[:, 0:n], float(E - 1), None, ALU.min)
                dve.drain()
                dve.tensor_copy(tab_e[:, 0:n], te[0:1, 0:n])
                dve.tensor_tensor(tw[:, 0:n], ge_ex[:, 0:n], cnt.unsqueeze(1).to_broadcast([P, n, E]), ALU.mult)
                dve.tensor_tensor(tb[:, 0:n], iota_t[:, 0:n], tb[:, 0:n], ALU.subtract)
                dve.drain()
                dve.tensor_scalar(tb[:, 0:n], tb[:, 0:n], float(NTILE - 1), float(P), ALU.min, ALU.mult)
                dve.tensor_reduce(tn[:, 0:n], tw[:, 0:n], AX.X, ALU.add)
                dve.drain()
                dve.scalar_tensor_tensor(tb[:, 0:n], tn[:, 0:n], 0.0, tb[:, 0:n], ALU.is_gt, ALU.mult)
                dve.drain()
                dve.scalar_tensor_tensor(tabf[:, 0:n], te[:, 0:n], float(REGION), tb[:, 0:n], ALU.mult, ALU.add)
                dve.tensor_scalar(tb[:, 0:n], tb[:, 0:n], part[:], None, ALU.add)
                dve.drain()
                dve.tensor_tensor(valid[:, 0:n], tn[:, 0:n], tb[:, 0:n], ALU.is_gt)
                dve.tensor_copy(tab_r[:, 0:n], tabf[0:1, 0:n]).then_inc(Z["m_tab"], 1)
                dve.drain()
                dve.tensor_scalar(away[:, 0:n], valid[:, 0:n], -float(NOWHERE), float(NOWHERE), ALU.mult, ALU.add)
                dve.drain()

            def shared(l, g):
                for j in range(NSH[l]):
                    n = 2 * (NG * grown(NSH, l) + NSH[l] * g + j)
                    for c in range(2):
                        dve.wait_ge(Z["s_gate"], n + c + 1)
                        m = (0 if l == 0 else NG) + g
                        if m:
                            dve.wait_ge(Z["s_y"], m)
                        dve.tensor_tensor(hsh[:, 2 * j + c, :], gat[:, c, :], bank[4 + c][:], ALU.mult).then_inc(Z["s_act"], 1)
                m = (0 if l == 0 else NG) + g
                dve.wait_ge(Z["s_y"], m + 1)
                xs = x[:, g * GT:(g + 1) * GT].rearrange("p t d -> p (t d)")
                dve.scalar_tensor_tensor(xs, bank[6 + g % 2][:], tg[:, 4 + l:5 + l], xs, ALU.mult,
                                         ALU.add).then_inc(Z["s_x"], 1)

            def experts(l):
                base = tile_base(l)
                pbase = tile_base(l, PRE)
                nf = FC[l]
                n = TILES[l]

                def ids(s, k):
                    q = k % RING
                    dve.wait_ge(filled[q], (s + (RING - q)) * (16 // RING) + ring_base(l, q))
                    if k >= RING:
                        dve.wait_ge(put[q], (s - q) * (16 // RING) + ring_base(l, q))
                    dve.scalar_tensor_tensor(row[:, q:q + 1], xg[:, q, D:D + 1], valid[:, bass.ds(s, 1)],
                                             away[:, bass.ds(s, 1)], ALU.mult, ALU.add).then_inc(Z["t_id"], 1)

                def gate_up(s, k):
                    p = k % 2
                    dve.wait_ge(Z["t_pre"], s + (pbase + 1))
                    if k >= 2:
                        dve.wait_ge(Z["t_ht"], s + (base - 1))
                    dve.tensor_tensor(hid[:, p, 0:256], pre[:, p, 0:256], bank[2 + p][:, 256:512], ALU.mult).then_inc(Z["t_hid"], 1)

                def bias(s, k, e):
                    p = k % 2
                    dve.wait_ge(Z["t_h"], s + (base + 1))
                    if k >= 2:
                        dve.wait_ge(Z["t_hid"], s + (base - 1))
                    dve.tensor_tensor(pre[:, p, :], bank[2 + p][:], b1[:, bass.ds(e * WIDE, WIDE)], ALU.add).then_inc(Z["t_pre"], 1)

                def copy_h(s, k):
                    p = k % 2
                    dve.wait_ge(Z["t_ht"], s + (base + 1))
                    if k >= 2:
                        dve.wait_ge(Z["t_y"], s + (base - 1))
                    dve.tensor_copy(hidT[:, p, 0:nf].rearrange("p c n -> p (c n)"), bank[4 + p][:, 0:nf * P]).then_inc(Z["t_hT"], 1)

                def copy_y(s, k, e):
                    p, q = k % 2, k % RING
                    dve.wait_ge(Z["t_y"], s + (base + 1))
                    if l == 3:
                        dve.tensor_tensor(ysb[:, q, :], bank[6 + p][:, 0:D], b2[:, bass.ds(e * D, D)], ALU.add).then_inc(Z["t_ysb"], 1)
                    else:
                        dve.tensor_copy(ysb[:, q, :], bank[6 + p][:, 0:D]).then_inc(Z["t_ysb"], 1)

                def step(s, k, e, full=False):
                    if l == 3 and (full or k < n):
                        bias(s, k, e[k])
                    if l != 3 and (full or 0 <= k - 1 < n):
                        copy_h(s - 1, k - 1)
                    if l in (0, 2) and (full or k < n):
                        gate_up(s, k)
                    if full or k < n:
                        ids(s, k)
                    if full or 0 <= k - 2 < n:
                        copy_y(s - 2, k - 2, e.get(k - 2))

                steps(dve, n, step, (mybir.EngineType.DVE, l) if l == 3 else None)

            def combine(l, g):
                dve.wait_ge(back[g], 16 * sum(TOPK[:l + 1]))
                dve.drain()
                for k in range(TOPK[l]):
                    for t in range(g * GT, (g + 1) * GT):
                        last = dve.scalar_tensor_tensor(x[:, t, :], pay[:, k, t, 0:D], wts[:, t, k:k + 1], x[:, t, :],
                                                        ALU.mult, ALU.add)
                    dve.drain()
                if l == 1:
                    xs = x[:, g * GT:(g + 1) * GT]
                    dve.tensor_tensor(xs, xs, brow[:].unsqueeze(1).to_broadcast([P, GT, D]), ALU.add)
                    dve.drain()
                if l == LAYERS - 1:
                    last.then_inc(Z["x_done"], 1)

            def combine_last(l, g):
                combine(l - 1, g)

            context(0)
            dve.wait_ge(ld_x, 16)
            for l in range(LAYERS):
                three = GROUPS if l == 3 else ()
                route = routed_at(l)
                walk(l, tile, [
                    (0, three, soft3), (1, three, norm3), (4, three, into_x3),
                    (-8, GROUPS if l else (), combine_last),
                    (-8, GROUPS, stats),
                    (route - 1, GROUPS, stats_routed),
                    (-6 if l else route + 1, GROUPS if l < 2 else (), stats2),
                    (route + (2 if l else 4), GROUPS, pick),
                    (route + (3 if l else 5), GROUPS, place_rows)])
                if l == 3:
                    dve.wait_ge(ld_w[3], 16 * 4)
                tables(l)
                if l + 1 < LAYERS:
                    context(l + 1)
                if NSH[l]:
                    for g in range(NG):
                        shared(l, g)
                experts(l)
            for g in range(NG):
                combine(LAYERS - 1, g)


def kernel(**inputs):
    import numpy as np
    import concourse.bacc as bacc
    from concourse.bass_utils import run_bass_kernel_spmd

    a = {k: np.asarray(v) for k, v in inputs.items()}
    c = np.ascontiguousarray

    def columns(*names):
        return [a[n].reshape(P, 1) for n in names]

    def wide(*parts):
        return c(np.concatenate(parts, axis=2).transpose(1, 0, 2))

    def tall(w):
        e, f, d = w.shape
        return c(w.reshape(e, f // P, P, d).transpose(2, 0, 1, 3).reshape(P, e * (f // P), d))

    def stack(*ws):
        return np.concatenate([w if w.ndim == 3 else w[None] for w in ws], axis=0)

    cols = c(np.concatenate(columns("L0_xattn_bq", "L0_xattn_bk", "L1_xattn_ln1_g", "L1_xattn_ln1_b", "L1_xattn_ln2_g",
                                    "L1_xattn_ln2_b", "L0_ffn_ln_scale", "L0_ffn_ln_bias", "L3_xattn_bq", "L3_xattn_bv")
                            + [a["L0_ffn_gate_w"].T, a["L1_ffn_router_w"], a["L2_ffn_router_w"].T, a["L3_ffn_Wr"]], axis=1))
    rows = c(np.concatenate([a["L0_xattn_bv"], a["L0_xattn_bo"], a["L2_xattn_bout"], a["L3_xattn_bv"],
                             a["L1_ffn_bias"].reshape(-1), a["L2_ffn_expert_bias"], a["g_xattn"], a["g_ffn"]])[None])
    attnw = c(np.stack([a["L0_xattn_Wq"].T, a["L0_xattn_Wk"].T, a["L0_xattn_Wv"].T, a["L0_xattn_Wo"].T,
                        a["L1_xattn_Wq"], a["L1_xattn_Wk"], a["L1_xattn_Wv"], a["L1_xattn_Wfc"],
                        a["L2_xattn_Wout"].T, a["L3_xattn_Wq"], a["L3_xattn_Wv"]], axis=1))
    small = c(np.stack([a["L2_xattn_Wq"].T, a["L2_xattn_Wk"].T, a["L2_xattn_Wv"].T], axis=1))
    T = lambda w: w.transpose(0, 2, 1)
    w1 = [wide(stack(a["L0_ffn_Wg"], a["L0_ffn_sWg"]), stack(a["L0_ffn_Wu"], a["L0_ffn_sWu"])),
          wide(a["L1_ffn_w1"]),
          wide(stack(T(a["L2_ffn_w1"]), T(a["L2_ffn_sw1"])), stack(T(a["L2_ffn_w3"]), T(a["L2_ffn_sw3"]))),
          wide(a["L3_ffn_W1"])]
    w2 = [tall(stack(a["L0_ffn_Wd"], a["L0_ffn_sWd"])), tall(a["L1_ffn_w2"]),
          tall(stack(T(a["L2_ffn_w2"]), T(a["L2_ffn_sw2"]))), tall(a["L3_ffn_W2"])]
    arrays = {"x": c(a["x"].reshape(TOK, D)), "ctx": c(a["ctx_1024"].reshape(B * KEYS, D)),
              "mask": c(a["mask_Bx1xSxS2_ik1"].reshape(TOK, KEYS).T), "cols": cols, "rows": rows, "attnw": attnw,
              "small": small, **{f"w1_{l}": w1[l] for l in range(LAYERS)}, **{f"w2_{l}": w2[l] for l in range(LAYERS)},
              "b1": c(a["L3_ffn_b1"].reshape(1, -1)), "b2": c(a["L3_ffn_b2"].reshape(1, -1))}
    nc = bacc.Bacc("TRN2", target_bir_lowering=False, num_devices=1)
    h = {n: nc.dram_tensor(f"in_{n}", v.shape, mybir.dt.from_np(v.dtype), kind="ExternalInput").ap()
         for n, v in arrays.items()}
    out = nc.dram_tensor("out_0", (TOK, D), F32, kind="ExternalOutput").ap()
    flamingo(nc, h["x"], h["ctx"], h["mask"], h["cols"], h["rows"], h["attnw"], h["small"],
             [h[f"w1_{l}"] for l in range(LAYERS)], [h[f"w2_{l}"] for l in range(LAYERS)], h["b1"], h["b2"], out)
    got = run_bass_kernel_spmd(nc, [{f"in_{n}": v for n, v in arrays.items()}], core_ids=[0])
    return got.results[0]["out_0"].reshape(B, S, D)
```

```python
import concourse.bass as bass
from concourse import mybir
from contextlib import ExitStack

F32 = mybir.dt.float32
BF16 = mybir.dt.bfloat16
I32 = mybir.dt.int32
U32 = mybir.dt.uint32
ALU = mybir.AluOpType
ACT = mybir.ActivationFunctionType
AX = mybir.AxisListType

P = 128
B, S, D, KEYS = 4, 512, 128, 32
TOK = B * S
NTILE = TOK // P
NG = B
GT = S // P
HEADS, HD = 16, 8
HC = P // KEYS
NC = HEADS // HC
VW = HC * HD + HC
E = 8
EPS = 1e-5
LAYERS = 4
TOPK = [2, 2, 2, 1]
WIDE = 512
FC = [2, 4, 2, 4]
CAP = TOK // E
SEG = 2 * E
REGION = TOK + P
ROW = P + 1
NOWHERE = 2 * TOK
TILES = [(k * TOK + E * (P - 1)) // P for k in TOPK]
TILES[1] = SEG * CAP // P
MAXT = max(TILES)
RING = 4
TURN = 2 * RING
HEAD = RING + 2


def flamingo(nc, x_d, ctx_d, mask_d, cols_d, rows_d, attnw_d, small_d, w1_d, w2_d, b1_d, b2_d, out_d):
    ctx = ExitStack()
    with ctx:
        def sb(name, shape, dt=F32):
            return ctx.enter_context(nc.sbuf_tensor(name, shape, dt))

        def sem(name):
            return ctx.enter_context(nc.semaphore(name))

        x = sb("x", [P, NTILE, D])
        ctx_sb = sb("ctx_sb", [P, D])
        ctxn = sb("ctxn", [P, D])
        ctxT = sb("ctxT", [P, P])
        ctxTn = sb("ctxTn", [P, P])
        ctxR = sb("ctxR", [P, 2, B, HC, KEYS])
        cols = sb("cols", [P, 10 + 4 * E])
        rows = sb("rows", [P, 5 * P + 8 + 8])
        attnw = sb("attnw", [P, 11, P])
        small = sb("small", [P, 3, HD])
        blockw = sb("blockw", [P, 3, P])
        tg = sb("tg", [P, 8])
        brow = sb("brow", [P, P])
        w1 = [sb("w1_0", [P, E + 1, WIDE]), sb("w1_1", [P, E, WIDE]), sb("w1_2", [P, E + 2, WIDE])]
        w2 = [sb("w2_0", [P, E * 4, D]), sb("w2_1", [P, E * 4, D]), sb("w2_2", [P, (E + 2) * 2, D])]
        w1.append(w1[0])
        w2.append(w2[0])
        b1 = sb("b1", [P, E * WIDE // P])
        b2 = w2[1][:, 0:E].rearrange("p c n -> p (c n)")
        kT = sb("kT", [P, P])
        kblk = sb("kblk", [P, B, HEADS, KEYS])
        vblk = sb("vblk", [P, B, NC, VW])
        v3 = sb("v3", [KEYS, B, D])
        xn = sb("xn", [P, GT, D])
        xT = sb("xT", [P, S])
        qT = sb("qT", [P, 2, S])
        prob = sb("prob", [P, 2, HEADS, KEYS])
        probT = sb("probT", [P, 2, NC, P])
        o = sb("o", [P, 2, P])
        oT = sb("oT", [P, 2, P])
        xn2 = sb("xn2", [P, GT, D])
        xnT = sb("xnT", [P, S])
        stat = sb("stat", [P, 2 * GT, 6])
        mv = [sb(f"mv{i}", [P, 2 * GT, 2]) for i in range(2)]
        rstd = [sb(f"rstd{i}", [P, 2 * GT]) for i in range(2)]
        shift = [sb(f"shift{i}", [P, 2 * GT]) for i in range(2)]
        mx = sb("mx", [P, 2, HEADS])
        rinv = sb("rinv", [P, 2, HEADS])
        maskT = sb("maskT", [KEYS, TOK], BF16)
        every = sb("every", [KEYS, HEADS, KEYS], BF16)
        xfT = sb("xfT", [P, TOK])
        mask_i = xfT[0:KEYS, :].bitcast(I32)
        pay = sb("pay", [P, 2, NTILE, ROW])
        top = sb("top", [P, NTILE, 8])
        topi = sb("topi", [P, GT, 8], U32)
        ex = sb("ex", [P, NTILE, 8])
        sums = sb("sums", [P, NTILE])
        over = sb("over", [P, NTILE])
        wts = sb("wts", [P, NTILE, 2])
        picks = sb("picks", [P, NG, GT, 2, E], BF16)
        place = sb("place", [P, GT, 2, E])
        kept = sb("kept", [P, NTILE, 2])
        pos = sb("pos", [P, NTILE, 2], U32)
        gsum = sb("gsum", [P, NG, 2, E], BF16)
        count = sb("count", [P, SEG])
        ntil = sb("ntil", [P, E])
        cmp1 = sb("cmp1", [P, E, NTILE])
        cmp2 = sb("cmp2", [P, E, E])
        cum = sb("cum", [P, E])
        cumx = sb("cumx", [P, E])
        ge_in, ge_ex, tw = [sb(n, [P, E]) for n in ("ge_in", "ge_ex", "tw")]
        te, tb, tn, fill, start = [sb(n, [P, 1]) for n in ("te", "tb", "tn", "fill", "start")]
        diagonals = sb("diagonals", [P, 3, MAXT], BF16)
        valid = sb("valid", [P, MAXT])
        away = sb("away", [P, MAXT])
        tab_e = sb("tab_e", [1, MAXT], I32)
        tab_r = sb("tab_r", [1, MAXT], I32)
        pad_f = sb("pad_f", [P, E])
        pad_r = sb("pad_r", [1, E], I32)
        gat = sb("gat", [P, 2, S])
        hsh = sb("hsh", [P, 4, S])
        xg = sb("xg", [P, RING, ROW])
        xgT = xnT[:, 0:2 * P].rearrange("p (b n) -> p b n", b=2)
        hid = hsh[:, 0:2]
        pre = hsh[:, 2:4]
        wide = gat[:]
        ysb = xn2
        row = sb("row", [P, TURN], U32)
        ident = sb("ident", [P, P])
        headmask = sb("headmask", [P, HEADS])
        chunkmask = sb("chunkmask", [P, HC])
        before = sb("before", [P, P], BF16)
        onesb = sb("onesb", [P, P], BF16)
        ones = sb("ones", [1, P])
        minus_half = sb("minus_half", [P, 2 * GT])
        iota_e = sb("iota_e", [P, E])
        region0 = sb("region0", [P, E])
        limit = sb("limit", [P, 2, E])
        row_base = [sb(f"row_base{i}", [P, 2, E], BF16) for i in range(2)]
        slot128 = sb("slot128", [P, NTILE])
        part = sb("part", [P, 1])
        upper = sb("upper", [P, E, E])
        seg_at = sb("seg_at", [P, TILES[1]])
        zeros = sb("zeros", [P, ROW])
        unused = sb("unused", [P, 1])

        bank = [ctx.enter_context(nc.psum_tensor(f"bank{i}", [P, 512], F32)) for i in range(8)]

        slots = nc.dram_tensor("slots", [E * REGION, ROW], F32, kind="Internal").ap()
        slots1 = nc.dram_tensor("slots1", [SEG * CAP, ROW], F32, kind="Internal").ap()
        result = nc.dram_tensor("result", [2 * TOK, D], F32, kind="Internal").ap()

        C = {n: cols[:, i:i + 1] for i, n in enumerate(
            ["bq0", "bk0", "ln1_g", "ln1_b", "ln2_g", "ln2_b", "ffn_g", "ffn_b", "bq3", "bv3"])}
        router = [cols[:, 10 + E * l:10 + E * (l + 1)] for l in range(LAYERS)]
        R = {n: i * P for i, n in enumerate(["bv0", "bo0", "bo2", "bv3", "ffn1"])}
        ebias = rows[:, 5 * P:5 * P + E]
        gates = rows[:, 5 * P + E:5 * P + E + 8]
        WQ = [attnw[:, 0, :], attnw[:, 4, :], blockw[:, 0, :], attnw[:, 9, :]]
        WK = [attnw[:, 1, :], attnw[:, 5, :], blockw[:, 1, :], attnw[:, 10, :]]
        WV = [attnw[:, 2, :], attnw[:, 6, :], blockw[:, 2, :], attnw[:, 10, :]]
        WO = [attnw[:, 3, :], attnw[:, 7, :], attnw[:, 8, :], None]
        SCALE = [HD ** -0.5, HD ** -0.5, D ** -0.5, 1.0]

        ld_ctx = sem("ld_ctx")
        ld_x = sem("ld_x")
        ld_more_x = sem("ld_more_x")
        ld_small = sem("ld_small")
        ld_attn = sem("ld_attn")
        ld_mask = sem("ld_mask")
        ld_heads = sem("ld_heads")
        ld_w = [sem(f"ld_w{l}") for l in range(LAYERS)]
        zero_done = sem("zero_done")
        const = sem("const")
        blk_done = sem("blk_done")
        tg_done = sem("tg_done")
        names = [
            "c_stat", "c_root", "c_norm", "c_t", "c_T", "c_k", "c_kT", "c_v", "c_blk",
            "a_stat", "a_root", "r_stat", "r_root", "stat2", "root2", "p_self",
            "a_sc", "a_sc2", "a_xt", "a_xT", "a_q", "a_qT",
            "a_s", "a_sub", "a_exp", "a_pt", "a_pT", "a_pv", "a_o", "a_ot", "a_oT", "a_pr", "a_x",
            "x_done",
            "r_sc", "r_rows", "r_sc2", "r_xt", "r_xT", "r_xt2", "r_xT2", "r_lg", "r_pick", "r_rank", "r_pos", "r_top",
            "r_ex",
            "m_pad", "m_diag", "m_row", "m_tab",
            "s_h", "s_gate", "s_act", "s_y", "s_x",
            "t_x", "t_xT", "t_w", "t_h", "t_pre", "t_hid", "t_y", "t_ysb", "t_id", "t_go"]
        Z = {n: sem(n) for n in names}
        scat = [sem(f"scat{l}") for l in range(LAYERS)]
        padded = sem("padded")
        filled = [sem(f"filled{q}") for q in range(RING)]
        put = [sem(f"put{q}") for q in range(RING)]
        back = [sem(f"back{g}") for g in range(NG)]
        out_done = sem("out_done")

        def grown(per_layer, l):
            return sum(per_layer[:l])

        PRE = [TILES[0], 0, TILES[2], 0]

        def tile_base(l, counts=TILES):
            return grown(counts, l)

        def ring_base(l, q, n=RING):
            return 16 * sum(len(range(q, TILES[i], n)) for i in range(l))

        def g_at(l, g):
            return l * NG + g

        def n_at(l, n):
            return l * NTILE + n

        PERIOD = [4, 4, 4, 3]
        AT = [dict(combine=-8, stats=-8, scale=-7, tokens=-6, context=-5, queries=-3.5, stats_r=7, scale_r=7,
                   stats2=8, scale2=9, tokens_r=10, tokens_r2=10, logits=11, pick=11, ranks=12, scatter=12,
                   place=13, next_context=18),
              dict(combine=-9, stats=-7.5, scale=-7, stats2=-6, scale2=-5.5, tokens=-4, queries=-3, stats_r=7,
                   scale_r=8, tokens_r=10, logits=10, pick=11, ranks=11, scatter=11, place=12, next_context=18),
              dict(combine=-9, stats=-7, scale=-6, tokens=-5, queries=-4, stats_r=7, scale_r=8, tokens_r=9,
                   logits=10, pick=11, ranks=12, scatter=12, place=13, next_context=20),
              dict(combine=-11.5, stats=-11.5, scale=-6, tokens=-5, queries=-5, stats_r=4, scale_r=5, tokens_r=7,
                   logits=8, pick=9, ranks=9, place=10, scatter=11)]
        BANK_R = [(1, 1, 1), (1, 1, 1), (1, 1, 1), (1, 3, 5)]
        GROUPS = range(NG)
        NSH = [1, 0, 2, 0]
        FIRST_PART = [20, 0, 24, 0]

        def shared_parts(l):
            return [(g, i) for g in GROUPS for i in range(2 * NSH[l] + 1)] if NSH[l] else []

        def last_step(l):
            return int(max(AT[l]["place"], AT[l]["scatter"] + 3) + 0.5) + PERIOD[l] * (NG - 1)

        def walk(l, tile, pieces, part=None):
            for s in range(int(min(AT[l].values())) - 1, last_step(l) + 1):
                for now in (s - 0.5, s):
                    if now == s:
                        tile(l, s)
                    for distance, groups, piece in pieces:
                        g, rest = divmod(now - distance, PERIOD[l])
                        if rest == 0 and g in groups:
                            piece(l, int(g))
                if part is not None and FIRST_PART[l] <= s < FIRST_PART[l] + len(shared_parts(l)):
                    part(l, *shared_parts(l)[s - FIRST_PART[l]])

        def rest_of_parts(l, part, between=None):
            rest = shared_parts(l)[max(0, last_step(l) + 1 - FIRST_PART[l]):]
            for g, i in rest[:1]:
                part(l, g, i)
            if between is not None:
                between(l)
            for g, i in rest[1:]:
                part(l, g, i)

        def numbers(engine, table, start, n, top):
            return nc.values_load_multi_w_load_instructions(
                table[0:1, bass.ds(start, n) if not isinstance(start, int) else slice(start, start + n)],
                engines=[engine], min_val=0, max_val=top,
                skip_runtime_bounds_check_because="the table's entries are clamped when it is made")[1]

        def steps(eng, tiles, step, engine=None):
            def experts_of(first, k, n):
                if engine is None:
                    return {}
                if engine[1] == 1:
                    return {k + i: (first + i) // RING if isinstance(first, int) else first + (k + i) // RING
                            for i in range(n)}
                return dict(zip(range(k, k + n), numbers(engine[0], tab_e, first, n, E - 1)))

            turns = (tiles - HEAD) // TURN
            e = experts_of(0, 0, HEAD)
            for s in range(HEAD):
                step(s, s, e)
            with eng.Fori(0, turns) as turn:
                first = turn * (TURN // RING) if engine is not None and engine[1] == 1 else turn * TURN + (HEAD - 2)
                e = experts_of(first, HEAD - 2, TURN + 2)
                for k in range(HEAD, HEAD + TURN):
                    step(turn * TURN + k, k, e, True)
            s = HEAD + turns * TURN
            e = experts_of(s - 2, s - 2, tiles - s + 2)
            for s in range(s, tiles + 2):
                step(s, s, e)

        block = ctx.enter_context(nc.Block())

        @block.sync
        def _(sp):
            x_rows = x_d.rearrange("(t p) d -> p t d", p=P)
            sp.dma_start(ctx_sb[:], ctx_d).then_inc(ld_ctx, 16)
            sp.dma_start(x[:, 0:GT], x_rows[:, 0:GT]).then_inc(ld_x, 16)
            sp.dma_start(cols[:], cols_d).then_inc(ld_small, 16)
            sp.dma_start(attnw[:, 0:4], attnw_d[:, 0:4]).then_inc(ld_small, 16)
            sp.dma_start(rows[:], rows_d.to_broadcast([P, 5 * P + 16])).then_inc(ld_small, 16)
            sp.dma_start(x[:, GT:], x_rows[:, GT:]).then_inc(ld_more_x, 16)
            sp.dma_start(mask_i, mask_d).then_inc(ld_mask, 16)
            sp.dma_start(attnw[:, 4:], attnw_d[:, 4:]).then_inc(ld_attn, 16)
            sp.dma_start(w1[0][:], w1_d[0]).then_inc(ld_w[0], 16)
            sp.dma_start(w2[0][:, 0:(E + 1) * 2], w2_d[0]).then_inc(ld_w[0], 16)
            sp.wait_ge(const, 1)
            sp.dma_start(slots1.rearrange("(t p) d -> p t d", p=P),
                         zeros[:].unsqueeze(1).to_broadcast([P, SEG * CAP // P, ROW])).then_inc(zero_done, 16)
            for h in range(HEADS):
                sp.dma_start(small[h * HD:(h + 1) * HD], small_d).then_inc(ld_heads, 16)
            for l in (1, 2):
                sp.dma_start(w1[l][:], w1_d[l]).then_inc(ld_w[l], 16)
                sp.dma_start(w2[l][:], w2_d[l]).then_inc(ld_w[l], 16)

            for l in range(LAYERS):
                src = slots1 if l == 1 else slots
                if l != 1:
                    npad = sum(1 for i in range(l + 1) if i != 1)
                    sp.wait_ge(Z["m_pad"], npad)
                    for r in numbers(mybir.EngineType.SP, pad_r, 0, E, E * REGION - P):
                        sp.dma_start(slots[bass.ds(r, P), :], zeros[:]).then_inc(padded, 16)
                    sp.wait_ge(padded, 16 * E * npad)
                else:
                    sp.wait_ge(zero_done, 16)
                sp.wait_ge(scat[l], 16 * TOPK[l] * NTILE)
                sp.wait_ge(Z["m_tab"], l + 1)
                base = tile_base(l)

                def load(s, k, q, r):
                    if k >= RING:
                        sp.wait_ge(Z["t_x"], s + (base - RING + 1))
                        sp.wait_ge(Z["t_id"], s + (base - RING + 1))
                    sp.dma_start(xg[:, q, :], src[bass.ds(r, P), :]).then_inc(filled[q], 16)

                def starts(first, n):
                    if l == 1:
                        return [(first + i) * P for i in range(n)]
                    return numbers(mybir.EngineType.SP, tab_r, first, n, E * REGION - P)

                n = TILES[l]
                turns = n // RING - 1
                for s, r in enumerate(starts(0, RING)):
                    load(s, s, s, r)
                with sp.Fori(0, turns) as turn:
                    for k, r in enumerate(starts(turn * RING + RING, RING)):
                        load(turn * RING + (RING + k), RING, k, r)
                s = RING * (turns + 1)
                if s < n:
                    for k, r in enumerate(starts(s, n - s)):
                        load(s + k, s, k, r)
                for q in range(RING):
                    sp.wait_ge(put[q], ring_base(l + 1, q))
                for g in range(NG):
                    for k in range(TOPK[l]):
                        r0 = k * TOK + g * S
                        sp.dma_start(pay[:, k, g * GT:(g + 1) * GT, 0:D],
                                     result[r0:r0 + S, :].rearrange("(t p) d -> p t d", p=P)).then_inc(back[g], 16)
                if l == 0:
                    sp.dma_start(w1[3][:, 0:E], w1_d[3]).then_inc(ld_w[3], 16)
                    sp.dma_start(w2[3][:, 0:4 * E], w2_d[3]).then_inc(ld_w[3], 16)
                if l == 1:
                    sp.dma_start(b1[:], b1_d).then_inc(ld_w[3], 16)
                    sp.dma_start(b2, b2_d.to_broadcast([P, E * D])).then_inc(ld_w[3], 16)
            for g in range(NG):
                sp.wait_ge(Z["x_done"], g + 1)
                sp.dma_start(out_d[g * S:(g + 1) * S, :].rearrange("(t p) d -> p t d", p=P),
                             x[:, g * GT:(g + 1) * GT]).then_inc(out_done, 16)
            sp.wait_ge(out_done, 16 * NG)

        @block.gpsimd
        def _(pool):
            pool.memset(zeros[:], 0.0).then_inc(const, 1)
            pool.memset(ident[:], 0.0)
            pool.memset(headmask[:], 1.0)
            pool.memset(chunkmask[:], 1.0)
            pool.memset(before[:], 1.0)
            pool.memset(onesb[:], 1.0)
            pool.memset(ones[:], 1.0)
            pool.memset(minus_half[:], -0.5)
            pool.memset(upper[:], 1.0)
            pool.memset(every[:], 0.0)
            pool.iota(iota_e[:], [[1, E]], base=0, channel_multiplier=0, allow_small_or_imprecise_dtypes=True)
            pool.iota(region0[:], [[REGION, E]], base=0, channel_multiplier=0, allow_small_or_imprecise_dtypes=True)
            pool.iota(limit[:], [[CAP, 2], [2 * CAP, E]], base=CAP, channel_multiplier=0, allow_small_or_imprecise_dtypes=True)
            pool.iota(row_base[0][:], [[0, 2], [REGION // P, E]], base=0, channel_multiplier=0,
                      allow_small_or_imprecise_dtypes=True)
            pool.iota(row_base[1][:], [[CAP // P, 2], [2 * CAP // P, E]], base=0, channel_multiplier=0,
                      allow_small_or_imprecise_dtypes=True)
            pool.iota(slot128[:], [[P, NTILE]], base=0, channel_multiplier=0, allow_small_or_imprecise_dtypes=True)
            pool.iota(part[:], [[0, 1]], base=0, channel_multiplier=1, allow_small_or_imprecise_dtypes=True)
            pool.iota(seg_at[:], [[0, SEG], [P, CAP // P]], base=0, channel_multiplier=1, allow_small_or_imprecise_dtypes=True)
            pool.iota(pay[:, :, :, D], [[TOK, 2], [P, NTILE]], base=0, channel_multiplier=1, allow_small_or_imprecise_dtypes=True)
            pool.drain()
            pool.affine_select(out=ident[:], in_=ident[:], compare_op=ALU.not_equal, fill=1.0, base=0,
                               pattern=[[-1, P]], channel_multiplier=1)
            pool.affine_select(out=before[:], in_=before[:], compare_op=ALU.is_gt, fill=0.0, base=0,
                               pattern=[[1, P]], channel_multiplier=-1)
            pool.affine_select(out=upper[:], in_=upper[:], compare_op=ALU.is_ge, fill=0.0, base=0,
                               pattern=[[1, E], [-1, E]], channel_multiplier=0)
            pool.affine_select(out=every[:], in_=every[:], compare_op=ALU.not_equal, fill=1.0, base=0,
                               pattern=[[0, HEADS], [-1, KEYS]], channel_multiplier=1)
            pool.affine_select(out=headmask[:], in_=headmask[:], compare_op=ALU.is_ge, fill=0.0, base=0,
                               pattern=[[-HD, HEADS]], channel_multiplier=1)
            pool.affine_select(out=chunkmask[:], in_=chunkmask[:], compare_op=ALU.is_ge, fill=0.0, base=0,
                               pattern=[[-KEYS, HC]], channel_multiplier=1)
            pool.drain()
            pool.affine_select(out=headmask[:], in_=headmask[:], compare_op=ALU.is_ge, fill=0.0, base=HD - 1,
                               pattern=[[HD, HEADS]], channel_multiplier=-1)
            pool.affine_select(out=chunkmask[:], in_=chunkmask[:], compare_op=ALU.is_ge, fill=0.0, base=KEYS - 1,
                               pattern=[[KEYS, HC]], channel_multiplier=-1)
            pool.drain()
            pool.sem_inc(const, 1)

            selfs = [0]

            def own(instruction):
                selfs[0] += 1
                instruction.then_inc(Z["p_self"], 1)
                pool.wait_ge(Z["p_self"], selfs[0])

            def roots(i, lo, hi, done):
                pool.tensor_scalar(shift[i][:, lo:hi], mv[i][:, lo:hi, 0], -1.0, None, ALU.mult)
                own(pool.tensor_scalar(rstd[i][:, lo:hi], mv[i][:, lo:hi, 1], EPS, None, ALU.add))
                own(pool.tensor_tensor(rstd[i][:, lo:hi], rstd[i][:, lo:hi], minus_half[:, lo:hi], ALU.pow))
                pool.tensor_tensor(shift[i][:, lo:hi], shift[i][:, lo:hi], rstd[i][:, lo:hi],
                                   ALU.mult).then_inc(done, 1)

            def root(l, g):
                pool.wait_ge(Z["a_stat"], g_at(l, g) + 1)
                if g_at(l, g):
                    pool.wait_ge(Z["a_sc"], g_at(l, g))
                roots(0, 0, GT, Z["a_root"])

            def root_routed(l, g):
                pool.wait_ge(Z["r_stat"], g_at(l, g) + 1)
                if g_at(l, g):
                    pool.wait_ge(Z["r_sc"], g_at(l, g))
                roots(0, GT, 2 * GT, Z["r_root"])

            def root2(l, g):
                pool.wait_ge(Z["stat2"], g_at(l, g) + 1)
                if g:
                    pool.wait_ge(Z["a_sc2" if l else "r_sc2"], g)
                roots(1, 0 if l else GT, GT if l else 2 * GT, Z["root2"])

            def scatter_rows(k, half):
                def scatter(l, g):
                    if k >= TOPK[l]:
                        return
                    pool.wait_ge(Z["r_pos"], g_at(l, g) + 1)
                    if k == 1:
                        pool.wait_ge(Z["r_rows"], g_at(l, g) + 1)
                    if l == 1 and g == 0 and k == half == 0:
                        pool.wait_ge(zero_done, 16)
                    for t in range(g * GT + half * GT // 2, g * GT + (half + 1) * GT // 2):
                        pool.indirect_dma_start(
                            out=(slots1 if l == 1 else slots)[:, :],
                            out_offset=bass.IndirectOffsetOnAxis(ap=pos[:, t, k:k + 1], axis=0),
                            in_=pay[:, k, t, :], in_offset=None,
                            bounds_check=(SEG * CAP if l == 1 else E * REGION) - 1, oob_is_err=False).then_inc(scat[l], 16)
                return scatter

            def context(l, g):
                pool.wait_ge(Z["c_stat"], 1)
                roots(0, GT, GT + 1, Z["c_root"])

            for l in range(LAYERS):
                at = AT[l]
                walk(l, lambda l, s: None, [
                    (at["stats"], GROUPS, root),
                    (at["context"] if l == 0 else 0, (0,) if l == 0 else (), context),
                    (at["stats_r"], GROUPS, root_routed),
                    *([(at["stats2"], GROUPS, root2)] if l < 2 else []),
                    *[(at["scatter"] + 2 * k + half, GROUPS, scatter_rows(k, half))
                      for k in range(TOPK[l]) for half in range(2)]])
                base = tile_base(l)

                def scatter(s, i):
                    q = i % RING
                    pool.wait_ge(Z["t_ysb"], s + (base + 1))
                    pool.wait_ge(Z["t_id"], s + (base + 1))
                    pool.sem_inc(Z["t_go"], 1)
                    pool.indirect_dma_start(
                        out=result[:, :], out_offset=bass.IndirectOffsetOnAxis(ap=row[:, i:i + 1], axis=0),
                        in_=ysb[:, q, :], in_offset=None,
                        bounds_check=2 * TOK - 1, oob_is_err=False).then_inc(put[q], 16)

                with pool.Fori(0, TILES[l] // TURN) as turn:
                    for i in range(TURN):
                        scatter(turn * TURN + i, i)
                for s in range(TILES[l] // TURN * TURN, TILES[l]):
                    scatter(s, s % TURN)

        @block.tensor
        def _(pe):
            pe.wait_ge(const, 2)

            def context(l, g=0):
                src = ctxTn if l == 1 else ctxT
                out = bank[5]
                if l == 0:
                    pe.wait_ge(ld_ctx, 16)
                    pe.transpose(out[:, 0:P], ctx_sb[:], ident[:])
                    pe.wait_ge(Z["c_norm"], 1)
                    pe.transpose(out[:, P:2 * P], ctxn[:], ident[:]).then_inc(Z["c_t"], 1)
                    pe.wait_ge(Z["c_T"], 1)
                    pe.wait_ge(ld_small, 16 * 3)
                if l == 1:
                    pe.wait_ge(ld_attn, 16)
                if l == 2:
                    pe.wait_ge(blk_done, 1)
                pe.matmul(out[:, 0:P], WK[l], src[:], start=True, stop=True).then_inc(Z["c_k"], 1)
                if l < 3:
                    for b in range(B):
                        keys = ctxR[:, 1 if l == 1 else 0, b].rearrange("p j k -> p (j k)")
                        last = pe.matmul(bank[6][:, b * P:(b + 1) * P], keys, WV[l], start=True, stop=l != 0)
                        if l == 0:
                            last = pe.matmul(bank[6][:, b * P:(b + 1) * P], ones[:],
                                             rows[0:1, R["bv0"]:R["bv0"] + P], start=False, stop=True)
                else:
                    for b in range(B):
                        pe.matmul(bank[6][0:KEYS, b * P:(b + 1) * P], src[:, b * KEYS:(b + 1) * KEYS], WV[l],
                                  start=True, stop=False)
                        last = pe.matmul(bank[6][0:KEYS, b * P:(b + 1) * P], ones[:, 0:KEYS],
                                         rows[0:1, R["bv3"]:R["bv3"] + P], start=False, stop=True)
                last.then_inc(Z["c_v"], 1)

            def next_context(l, g):
                context(l + 1)

            def transpose_tokens(l, g):
                if l == 1:
                    pe.wait_ge(Z["a_sc2"], g + 1)
                else:
                    pe.wait_ge(Z["a_sc"], g_at(l, g) + 1)
                for t in range(GT):
                    last = pe.transpose(bank[0][:, t * P:(t + 1) * P], xn[:, t, :], ident[:])
                last.then_inc(Z["a_xt"], 1)

            def queries(l, g):
                pe.wait_ge(Z["a_xT"], g_at(l, g) + 1)
                if l == g == 0:
                    pe.wait_ge(ld_small, 16 * 3)
                pe.matmul(bank[0][:], WQ[l], xT[:], start=True, stop=True).then_inc(Z["a_q"], 1)

            def tile(l, s):
                if l == 3:
                    return
                if 0 <= s - 1 < NTILE:
                    n, N = s - 1, n_at(l, s - 1)
                    pe.wait_ge(Z["a_exp"], N + 1)
                    if N >= 1:
                        pe.wait_ge(Z["a_pT"], N)
                    pt = prob[:, n % 2].rearrange("p (c j) k -> p c (j k)", c=NC)
                    for c in range(NC):
                        last = pe.transpose(bank[4][:, c * P:(c + 1) * P], pt[:, c, :], ident[:])
                    last.then_inc(Z["a_pt"], 1)
                if 0 <= s - 3 < NTILE:
                    n, N = s - 3, n_at(l, s - 3)
                    pe.wait_ge(Z["a_oT"], N + 1)
                    if N >= 1:
                        pe.wait_ge(Z["a_x"], N)
                    last = pe.matmul(bank[7][:, 0:P], oT[:, n % 2, :], WO[l], start=True, stop=l == 1)
                    if l != 1:
                        r = R["bo0" if l == 0 else "bo2"]
                        last = pe.matmul(bank[7][:, 0:P], ones[:], rows[0:1, r:r + P], start=False, stop=True)
                    last.then_inc(Z["a_pr"], 1)
                if 0 <= s + 1 < NTILE:
                    n, N, g = s + 1, n_at(l, s + 1), (s + 1) // GT
                    pe.wait_ge(Z["a_qT"], g_at(l, g) + 1)
                    if N == 0:
                        pe.wait_ge(Z["c_blk"], 1)
                    if N >= 2:
                        pe.wait_ge(Z["a_sub"], N - 1)
                    out = bank[2 + n % 2][:]
                    last = pe.matmul(out, qT[:, g % 2, n % GT * P:(n % GT + 1) * P],
                                     kblk[:, g].rearrange("p h k -> p (h k)"), start=True, stop=l != 2)
                    if l == 2:
                        last = pe.matmul(out, maskT[:, n * P:(n + 1) * P], every[:].rearrange("k h i -> k (h i)"),
                                         start=False, stop=True)
                    last.then_inc(Z["a_s"], 1)
                if 0 <= s - 1 < NTILE:
                    n, N = s - 1, n_at(l, s - 1)
                    pe.wait_ge(Z["a_pT"], N + 1)
                    if N >= 1:
                        pe.wait_ge(Z["a_o"], N)
                    for c in range(NC):
                        last = pe.matmul(bank[6][:, c * VW:(c + 1) * VW], probT[:, n % 2, c, :], vblk[:, n // GT, c, :],
                                         start=True, stop=True)
                    last.then_inc(Z["a_pv"], 1)
                if 0 <= s - 2 < NTILE:
                    n, N = s - 2, n_at(l, s - 2)
                    pe.wait_ge(Z["a_o"], N + 1)
                    if N >= 1:
                        pe.wait_ge(Z["a_oT"], N)
                    pe.transpose(bank[5][:, 0:P], o[:, n % 2, :], ident[:]).then_inc(Z["a_ot"], 1)

            def scores3(l, g):
                pe.wait_ge(Z["a_qT"], g_at(l, g) + 1)
                pe.wait_ge(Z["a_sub"], n_at(3, g))
                for t in range(GT):
                    last = pe.matmul(bank[2][:, t * KEYS:(t + 1) * KEYS], qT[:, g % 2, t * P:(t + 1) * P],
                                     kT[:, g * KEYS:(g + 1) * KEYS], start=True, stop=True)
                last.then_inc(Z["a_s"], 1)

            def transpose3(l, g):
                pe.wait_ge(Z["a_o"], n_at(3, g) + 1)
                pe.wait_ge(Z["a_pT"], n_at(3, g))
                for t in range(GT):
                    last = pe.transpose(bank[4][0:KEYS, t * P:(t + 1) * P], prob[:, 0, t, :], ident[:])
                last.then_inc(Z["a_pt"], 1)

            def values3(l, g):
                pe.wait_ge(Z["a_pT"], n_at(3, g) + 1)
                pe.wait_ge(Z["a_x"], n_at(3, g))
                for t in range(GT):
                    last = pe.matmul(bank[6][:, t * P:(t + 1) * P], probT[0:KEYS, 0, t, :], v3[:, g, :],
                                     start=True, stop=True)
                last.then_inc(Z["a_pr"], 1)

            def transpose_routed(l, g):
                pe.wait_ge(Z["r_sc"], g_at(l, g) + 1)
                if g_at(l, g) and (l < 3 or g == 0):
                    pe.wait_ge(Z["r_pos"], g_at(l, g))
                elif l == 3:
                    pe.wait_ge(Z["r_xT"], g_at(l, g))
                for t in range(GT):
                    last = pe.transpose(bank[1][:, t * P:(t + 1) * P], pay[:, 0, g * GT + t, 0:D], ident[:])
                last.then_inc(Z["r_xt"], 1)

            def transpose_routed2(l, g):
                pe.wait_ge(Z["r_sc2"], g + 1)
                pe.wait_ge(Z["r_xT"], g_at(l, g) + 1)
                for t in range(GT):
                    last = pe.transpose(bank[1][:, t * P:(t + 1) * P], xn2[:, t, :], ident[:])
                last.then_inc(Z["r_xt2"], 1)

            def logits(l, g):
                if l == 0:
                    pe.wait_ge(Z["r_xT2"], g + 1)
                else:
                    pe.wait_ge(Z["r_xT"], g_at(l, g) + 1)
                if l == 3 and g:
                    pe.wait_ge(Z["r_pick"], g_at(l, g))
                src = xnT if l == 0 else xfT[:, g * S:(g + 1) * S]
                for t in range(GT):
                    last = pe.matmul(bank[BANK_R[l][1]][:, t * E:(t + 1) * E], src[:, t * P:(t + 1) * P], router[l],
                                     start=True, stop=l != 2)
                    if l == 2:
                        last = pe.matmul(bank[BANK_R[l][1]][:, t * E:(t + 1) * E], ones[:], ebias[0:1], start=False,
                                         stop=True)
                last.then_inc(Z["r_lg"], 1)

            def ranks(l, g):
                pe.wait_ge(Z["r_pick"], g_at(l, g) + 1)
                if l == 3 and g:
                    pe.wait_ge(Z["r_pos"], g_at(l, g))
                out = bank[BANK_R[l][2]][:, 0:GT * SEG].rearrange("p (t k e) -> p t k e", t=GT, k=2)

                def add(out, w, counts, n, start=False, stop=False):
                    if l == 1:
                        return pe.matmul(out, w[:], counts.to_broadcast([P, n, 2, E]), start=start, stop=stop)
                    for k in range(TOPK[l]):
                        last = pe.matmul(out, w[:], counts[:, :, k:k + 1, :].to_broadcast([P, n, 2, E]),
                                         start=start and k == 0, stop=stop and k == TOPK[l] - 1)
                    return last

                pe.matmul(out, onesb[:], row_base[l == 1][:].unsqueeze(1).to_broadcast([P, GT, 2, E]), start=True, stop=False)
                for u in range(g):
                    add(out, onesb, gsum[:, u:u + 1], GT)
                for t in range(GT - 1):
                    add(out[:, t + 1:], onesb, picks[:, g, t:t + 1], GT - 1 - t)
                last = add(out, before, picks[:, g], GT, stop=True)
                if g == NG - 1:
                    total = bank[BANK_R[l][2]][:, GT * SEG:(GT + 1) * SEG].rearrange("p (t k e) -> p t k e", t=1, k=2)
                    for u in range(g):
                        add(total, onesb, gsum[:, u:u + 1], 1, start=u == 0)
                    for t in range(GT):
                        last = add(total, onesb, picks[:, g, t:t + 1], 1, stop=t == GT - 1)
                last.then_inc(Z["r_rank"], 1)

            def spread_tables(l):
                if l == 1:
                    return
                n = TILES[l]
                pe.wait_ge(Z["m_diag"], max(1, l))
                pe.matmul(bank[BANK_R[l][2]][:, 0:3 * n].rearrange("p (i n) -> p i n", i=3), onesb[:],
                          diagonals[:, :, 0:n], start=True, stop=True).then_inc(Z["m_row"], 1)

            def shared(l, g, i):
                n = 2 * (NG * grown(NSH, l) + NSH[l] * g) + i
                if i < 2 * NSH[l]:
                    j, c = i // 2, i % 2
                    if g == 0 and i == 0:
                        pe.wait_ge(ld_w[l], 32)
                        pe.wait_ge(Z["c_blk"], l + 2)
                    if n >= 2:
                        pe.wait_ge(Z["s_act"], n - 1)
                    pe.matmul(bank[2 + c][:], w1[l][:, E + j, c * P:(c + 1) * P], xfT[:, g * S:(g + 1) * S],
                              start=True, stop=True)
                    pe.matmul(bank[4 + c][:], w1[l][:, E + j, (2 + c) * P:(3 + c) * P], xfT[:, g * S:(g + 1) * S],
                              start=True, stop=True).then_inc(Z["s_h"], 1)
                    return
                pe.wait_ge(Z["s_act"], n)
                pe.wait_ge(Z["a_x"], n_at(l, NTILE))
                m = (0 if l == 0 else NG) + g
                if m >= 2:
                    pe.wait_ge(Z["s_x"], m - 1)
                for t in range(GT):
                    for c in range(i):
                        last = pe.matmul(bank[6 + g % 2][:, t * P:(t + 1) * P], hsh[:, c, t * P:(t + 1) * P],
                                         w2[l][:, E * 2 + c, :], start=c == 0, stop=c == i - 1)
                last.then_inc(Z["s_y"], 1)

            def experts(l):
                base = tile_base(l)
                nf = FC[l]
                w2f = w2[l][:].rearrange("p c n -> p (c n)")

                def transpose_x(s, k):
                    q = k % RING
                    pe.wait_ge(filled[q], (s + (RING - q)) * (16 // RING) + ring_base(l, q))
                    if k >= 2:
                        pe.wait_ge(Z["t_xT"], s + (base - 1))
                    pe.transpose(bank[k % 2][:, 0:P], xg[:, q, 0:D], ident[:]).then_inc(Z["t_x"], 1)

                def first(s, k):
                    p = k % 2
                    pe.wait_ge(Z["t_xT"], s + (base + 1))
                    pe.wait_ge(Z["t_w"], s + (base + 1))
                    if k >= 2:
                        pe.wait_ge(Z["t_hid"], s + (base - 1))
                    for c in range(WIDE // P):
                        last = pe.matmul(bank[2 + p][:, c * P:(c + 1) * P], wide[:, p, c * P:(c + 1) * P], xgT[:, p, :],
                                         start=True, stop=True)
                    last.then_inc(Z["t_h"], 1)

                def second(s, k, e):
                    pe.wait_ge(Z["t_hid"], s + (base + 1))
                    if l == 1 and k == 0:
                        pe.wait_ge(Z["c_blk"], l + 2)
                    if k >= 2:
                        pe.wait_ge(Z["t_ysb"], s + (base - 1))
                    for c in range(nf):
                        last = pe.matmul(bank[6 + k % 2][:, 0:D], hid[:, k % 2, c * P:(c + 1) * P],
                                         w2f[:, bass.ds(e * (nf * D) + c * D, D)], start=c == 0, stop=c == nf - 1)
                    last.then_inc(Z["t_y"], 1)

                n = TILES[l]

                def step(s, k, e, full=False):
                    if full or k < n:
                        transpose_x(s, k)
                    if full or 0 <= k - 1 < n:
                        first(s - 1, k - 1)
                    if full or 0 <= k - 2 < n:
                        second(s - 2, k - 2, e[k - 2])

                steps(pe, n, step, (mybir.EngineType.PE, l))

            for l in range(LAYERS):
                three = GROUPS if l == 3 else ()
                at = AT[l]
                walk(l, tile, [
                    (at["context"] if l == 0 else 0, (0,) if l == 0 else (), context),
                    (at["next_context"] if l < 3 else 0, (0,) if l < 3 else (), next_context),
                    (at["tokens"], GROUPS, transpose_tokens),
                    (at["queries"], GROUPS, queries),
                    (0, three, scores3), (2, three, transpose3), (3, three, values3),
                    (at["tokens_r"], GROUPS, transpose_routed),
                    *([(at["tokens_r2"], GROUPS, transpose_routed2)] if l == 0 else []),
                    (at["logits"], GROUPS, logits),
                    (at["ranks"], GROUPS, ranks)], shared)
                pe.wait_ge(ld_w[l], 16 * (4 if l == 3 else 2))
                rest_of_parts(l, shared, spread_tables)
                pe.wait_ge(Z["m_tab"], l + 1)
                experts(l)

        @block.scalar
        def _(act):
            act.wait_ge(const, 1)

            def preload(function):
                act.activation(unused[:], zeros[:, 0:1], function)
                act.drain()

            def context(l, g=0):
                src = bank[5]
                if l == 0:
                    act.wait_ge(ld_small, 16 * 3)
                    act.activation(tg[:], gates, ACT.Tanh).then_inc(tg_done, 1)
                    preload(ACT.Exp)
                    act.wait_ge(Z["c_t"], 1)
                    act.copy(ctxT[:], src[:, 0:P])
                    act.activation(ctxTn[:], src[:, P:2 * P], ACT.Identity, bias=C["ln1_b"],
                                       scale=C["ln1_g"])
                    act.drain()
                    for i, keys in enumerate((ctxT, ctxTn)):
                        for b in range(B):
                            last = act.copy(ctxR[:, i, b], keys[:, b * KEYS:(b + 1) * KEYS].unsqueeze(1)
                                            .to_broadcast([P, HC, KEYS]))
                    last.then_inc(Z["c_T"], 1)
                act.wait_ge(Z["c_k"], l + 1)
                if l in (0, 3):
                    act.activation(kT[:], src[:, 0:P], ACT.Identity,
                                   bias=C["bk0" if l == 0 else "bv3"]).then_inc(Z["c_kT"], 1)
                else:
                    act.copy(kT[:], src[:, 0:P]).then_inc(Z["c_kT"], 1)

            def next_context(l, g):
                context(l + 1)

            def scale(dst, src, i, lo, done):
                for t in range(GT):
                    last = act.activation(dst(t), src(t), ACT.Identity, bias=shift[i][:, lo + t:lo + t + 1],
                                          scale=rstd[i][:, lo + t:lo + t + 1])
                last.then_inc(done, 1)

            def scale_tokens(l, g):
                act.wait_ge(Z["a_root"], g_at(l, g) + 1)
                if g_at(l, g):
                    act.wait_ge(Z["a_xt"], g_at(l, g))
                scale(lambda t: xn[:, t, :], lambda t: x[:, g * GT + t, :], 0, 0, Z["a_sc"])

            def scale_tokens2(l, g):
                act.wait_ge(Z["root2"], g_at(l, g) + 1)
                scale(lambda t: xn[:, t, :], lambda t: xn[:, t, :], 1, 0, Z["a_sc2"])

            def scale_routed(l, g):
                act.wait_ge(Z["r_root"], g_at(l, g) + 1)
                scale(lambda t: pay[:, 0, g * GT + t, 0:D], lambda t: x[:, g * GT + t, :], 0, GT, Z["r_sc"])

            def scale_routed2(l, g):
                act.wait_ge(Z["root2"], g_at(l, g) + 1)
                if g:
                    act.wait_ge(Z["r_xt2"], g)
                scale(lambda t: xn2[:, t, :], lambda t: pay[:, 0, g * GT + t, 0:D], 1, GT, Z["r_sc2"])

            def copy_tokens(l, g):
                act.wait_ge(Z["a_xt"], g_at(l, g) + 1)
                if g_at(l, g):
                    act.wait_ge(Z["a_q"], g_at(l, g))
                if l == 1:
                    act.activation(xT[:], bank[0][:], ACT.Identity, bias=C["ln2_b"], scale=C["ln2_g"]).then_inc(Z["a_xT"], 1)
                else:
                    act.copy(xT[:], bank[0][:]).then_inc(Z["a_xT"], 1)

            def copy_queries(l, g):
                act.wait_ge(Z["a_q"], g_at(l, g) + 1)
                if l in (0, 3):
                    act.activation(qT[:, g % 2], bank[0][:], ACT.Identity,
                                   bias=C["bq0" if l == 0 else "bq3"]).then_inc(Z["a_qT"], 1)
                else:
                    act.copy(qT[:, g % 2], bank[0][:]).then_inc(Z["a_qT"], 1)

            def tile(l, s):
                if l == 3:
                    return
                if 0 <= s - 1 < NTILE:
                    n, N = s - 1, n_at(l, s - 1)
                    act.wait_ge(Z["a_pt"], N + 1)
                    if N >= 2:
                        act.wait_ge(Z["a_pv"], N - 1)
                    act.copy(probT[:, n % 2].rearrange("p c n -> p (c n)"), bank[4][:]).then_inc(Z["a_pT"], 1)
                if 0 <= s < NTILE:
                    act.wait_ge(Z["a_sub"], n_at(l, s) + 1)
                    act.activation(prob[:, s % 2], prob[:, s % 2], ACT.Exp, scale=SCALE[l]).then_inc(Z["a_exp"], 1)
                if 0 <= s - 2 < NTILE:
                    n, N = s - 2, n_at(l, s - 2)
                    act.wait_ge(Z["a_ot"], N + 1)
                    if N >= 2:
                        act.wait_ge(Z["a_pr"], N - 1)
                    act.copy(oT[:, n % 2, :], bank[5][:, 0:P]).then_inc(Z["a_oT"], 1)

            def exp3(l, g):
                act.wait_ge(Z["a_sub"], n_at(3, g) + 1)
                act.activation(prob[:, 0, 0:GT, :], prob[:, 0, 0:GT, :], ACT.Exp).then_inc(Z["a_exp"], 1)

            def copy3(l, g):
                act.wait_ge(Z["a_pt"], n_at(3, g) + 1)
                act.wait_ge(Z["a_pr"], n_at(3, g))
                act.copy(probT[0:KEYS, 0].rearrange("p t n -> p (t n)"), bank[4][0:KEYS, :]).then_inc(Z["a_pT"], 1)

            def copy_routed(l, g):
                act.wait_ge(Z["r_xt"], g_at(l, g) + 1)
                act.copy(xfT[:, g * S:(g + 1) * S], bank[1][:]).then_inc(Z["r_xT"], 1)
                if TOPK[l] == 2:
                    act.wait_ge(Z["r_sc"], g_at(l, g) + 1)
                    act.copy(pay[:, 1, g * GT:(g + 1) * GT, 0:D],
                             pay[:, 0, g * GT:(g + 1) * GT, 0:D]).then_inc(Z["r_rows"], 1)

            def copy_routed2(l, g):
                act.wait_ge(Z["r_xt2"], g + 1)
                if g:
                    act.wait_ge(Z["r_lg"], g)
                act.activation(xnT[:], bank[1][:], ACT.Identity, bias=C["ffn_b"], scale=C["ffn_g"]).then_inc(Z["r_xT2"], 1)

            def exp_logits(l):
                act.wait_ge(Z["r_top"], l + 1)
                act.activation(ex[:], ex[:], ACT.Exp).then_inc(Z["r_ex"], 1)

            def shared(l, g, i):
                if i < 2 * NSH[l]:
                    n, c = 2 * (NG * grown(NSH, l) + NSH[l] * g) + i, i % 2
                    act.wait_ge(Z["s_h"], n + 1)
                    if n >= 2:
                        act.wait_ge(Z["s_act"], n - 1)
                    act.activation(gat[:, c, :], bank[2 + c][:], ACT.Silu).then_inc(Z["s_gate"], 1)

            def experts(l):
                base = tile_base(l)
                nf = FC[l]

                def copy_x(s, k):
                    act.wait_ge(Z["t_x"], s + (base + 1))
                    if k >= 2:
                        act.wait_ge(Z["t_h"], s + (base - 1))
                    act.copy(xgT[:, k % 2, :], bank[k % 2][:, 0:P]).then_inc(Z["t_xT"], 1)

                def function(s, k, e):
                    p = k % 2
                    act.wait_ge(Z["t_h"], s + (base + 1))
                    if l in (0, 2):
                        if k >= 2:
                            act.wait_ge(Z["t_hid"], s + (base - 1))
                        act.activation(pre[:, p, 0:256], bank[2 + p][:, 0:256], ACT.Silu).then_inc(Z["t_pre"], 1)
                        return
                    if k >= 2:
                        act.wait_ge(Z["t_y"], s + (base - 1))
                    if l == 1:
                        act.activation(hid[:, p, :], bank[2 + p][:], ACT.Gelu_apprx_tanh).then_inc(Z["t_hid"], 1)
                        return
                    for c in range(nf):
                        last = act.activation(hid[:, p, c * P:(c + 1) * P], bank[2 + p][:, c * P:(c + 1) * P], ACT.Gelu,
                                              bias=b1[:, bass.ds(e * nf + c, 1)])
                    last.then_inc(Z["t_hid"], 1)

                n = TILES[l]

                def step(s, k, e, full=False):
                    if full or k < n:
                        copy_x(s, k)
                    if full or 0 <= k - 1 < n:
                        function(s - 1, k - 1, e.get(k - 1))

                steps(act, n, step, (mybir.EngineType.Activation, l) if l == 3 else None)

            for l in range(LAYERS):
                three = GROUPS if l == 3 else ()
                at = AT[l]
                walk(l, tile, [
                    (at["context"] if l == 0 else 0, (0,) if l == 0 else (), context),
                    (at["next_context"] if l < 3 else 0, (0,) if l < 3 else (), next_context),
                    (at["scale"], GROUPS, scale_tokens),
                    *([(at["scale2"], GROUPS, scale_tokens2)] if l == 1 else []),
                    (at["tokens"], GROUPS, copy_tokens),
                    (at["queries"], GROUPS, copy_queries),
                    (0, three, exp3), (2, three, copy3),
                    (at["scale_r"], GROUPS, scale_routed),
                    (at["tokens_r"], GROUPS, copy_routed),
                    *([(at["scale2"], GROUPS, scale_routed2),
                       (at["tokens_r2"], GROUPS, copy_routed2)] if l == 0 else [])], shared)
                exp_logits(l)
                if l in (1, 3):
                    preload(ACT.Gelu_apprx_tanh if l == 1 else ACT.Gelu)
                rest_of_parts(l, shared)
                if l == 3:
                    act.wait_ge(Z["m_tab"], l + 1)
                    act.wait_ge(ld_w[3], 16 * 4)
                experts(l)
                if l + 1 < LAYERS:
                    preload(ACT.Exp)

        @block.vector
        def _(dve):
            dve.wait_ge(const, 2)

            def statistics(i, src, lo, done):
                dve.drain()
                for t in range(GT):
                    dve.bn_stats(stat[:, lo + t, :], src(t))
                dve.drain()
                for t in range(GT):
                    last = dve.bn_aggr(mv[i][:, lo + t, :], stat[:, lo + t, :])
                last.then_inc(done, 1)

            def stats(l, g):
                if g_at(l, g):
                    dve.wait_ge(Z["a_root"], g_at(l, g))
                if l == 0 and g < 2:
                    dve.wait_ge((ld_x, ld_more_x)[g], 16)
                statistics(0, lambda t: x[:, g * GT + t, :], 0, Z["a_stat"])

            def stats_routed(l, g):
                if g_at(l, g):
                    dve.wait_ge(Z["r_root"], g_at(l, g))
                statistics(0, lambda t: x[:, g * GT + t, :], GT, Z["r_stat"])

            def stats2(l, g):
                if g_at(l, g):
                    dve.wait_ge(Z["root2"], g_at(l, g))
                if l == 0:
                    dve.wait_ge(Z["r_sc"], g + 1)
                    statistics(1, lambda t: pay[:, 0, g * GT + t, 0:D], GT, Z["stat2"])
                else:
                    dve.wait_ge(Z["a_sc"], g_at(l, g) + 1)
                    statistics(1, lambda t: xn[:, t, :], 0, Z["stat2"])

            def prepare(l, g):
                dve.wait_ge(ld_mask, 16)
                dve.tensor_scalar(maskT[:], mask_i, 0.0, -1e20, ALU.is_equal, ALU.mult)
                dve.wait_ge(tg_done, 1)
                dve.tensor_scalar(brow[:], rows[:, R["ffn1"]:R["ffn1"] + P], tg[:, 5:6], None, ALU.mult)

            def context(l, g=0):
                if l == 0:
                    dve.wait_ge(ld_ctx, 16)
                    dve.bn_stats(stat[:, GT, :], ctx_sb[:])
                    dve.drain()
                    dve.bn_aggr(mv[0][:, GT, :], stat[:, GT, :]).then_inc(Z["c_stat"], 1)
                    dve.wait_ge(Z["c_root"], 1)
                    dve.tensor_scalar(ctxn[:], ctx_sb[:], mv[0][:, GT, 0:1], rstd[0][:, GT:GT + 1], ALU.subtract,
                                      ALU.mult).then_inc(Z["c_norm"], 1)
                    dve.tensor_copy(vblk[:, :, :, HC * HD:VW].rearrange("p b c j -> p (b c) j"),
                                    chunkmask[:].unsqueeze(1).to_broadcast([P, B * NC, HC]))
                if l == 2:
                    dve.wait_ge(ld_heads, 16 * HEADS)
                    for i in range(3):
                        last = dve.tensor_tensor(blockw[:, i, :].rearrange("p (h e) -> p h e", h=HEADS),
                                                 small[:, i, :].unsqueeze(1).to_broadcast([P, HEADS, HD]),
                                                 headmask[:].unsqueeze(2).to_broadcast([P, HEADS, HD]), ALU.mult)
                    last.then_inc(blk_done, 1)
                if l < 3:
                    dve.wait_ge(Z["c_kT"], l + 1)
                    for b in range(B):
                        dve.tensor_tensor(kblk[:, b],
                                          kT[:, b * KEYS:(b + 1) * KEYS].unsqueeze(1).to_broadcast([P, HEADS, KEYS]),
                                          headmask[:].unsqueeze(2).to_broadcast([P, HEADS, KEYS]), ALU.mult)
                    dve.wait_ge(Z["c_v"], l + 1)
                    for b in range(B):
                        last = dve.tensor_tensor(
                            vblk[:, b, :, 0:HC * HD].rearrange("p c (j d) -> p c j d", j=HC),
                            bank[6][:, b * P:(b + 1) * P].rearrange("p (c j d) -> p c j d", c=NC, j=HC),
                            chunkmask[:].unsqueeze(1).unsqueeze(3).to_broadcast([P, NC, HC, HD]), ALU.mult)
                    last.then_inc(Z["c_blk"], 1)
                else:
                    dve.wait_ge(Z["c_kT"], l + 1)
                    dve.wait_ge(Z["c_v"], l + 1)
                    dve.tensor_copy(v3[:].rearrange("p b d -> p (b d)"), bank[6][0:KEYS, :]).then_inc(Z["c_blk"], 1)

            def next_context(l, g):
                context(l + 1)

            def tile(l, s):
                if l == 3:
                    return
                if 0 <= s - 4 < NTILE:
                    dve.wait_ge(Z["a_pr"], n_at(l, s - 4) + 1)
                    dve.scalar_tensor_tensor(x[:, s - 4, :], bank[7][:, 0:P], tg[:, l:l + 1], x[:, s - 4, :],
                                             ALU.mult, ALU.add).then_inc(Z["a_x"], 1)
                soft, norm = 0 <= s < NTILE, 0 <= s - 2 < NTILE
                if norm:
                    p, M = (s - 2) % 2, n_at(l, s - 2)
                    dve.wait_ge(Z["a_pv"], M + 1)
                    pv = bank[6][:, 0:NC * VW].rearrange("p (c w) -> p c w", c=NC)
                    dve.reciprocal(rinv[:, p, :].rearrange("p (c j) -> p c j", c=NC), pv[:, :, HC * HD:VW])
                if soft:
                    N = n_at(l, s)
                    dve.wait_ge(Z["a_s"], N + 1)
                    sc = bank[2 + s % 2][:].rearrange("p (h k) -> p h k", h=HEADS)
                    dve.tensor_reduce(mx[:, s % 2, :], sc, AX.X, ALU.max)
                if soft or norm:
                    dve.drain()
                if norm:
                    if M >= 2:
                        dve.wait_ge(Z["a_ot"], M - 1)
                    dve.tensor_tensor(o[:, p, :].rearrange("p (c j d) -> p c j d", c=NC, j=HC),
                                      pv[:, :, 0:HC * HD].rearrange("p c (j d) -> p c j d", j=HC),
                                      rinv[:, p, :].rearrange("p (c j) -> p c j", c=NC).unsqueeze(3)
                                      .to_broadcast([P, NC, HC, HD]), ALU.mult).then_inc(Z["a_o"], 1)
                if soft:
                    if N >= 2:
                        dve.wait_ge(Z["a_pt"], N - 1)
                    dve.tensor_tensor(prob[:, s % 2], sc, mx[:, s % 2, :].unsqueeze(2).to_broadcast([P, HEADS, KEYS]),
                                      ALU.subtract).then_inc(Z["a_sub"], 1)

            def soft3(l, g):
                dve.wait_ge(Z["a_s"], n_at(3, g) + 1)
                dve.wait_ge(Z["a_pt"], n_at(3, g))
                sc = bank[2][:, 0:GT * KEYS].rearrange("p (t k) -> p t k", t=GT)
                dve.tensor_reduce(mx[:, 0, 0:GT], sc, AX.X, ALU.max)
                dve.drain()
                dve.tensor_tensor(prob[:, 0, 0:GT, :], sc, mx[:, 0, 0:GT].unsqueeze(2).to_broadcast([P, GT, KEYS]),
                                  ALU.subtract).then_inc(Z["a_sub"], 1)

            def norm3(l, g):
                dve.wait_ge(Z["a_exp"], n_at(3, g) + 1)
                dve.tensor_reduce(rinv[:, 0, 0:GT], prob[:, 0, 0:GT, :], AX.X, ALU.add)
                dve.drain()
                dve.reciprocal(rinv[:, 1, 0:GT], rinv[:, 0, 0:GT])
                dve.drain()
                dve.tensor_tensor(prob[:, 0, 0:GT, :], prob[:, 0, 0:GT, :],
                                  rinv[:, 1, 0:GT].unsqueeze(2).to_broadcast([P, GT, KEYS]),
                                  ALU.mult).then_inc(Z["a_o"], 1)

            def into_x3(l, g):
                dve.wait_ge(Z["a_pr"], n_at(3, g) + 1)
                xs = x[:, g * GT:(g + 1) * GT].rearrange("p t d -> p (t d)")
                dve.scalar_tensor_tensor(xs, bank[6][:], tg[:, 3:4], xs, ALU.mult, ALU.add).then_inc(Z["a_x"], 1)

            def pick(l, g):
                dve.wait_ge(Z["r_lg"], g_at(l, g) + 1)
                lg = bank[BANK_R[l][1]][:, 0:GT * E].rearrange("p (t e) -> p t e", t=GT)
                for t in range(GT):
                    dve.max(top[:, g * GT + t, :], lg[:, t, :])
                dve.drain()
                for t in range(GT):
                    dve.max_index(topi[:, t, :], top[:, g * GT + t, :], lg[:, t, :])
                dve.drain()
                dve.tensor_tensor(picks[:, g], iota_e[:].unsqueeze(1).unsqueeze(1).to_broadcast([P, GT, 2, E]),
                                  topi[:, :, 0:2].unsqueeze(3).to_broadcast([P, GT, 2, E]),
                                  ALU.is_equal).then_inc(Z["r_pick"], 1)

            def place_rows(l, g):
                dve.wait_ge(Z["r_rank"], g_at(l, g) + 1)
                rk = bank[BANK_R[l][2]][:, 0:GT * SEG].rearrange("p (t k e) -> p t k e", t=GT, k=2)
                if l == 1:
                    dve.tensor_tensor(place[:], rk, limit[:].unsqueeze(1).to_broadcast([P, GT, 2, E]), ALU.is_ge)
                    dve.drain()
                    dve.scalar_tensor_tensor(place[:], place[:], float(NOWHERE), rk, ALU.mult, ALU.add)
                    dve.drain()
                    rk = place[:]
                dve.tensor_tensor(place[:], rk, picks[:, g], ALU.mult)
                with nc.allow_low_precision(reason="counts up to 4, and whole numbers below 2 ** 24"):
                    dve.tensor_reduce(gsum[:, g].rearrange("p k e -> p (k e)"),
                                      picks[:, g].rearrange("p t k e -> p (k e) t"), AX.X, ALU.add)
                    dve.drain()
                    dve.tensor_reduce(pos[:, g * GT:(g + 1) * GT, :], place[:], AX.X, ALU.add).then_inc(Z["r_pos"], 1)

            def weights(l):
                dve.wait_ge(Z["r_ex"], l + 1)
                if l == 2:
                    dve.tensor_tensor(sums[:], ex[:, :, 0], ex[:, :, 1], ALU.add)
                else:
                    dve.tensor_reduce(sums[:], ex[:], AX.X, ALU.add)
                if l == 1:
                    dve.tensor_scalar(kept[:], pos[:], float(NOWHERE), None, ALU.is_lt)
                dve.drain()
                dve.reciprocal(over[:], sums[:])
                dve.drain()
                dve.tensor_tensor(wts[:], ex[:, :, 0:2], over[:].unsqueeze(2).to_broadcast([P, NTILE, 2]), ALU.mult)
                dve.drain()
                if l == 0:
                    dve.tensor_tensor(sums[:], wts[:, :, 0], wts[:, :, 1], ALU.add)
                    dve.drain()
                    dve.tensor_scalar(sums[:], sums[:], EPS, None, ALU.add)
                    dve.drain()
                    dve.reciprocal(over[:], sums[:])
                    dve.drain()
                    dve.tensor_tensor(wts[:], wts[:], over[:].unsqueeze(2).to_broadcast([P, NTILE, 2]), ALU.mult)
                    dve.drain()
                if l == 1:
                    dve.tensor_tensor(wts[:], wts[:], kept[:], ALU.mult)
                    dve.drain()
                dve.tensor_scalar(wts[:], wts[:], tg[:, 4 + l:5 + l], None, ALU.mult)

            def tables(l):
                dve.tensor_tensor(ex[:], top[:], top[:, :, 0:1].to_broadcast([P, NTILE, 8]),
                                  ALU.subtract).then_inc(Z["r_top"], 1)
                if l == 1:
                    dve.tensor_copy(count[:], bank[1][:, GT * SEG:(GT + 1) * SEG])
                    dve.drain()
                    n = TILES[1]
                    dve.tensor_tensor(valid[:, 0:n].rearrange("p (e k j) -> p e k j", e=E, k=2),
                                      count[:].rearrange("p (k e) -> p e k", k=2).unsqueeze(3).to_broadcast([P, E, 2, CAP // P]),
                                      seg_at[:].rearrange("p (e k j) -> p e k j", e=E, k=2), ALU.is_gt)
                    dve.drain()
                    dve.tensor_scalar(away[:, 0:n], valid[:, 0:n], -float(NOWHERE), float(NOWHERE), ALU.mult,
                                      ALU.add).then_inc(Z["m_tab"], 1)
                    dve.drain()
                    return
                n = TILES[l]
                cnt = count[:, 0:E]
                dve.tensor_copy(cnt, bank[BANK_R[l][2]][:, GT * SEG:GT * SEG + E])
                dve.drain()
                dve.tensor_tensor(pad_f[:], cnt, region0[:], ALU.add)
                dve.tensor_tensor(cmp1[:], cnt.unsqueeze(2).to_broadcast([P, E, NTILE]),
                                  slot128[:].unsqueeze(1).to_broadcast([P, E, NTILE]), ALU.is_gt)
                dve.drain()
                dve.tensor_copy(pad_r[:], pad_f[0:1, :]).then_inc(Z["m_pad"], 1)
                dve.tensor_reduce(ntil[:], cmp1[:], AX.X, ALU.add)
                dve.drain()
                dve.tensor_tensor(cmp2[:], upper[:], ntil[:].unsqueeze(1).to_broadcast([P, E, E]), ALU.mult)
                dve.drain()
                dve.tensor_reduce(cum[:], cmp2[:], AX.X, ALU.add)
                dve.drain()
                dve.tensor_tensor(cumx[:], cum[:], ntil[:], ALU.subtract)
                dve.tensor_scalar(ge_in[:], cum[:], part[:], None, ALU.is_le)
                dve.drain()
                dve.tensor_scalar(ge_ex[:], cumx[:], part[:], None, ALU.is_le)
                dve.tensor_reduce(te[:], ge_in[:], AX.X, ALU.add)
                dve.tensor_tensor(tw[:], ge_in[:], ntil[:], ALU.mult)
                dve.drain()
                dve.tensor_reduce(tb[:], tw[:], AX.X, ALU.add)
                dve.tensor_tensor(ge_ex[:], ge_ex[:], ge_in[:], ALU.subtract)
                dve.tensor_scalar(te[:], te[:], float(E - 1), None, ALU.min)
                dve.drain()
                dve.tensor_tensor(tb[:], part[:], tb[:], ALU.subtract)
                dve.tensor_tensor(tw[:], ge_ex[:], cnt, ALU.mult)
                dve.drain()
                dve.tensor_scalar(tb[:], tb[:], float(NTILE - 1), None, ALU.min)
                dve.tensor_reduce(tn[:], tw[:], AX.X, ALU.add)
                dve.drain()
                dve.scalar_tensor_tensor(tb[:], tn[:], 0.0, tb[:], ALU.is_gt, ALU.mult)
                dve.drain()
                dve.scalar_tensor_tensor(start[:], te[:], float(REGION // P), tb[:], ALU.mult, ALU.add)
                dve.scalar_tensor_tensor(fill[:], tb[:], -float(P), tn[:], ALU.mult, ALU.add)
                dve.drain()
                dve.tensor_scalar(diagonals[:, 0, 0:n], ident[:, 0:n], te[:], None, ALU.mult)
                dve.tensor_scalar(diagonals[:, 1, 0:n], ident[:, 0:n], start[:], None, ALU.mult)
                dve.tensor_scalar(diagonals[:, 2, 0:n], ident[:, 0:n], fill[:], float(P), ALU.mult,
                                  ALU.min).then_inc(Z["m_diag"], 1)
                dve.wait_ge(Z["m_row"], max(1, l))
                spread = bank[BANK_R[l][2]][:, 0:3 * n].rearrange("p (i n) -> p i n", i=3)
                dve.tensor_copy(tab_e[:, 0:n], spread[0:1, 0])
                dve.tensor_scalar(tab_r[:, 0:n], spread[0:1, 1], float(P), None, ALU.mult)
                dve.tensor_scalar(valid[:, 0:n], spread[:, 2], part[:], None, ALU.is_gt).then_inc(Z["m_tab"], 1)
                dve.drain()
                dve.tensor_scalar(away[:, 0:n], valid[:, 0:n], -float(NOWHERE), float(NOWHERE), ALU.mult, ALU.add)
                dve.drain()

            def shared(l, g, i):
                m = (0 if l == 0 else NG) + g
                if i < 2 * NSH[l]:
                    n, c = 2 * (NG * grown(NSH, l) + NSH[l] * g) + i, i % 2
                    dve.wait_ge(Z["s_gate"], n + 1)
                    if m:
                        dve.wait_ge(Z["s_y"], m)
                    dve.tensor_tensor(hsh[:, i, :], gat[:, c, :], bank[4 + c][:], ALU.mult).then_inc(Z["s_act"], 1)
                    return
                dve.wait_ge(Z["s_y"], m + 1)
                xs = x[:, g * GT:(g + 1) * GT].rearrange("p t d -> p (t d)")
                dve.scalar_tensor_tensor(xs, bank[6 + g % 2][:], tg[:, 4 + l:5 + l], xs, ALU.mult,
                                         ALU.add).then_inc(Z["s_x"], 1)

            def experts(l):
                base = tile_base(l)
                pbase = tile_base(l, PRE)
                w1f = w1[l][:].rearrange("p e n -> p (e n)")
                n = TILES[l]

                def ids(s, k):
                    q, i = k % RING, k % TURN
                    dve.wait_ge(filled[q], (s + (RING - q)) * (16 // RING) + ring_base(l, q))
                    dve.scalar_tensor_tensor(row[:, i:i + 1], xg[:, q, D:D + 1], valid[:, bass.ds(s, 1)],
                                             away[:, bass.ds(s, 1)], ALU.mult, ALU.add).then_inc(Z["t_id"], 1)

                def stage(s, k, e):
                    if k >= 2:
                        dve.wait_ge(Z["t_h"], s + (base - 1))
                    dve.tensor_scalar(wide[:, k % 2, :], w1f[:, bass.ds(e * WIDE, WIDE)], 1.0, None,
                                      ALU.mult).then_inc(Z["t_w"], 1)

                def gate_up(s, k):
                    p = k % 2
                    dve.wait_ge(Z["t_pre"], s + (pbase + 1))
                    if k >= 2:
                        dve.wait_ge(Z["t_y"], s + (base - 1))
                    dve.tensor_tensor(hid[:, p, 0:256], pre[:, p, 0:256], bank[2 + p][:, 256:512], ALU.mult).then_inc(Z["t_hid"], 1)

                def copy_y(s, k, e):
                    p, q = k % 2, k % RING
                    dve.wait_ge(Z["t_y"], s + (base + 1))
                    if k >= RING:
                        dve.wait_ge(put[q], (s - q) * (16 // RING) + ring_base(l, q))
                    if l == 3:
                        dve.tensor_tensor(ysb[:, q, :], bank[6 + p][:, 0:D], b2[:, bass.ds(e * D, D)], ALU.add).then_inc(Z["t_ysb"], 1)
                    else:
                        dve.tensor_copy(ysb[:, q, :], bank[6 + p][:, 0:D]).then_inc(Z["t_ysb"], 1)

                def step(s, k, e, full=False):
                    if full or k < n:
                        stage(s, k, e[k])
                        ids(s, k)
                    if l in (0, 2) and (full or 0 <= k - 1 < n):
                        gate_up(s - 1, k - 1)
                    if full or 0 <= k - 2 < n:
                        copy_y(s - 2, k - 2, e.get(k - 2))
                    if k == n:
                        weights(l)

                steps(dve, n, step, (mybir.EngineType.DVE, l))

            def combine(l, g):
                dve.wait_ge(back[g], 16 * sum(TOPK[:l + 1]))
                dve.drain()
                for k in range(TOPK[l]):
                    for t in range(g * GT, (g + 1) * GT):
                        last = dve.scalar_tensor_tensor(x[:, t, :], pay[:, k, t, 0:D], wts[:, t, k:k + 1], x[:, t, :],
                                                        ALU.mult, ALU.add)
                    dve.drain()
                if l == 1:
                    xs = x[:, g * GT:(g + 1) * GT]
                    dve.tensor_tensor(xs, xs, brow[:].unsqueeze(1).to_broadcast([P, GT, D]), ALU.add)
                    dve.drain()
                if l == LAYERS - 1:
                    last.then_inc(Z["x_done"], 1)

            def combine_last(l, g):
                combine(l - 1, g)

            for l in range(LAYERS):
                three = GROUPS if l == 3 else ()
                at = AT[l]
                walk(l, tile, [
                    (0, three, soft3), (1, three, norm3), (4, three, into_x3),
                    (at["combine"], GROUPS if l else (), combine_last),
                    (at["stats"], GROUPS, stats),
                    (at["context"] if l == 0 else 0, (0,) if l == 0 else (), context),
                    (at["next_context"] if l < 3 else 0, (0,) if l < 3 else (), next_context),
                    (1, (0,) if l == 0 else (), prepare),
                    (at["stats_r"], GROUPS, stats_routed),
                    *([(at["stats2"], GROUPS, stats2)] if l < 2 else []),
                    (at["pick"], GROUPS, pick),
                    (at["place"], GROUPS, place_rows)], shared)
                if l == 3:
                    dve.wait_ge(ld_w[3], 16 * 4)
                tables(l)
                rest_of_parts(l, shared)
                experts(l)
            for g in range(NG):
                combine(LAYERS - 1, g)


def kernel(**inputs):
    import numpy as np
    import concourse.bacc as bacc
    from concourse.bass_utils import run_bass_kernel_spmd

    a = {k: np.asarray(v) for k, v in inputs.items()}
    c = np.ascontiguousarray

    def columns(*names):
        return [a[n].reshape(P, 1) for n in names]

    def wide(*parts):
        return c(np.concatenate(parts, axis=2).transpose(1, 0, 2))

    def tall(w):
        e, f, d = w.shape
        return c(w.reshape(e, f // P, P, d).transpose(2, 0, 1, 3).reshape(P, e * (f // P), d))

    def stack(*ws):
        return np.concatenate([w if w.ndim == 3 else w[None] for w in ws], axis=0)

    cols = c(np.concatenate(columns("L0_xattn_bq", "L0_xattn_bk", "L1_xattn_ln1_g", "L1_xattn_ln1_b", "L1_xattn_ln2_g",
                                    "L1_xattn_ln2_b", "L0_ffn_ln_scale", "L0_ffn_ln_bias", "L3_xattn_bq", "L3_xattn_bv")
                            + [a["L0_ffn_gate_w"].T, a["L1_ffn_router_w"], a["L2_ffn_router_w"].T, a["L3_ffn_Wr"]], axis=1))
    rows = c(np.concatenate([a["L0_xattn_bv"], a["L0_xattn_bo"], a["L2_xattn_bout"], a["L3_xattn_bv"],
                             a["L1_ffn_bias"].reshape(-1), a["L2_ffn_expert_bias"], a["g_xattn"], a["g_ffn"]])[None])
    attnw = c(np.stack([a["L0_xattn_Wq"].T, a["L0_xattn_Wk"].T, a["L0_xattn_Wv"].T, a["L0_xattn_Wo"].T,
                        a["L1_xattn_Wq"], a["L1_xattn_Wk"], a["L1_xattn_Wv"], a["L1_xattn_Wfc"],
                        a["L2_xattn_Wout"].T, a["L3_xattn_Wq"], a["L3_xattn_Wv"]], axis=1))
    small = c(np.stack([a["L2_xattn_Wq"].T, a["L2_xattn_Wk"].T, a["L2_xattn_Wv"].T], axis=1))
    T = lambda w: w.transpose(0, 2, 1)
    w1 = [wide(stack(a["L0_ffn_Wg"], a["L0_ffn_sWg"]), stack(a["L0_ffn_Wu"], a["L0_ffn_sWu"])),
          wide(a["L1_ffn_w1"]),
          wide(stack(T(a["L2_ffn_w1"]), T(a["L2_ffn_sw1"])), stack(T(a["L2_ffn_w3"]), T(a["L2_ffn_sw3"]))),
          wide(a["L3_ffn_W1"])]
    w2 = [tall(stack(a["L0_ffn_Wd"], a["L0_ffn_sWd"])), tall(a["L1_ffn_w2"]),
          tall(stack(T(a["L2_ffn_w2"]), T(a["L2_ffn_sw2"]))), tall(a["L3_ffn_W2"])]
    arrays = {"x": c(a["x"].reshape(TOK, D)), "ctx": c(a["ctx_1024"].reshape(B * KEYS, D)),
              "mask": c(a["mask_Bx1xSxS2_ik1"].reshape(TOK, KEYS).T), "cols": cols, "rows": rows, "attnw": attnw,
              "small": small, **{f"w1_{l}": w1[l] for l in range(LAYERS)}, **{f"w2_{l}": w2[l] for l in range(LAYERS)},
              "b1": c(a["L3_ffn_b1"].reshape(-1, P).T), "b2": c(a["L3_ffn_b2"].reshape(1, -1))}
    nc = bacc.Bacc("TRN2", target_bir_lowering=False, num_devices=1)
    h = {n: nc.dram_tensor(f"in_{n}", v.shape, mybir.dt.from_np(v.dtype), kind="ExternalInput").ap()
         for n, v in arrays.items()}
    out = nc.dram_tensor("out_0", (TOK, D), F32, kind="ExternalOutput").ap()
    flamingo(nc, h["x"], h["ctx"], h["mask"], h["cols"], h["rows"], h["attnw"], h["small"],
             [h[f"w1_{l}"] for l in range(LAYERS)], [h[f"w2_{l}"] for l in range(LAYERS)], h["b1"], h["b2"], out)
    got = run_bass_kernel_spmd(nc, [{f"in_{n}": v for n, v in arrays.items()}], core_ids=[0])
    return got.results[0]["out_0"].reshape(B, S, D)
```
